# Optimizing a Trainium2 kernel written in Bass

```python
import numpy as np
import jax
import jax.numpy as jnp

def _softmax(x, axis=-1):
    return jax.nn.softmax(x, axis=axis)

def _gelu(x):
    return jax.nn.gelu(x, approximate=True)

def _silu(x):
    return jax.nn.silu(x)

def _sigmoid(x):
    return jax.nn.sigmoid(x)

def _layernorm(x, axis=-1, eps=1e-05):
    m = jnp.mean(x, axis=axis, keepdims=True)
    v = jnp.var(x, axis=axis, keepdims=True)
    return (x - m) / jnp.sqrt(v + eps)

def _scatter_add(tgt, idx, src, axis=0):
    return tgt.at[idx].add(src)

def _segment_sum(src, seg, n):
    return jax.ops.segment_sum(src, seg, n)
kernel_name = 'mk_hybrid_d1_jaxref_r8_93684c'

def setup_inputs(seed: int=0):
    np.random.seed(seed)
    _w = jnp.asarray

    def _L0_attn_a_setup():
        import jax, jax.numpy as jnp
        import numpy as np
        E = 128
        H = 16
        D = E // H
        B = 2
        N = 1024
        CHUNK = 128
        LAYER_IDX = 0
        NUM_LAYERS = 12
        EPS = 1e-05

        def _build_slopes(n):

            def po2(m):
                start = 2.0 ** (-2.0 ** (-(np.log2(m) - 3)))
                return [start * start ** i for i in range(m)]
            if np.log2(n).is_integer():
                return po2(n)
            closest = 2 ** int(np.floor(np.log2(n)))
            return po2(closest) + _build_slopes(2 * closest)[0::2][:n - closest]

        def _slope_rate():
            s = np.array(_build_slopes(H), dtype=np.float32)
            s = s * (1.0 - LAYER_IDX / (NUM_LAYERS - 1) + 1e-05)
            return jnp.asarray(s)

        def lightning_attn(q, k, v, s):
            b, h, n, d = q.shape
            nc = n // CHUNK
            idx = jnp.arange(CHUNK, dtype=q.dtype)
            diff = idx[:, None] - idx[None, :]
            mask = jnp.where(diff >= 0, jnp.exp(-s[:, None, None] * diff), 0.0)
            lam_q = jnp.exp(-s[:, None] * (idx + 1.0))
            lam_k = jnp.exp(-s[:, None] * (CHUNK - 1.0 - idx))
            lam_c = jnp.exp(-s * CHUNK)

            def to_chunks(t):
                return t.reshape(b, h, nc, CHUNK, d).transpose(2, 0, 1, 3, 4)
            qc, kc, vc = (to_chunks(q), to_chunks(k), to_chunks(v))

            def step(kv, xs):
                qi, ki, vi = xs
                scores = jnp.einsum('bhid,bhjd->bhij', qi, ki) * mask
                o = jnp.einsum('bhij,bhjd->bhid', scores, vi)
                o = o + lam_q[:, :, None] * jnp.einsum('bhid,bhde->bhie', qi, kv)
                kv = lam_c[:, None, None] * kv + jnp.einsum('bhid,bhie->bhde', ki * lam_k[:, :, None], vi)
                return (kv, o)
            kv0 = jnp.zeros((b, h, d, d), q.dtype)
            _, o = jax.lax.scan(step, kv0, (qc, kc, vc))
            return o.transpose(1, 2, 0, 3, 4).reshape(b, h, n, d)
        key = jax.random.key(seed)
        ks = jax.random.split(key, 8)
        sc = 1.0 / np.sqrt(E)
        return {'x': jax.random.normal(ks[0], (B, N, E), jnp.float32), 'Wq': jax.random.normal(ks[1], (E, E), jnp.float32) * sc, 'Wk': jax.random.normal(ks[2], (E, E), jnp.float32) * sc, 'Wv': jax.random.normal(ks[3], (E, E), jnp.float32) * sc, 'Wo': jax.random.normal(ks[4], (E, E), jnp.float32) * sc, 'gamma': jnp.ones((E,), jnp.float32), 'beta': jnp.zeros((E,), jnp.float32), 'Wg1': jax.random.normal(ks[5], (E, D), jnp.float32) * sc, 'Wg2': jax.random.normal(ks[6], (D, E), jnp.float32) * (1.0 / np.sqrt(D))}
    _L0_attn_a_in = _L0_attn_a_setup()

    def _L0_attn_b_setup():
        import jax, jax.numpy as jnp
        import numpy as np
        import math
        EMBED_DIM = 128
        NUM_HEADS = 16
        HEAD_DIM = EMBED_DIM // NUM_HEADS
        key = jax.random.key(seed)
        ks = jax.random.split(key, 5)
        B, S, D = (2, 256, EMBED_DIM)
        s = 1.0 / math.sqrt(D)
        x = jax.random.normal(ks[0], (B, S, D), dtype=jnp.float32)
        W_qkv = jax.random.normal(ks[1], (3 * D, D), dtype=jnp.float32) * s
        b_qkv = jax.random.normal(ks[2], (3 * D,), dtype=jnp.float32) * 0.01
        W_out = jax.random.normal(ks[3], (D, D), dtype=jnp.float32) * s
        b_out = jax.random.normal(ks[4], (D,), dtype=jnp.float32) * 0.01
        return {'x': x, 'W_qkv': W_qkv, 'b_qkv': b_qkv, 'W_out': W_out, 'b_out': b_out}
    _L0_attn_b_in = _L0_attn_b_setup()

    def _L0_ffn_setup():
        import jax, jax.numpy as jnp
        import numpy as np
        from jax.scipy.linalg import expm
        B, S, D, E, K, NROT = (2, 256, 128, 8, 2, 3)
        DF = 4 * D
        EPS = 1e-05
        key = jax.random.key(seed)
        ks = jax.random.split(key, 8)
        s = lambda d: 1.0 / np.sqrt(d)
        return {'x': jax.random.normal(ks[0], (B, S, D), jnp.float32), 'ln_g': jnp.ones((D,), jnp.float32), 'ln_b': jnp.zeros((D,), jnp.float32), 'abel_w': jax.random.normal(ks[1], (D, D), jnp.float32) * s(D), 'abel_b': jnp.zeros((D,), jnp.float32), 'gate_w_moe': jax.random.normal(ks[2], (D, E), jnp.float32) * s(D), 'gate_b_moe': jnp.zeros((E,), jnp.float32), 'w1': jax.random.normal(ks[3], (E, D, DF), jnp.float32) * s(D), 'b1': jnp.zeros((E, DF), jnp.float32), 'w2': jax.random.normal(ks[4], (E, DF, D), jnp.float32) * s(DF), 'b2': jnp.zeros((E, D), jnp.float32), 'gens': jax.random.normal(ks[5], (NROT, D, D), jnp.float32) * 0.02, 'mix_w': jax.random.normal(ks[6], (2 * D, 1), jnp.float32) * s(2 * D), 'mix_b': jnp.zeros((1,), jnp.float32)}
    _L0_ffn_in = _L0_ffn_setup()
    _d = {'L0_attn_a_x': _L0_attn_a_in['x'], 'L0_attn_a_Wq': _L0_attn_a_in['Wq'], 'L0_attn_a_Wk': _L0_attn_a_in['Wk'], 'L0_attn_a_Wv': _L0_attn_a_in['Wv'], 'L0_attn_a_Wo': _L0_attn_a_in['Wo'], 'L0_attn_a_gamma': _L0_attn_a_in['gamma'], 'L0_attn_a_beta': _L0_attn_a_in['beta'], 'L0_attn_a_Wg1': _L0_attn_a_in['Wg1'], 'L0_attn_a_Wg2': _L0_attn_a_in['Wg2'], 'L0_attn_b_W_qkv': _L0_attn_b_in['W_qkv'], 'L0_attn_b_b_qkv': _L0_attn_b_in['b_qkv'], 'L0_attn_b_W_out': _L0_attn_b_in['W_out'], 'L0_attn_b_b_out': _L0_attn_b_in['b_out'], 'L0_ffn_ln_g': _L0_ffn_in['ln_g'], 'L0_ffn_ln_b': _L0_ffn_in['ln_b'], 'L0_ffn_abel_w': _L0_ffn_in['abel_w'], 'L0_ffn_abel_b': _L0_ffn_in['abel_b'], 'L0_ffn_gate_w_moe': _L0_ffn_in['gate_w_moe'], 'L0_ffn_gate_b_moe': _L0_ffn_in['gate_b_moe'], 'L0_ffn_w1': _L0_ffn_in['w1'], 'L0_ffn_b1': _L0_ffn_in['b1'], 'L0_ffn_w2': _L0_ffn_in['w2'], 'L0_ffn_b2': _L0_ffn_in['b2'], 'L0_ffn_gens': _L0_ffn_in['gens'], 'L0_ffn_mix_w': _L0_ffn_in['mix_w'], 'L0_ffn_mix_b': _L0_ffn_in['mix_b']}
    _x0 = _d['L0_attn_a_x']
    _d['L0_attn_a_x'] = jax.random.normal(jax.random.fold_in(jax.random.key(seed), 1), (4, 1024, 128), dtype=_x0.dtype)
    del _x0
    return _d

def reference(L0_attn_a_x, L0_attn_a_Wq, L0_attn_a_Wk, L0_attn_a_Wv, L0_attn_a_Wo, L0_attn_a_gamma, L0_attn_a_beta, L0_attn_a_Wg1, L0_attn_a_Wg2, L0_attn_b_W_qkv, L0_attn_b_b_qkv, L0_attn_b_W_out, L0_attn_b_b_out, L0_ffn_ln_g, L0_ffn_ln_b, L0_ffn_abel_w, L0_ffn_abel_b, L0_ffn_gate_w_moe, L0_ffn_gate_b_moe, L0_ffn_w1, L0_ffn_b1, L0_ffn_w2, L0_ffn_b2, L0_ffn_gens, L0_ffn_mix_w, L0_ffn_mix_b):

    def _L0_attn_a_ref(x, Wq, Wk, Wv, Wo, gamma, beta, Wg1, Wg2):
        import jax, jax.numpy as jnp
        import numpy as np
        E = 128
        H = 16
        D = E // H
        B = 2
        N = 1024
        CHUNK = 128
        LAYER_IDX = 0
        NUM_LAYERS = 12
        EPS = 1e-05

        def _build_slopes(n):

            def po2(m):
                start = 2.0 ** (-2.0 ** (-(np.log2(m) - 3)))
                return [start * start ** i for i in range(m)]
            if np.log2(n).is_integer():
                return po2(n)
            closest = 2 ** int(np.floor(np.log2(n)))
            return po2(closest) + _build_slopes(2 * closest)[0::2][:n - closest]

        def _slope_rate():
            s = np.array(_build_slopes(H), dtype=np.float32)
            s = s * (1.0 - LAYER_IDX / (NUM_LAYERS - 1) + 1e-05)
            return jnp.asarray(s)

        def lightning_attn(q, k, v, s):
            b, h, n, d = q.shape
            nc = n // CHUNK
            idx = jnp.arange(CHUNK, dtype=q.dtype)
            diff = idx[:, None] - idx[None, :]
            mask = jnp.where(diff >= 0, jnp.exp(-s[:, None, None] * diff), 0.0)
            lam_q = jnp.exp(-s[:, None] * (idx + 1.0))
            lam_k = jnp.exp(-s[:, None] * (CHUNK - 1.0 - idx))
            lam_c = jnp.exp(-s * CHUNK)

            def to_chunks(t):
                return t.reshape(b, h, nc, CHUNK, d).transpose(2, 0, 1, 3, 4)
            qc, kc, vc = (to_chunks(q), to_chunks(k), to_chunks(v))

            def step(kv, xs):
                qi, ki, vi = xs
                scores = jnp.einsum('bhid,bhjd->bhij', qi, ki) * mask
                o = jnp.einsum('bhij,bhjd->bhid', scores, vi)
                o = o + lam_q[:, :, None] * jnp.einsum('bhid,bhde->bhie', qi, kv)
                kv = lam_c[:, None, None] * kv + jnp.einsum('bhid,bhie->bhde', ki * lam_k[:, :, None], vi)
                return (kv, o)
            kv0 = jnp.zeros((b, h, d, d), q.dtype)
            _, o = jax.lax.scan(step, kv0, (qc, kc, vc))
            return o.transpose(1, 2, 0, 3, 4).reshape(b, h, n, d)
        b, n, e = x.shape
        s = _slope_rate()
        silu = jax.nn.silu
        q = silu(x @ Wq)
        k = silu(x @ Wk)
        v = silu(x @ Wv)
        split = lambda t: t.reshape(b, n, H, D).transpose(0, 2, 1, 3)
        o = lightning_attn(split(q), split(k), split(v), s)
        o = o.transpose(0, 2, 1, 3).reshape(b, n, e)
        mu = jnp.mean(o, axis=-1, keepdims=True)
        var = jnp.var(o, axis=-1, keepdims=True)
        o = (o - mu) * jax.lax.rsqrt(var + EPS) * gamma + beta
        gate = jax.nn.sigmoid(x @ Wg1 @ Wg2)
        return o * gate @ Wo

    def _L0_attn_b_ref(x, W_qkv, b_qkv, W_out, b_out):
        import jax, jax.numpy as jnp
        import numpy as np
        import math
        EMBED_DIM = 128
        NUM_HEADS = 16
        HEAD_DIM = EMBED_DIM // NUM_HEADS
        B, S, D = x.shape
        H, Hd = (NUM_HEADS, HEAD_DIM)
        slopes = jnp.power(2.0, 8.0 * jnp.arange(0, -H, -1, dtype=jnp.float32) / H)
        qkv = x @ W_qkv.T + b_qkv
        qkv = qkv.reshape(B, S, 3, H, Hd).transpose(2, 0, 3, 1, 4)
        q, k, v = (qkv[0], qkv[1], qkv[2])
        scores = jnp.einsum('bhqd,bhkd->bhqk', q, k) / math.sqrt(Hd)
        pos = jnp.arange(S)
        rel = jnp.abs(pos[None, :] - pos[:, None]).astype(jnp.float32)
        bias = -slopes[:, None, None] * rel
        probs = jax.nn.softmax(scores + bias[None], axis=-1)
        out = jnp.einsum('bhqk,bhkd->bhqd', probs, v)
        out = out.transpose(0, 2, 1, 3).reshape(B, S, D)
        return out @ W_out.T + b_out

    def _L0_ffn_ref(x, ln_g, ln_b, abel_w, abel_b, gate_w_moe, gate_b_moe, w1, b1, w2, b2, gens, mix_w, mix_b):
        import jax, jax.numpy as jnp
        import numpy as np
        from jax.scipy.linalg import expm
        B, S, D, E, K, NROT = (2, 256, 128, 8, 2, 3)
        DF = 4 * D
        EPS = 1e-05
        residual = x
        mu = jnp.mean(x, axis=-1, keepdims=True)
        var = jnp.mean((x - mu) ** 2, axis=-1, keepdims=True)
        xn = (x - mu) * jax.lax.rsqrt(var + EPS) * ln_g + ln_b
        abel = jax.nn.gelu(xn @ abel_w + abel_b, approximate=False)
        logits = xn @ gate_w_moe + gate_b_moe
        tw, ti = jax.lax.top_k(logits, K)
        tw = jax.nn.softmax(tw, axis=-1)
        onehot = (ti[..., None] == jnp.arange(E)).astype(tw.dtype)
        wdense = jnp.sum(tw[..., None] * onehot, axis=2)
        h = jax.nn.gelu(jnp.einsum('bsd,edf->besf', xn, w1) + b1[None, :, None, :], approximate=False)
        eo = jnp.einsum('besf,efd->besd', h, w2) + b2[None, :, None, :]
        moe = jnp.einsum('besd,bse->bsd', eo, wdense)
        rot = expm(gens[0])
        for i in range(1, NROT):
            rot = rot @ expm(gens[i])
        nonabel = moe @ rot
        combined = jnp.concatenate([abel, nonabel], axis=-1)
        g = jax.nn.sigmoid(combined @ mix_w + mix_b)
        return residual + abel * (1.0 - g) + nonabel * g
    x = L0_attn_a_x
    x = x + _L0_attn_a_ref(_layernorm(x, axis=-1), L0_attn_a_Wq, L0_attn_a_Wk, L0_attn_a_Wv, L0_attn_a_Wo, L0_attn_a_gamma, L0_attn_a_beta, L0_attn_a_Wg1, L0_attn_a_Wg2)
    x = x + _L0_ffn_ref(_layernorm(x, axis=-1), L0_ffn_ln_g, L0_ffn_ln_b, L0_ffn_abel_w, L0_ffn_abel_b, L0_ffn_gate_w_moe, L0_ffn_gate_b_moe, L0_ffn_w1, L0_ffn_b1, L0_ffn_w2, L0_ffn_b2, L0_ffn_gens, L0_ffn_mix_w, L0_ffn_mix_b)
    x = x + _L0_attn_b_ref(_layernorm(x, axis=-1), L0_attn_b_W_qkv, L0_attn_b_b_qkv, L0_attn_b_W_out, L0_attn_b_b_out)
    x = x + _L0_ffn_ref(_layernorm(x, axis=-1), L0_ffn_ln_g, L0_ffn_ln_b, L0_ffn_abel_w, L0_ffn_abel_b, L0_ffn_gate_w_moe, L0_ffn_gate_b_moe, L0_ffn_w1, L0_ffn_b1, L0_ffn_w2, L0_ffn_b2, L0_ffn_gens, L0_ffn_mix_w, L0_ffn_mix_b)
    return x

_drawn_inputs = setup_inputs


def setup_inputs(seed=0):
    import zlib

    import numpy as np

    out = dict(_drawn_inputs(seed))
    spreads = {'L0_attn_a_gamma': (1.0, 0.2),
     'L0_attn_a_beta': (0.0, 0.1),
     'L0_ffn_ln_g': (1.0, 0.2),
     'L0_ffn_ln_b': (0.0, 0.1),
     'L0_ffn_abel_b': (0.0, 0.326),
     'L0_ffn_gate_b_moe': (0.0, 0.1),
     'L0_ffn_b1': (0.0, 0.328),
     'L0_ffn_b2': (0.0, 0.1)}
    factors = {'L0_attn_b_b_qkv': 8.0, 'L0_attn_b_b_out': 8.0}
    for name, (base, spread) in spreads.items():
        noise = np.random.default_rng([zlib.crc32(name.encode()), seed]).standard_normal(out[name].shape)
        drawn = base * np.exp(spread * noise) if base else spread * noise
        out[name] = jnp.asarray(drawn.astype(out[name].dtype))
    for name, factor in factors.items():
        out[name] = (out[name] * factor).astype(out[name].dtype)
    return out
```

```python
from contextlib import ExitStack

import numpy as np

import concourse.bass as bass
from concourse import mybir

ALU = mybir.AluOpType
ACT = mybir.ActivationFunctionType
AX = mybir.AxisListType
F32 = mybir.dt.float32
F32R = mybir.dt.float32r
I32 = mybir.dt.int32

P = 128
BATCH, SEQ = 4, 1024
H, D = 16, 8
TPB = SEQ // P
NT = BATCH * TPB
SLOTS, R = 4, 4
PART = 32
ROWS = 3 * D
AUG = 4
SHIFT = ROWS + AUG
EXPERTS, DF = 8, 512
FC = DF // P
GROUP = 4
NG = NT // GROUP
EPS = 1e-5
NROT = 3
TAYLOR = 14
THETA = 2.0
SQUARINGS = 16
QSCALE = float(D) ** -0.5


class Signal:

    def __init__(self, sem, per, unit=1):
        self.sem, self.per, self.unit = sem, per, unit

    def prime(self, eng):
        eng.sem_inc(self.sem, self.per * self.unit)

    def wait(self, eng, i, k):
        assert -self.per <= k < self.per
        eng.wait_ge(self.sem, (i + 1) * (self.per * self.unit) + (k + 1) * self.unit)


class Steps:

    def __init__(self, sem):
        self.sem, self.done, self.here, self.turn, self.per = sem, 0, 0, 0, 0

    def loop(self, i, per):
        self.done += self.here
        self.turn, self.per, self.here = i, per, 0

    def end(self, turns):
        assert self.here == self.per, (self.here, self.per)
        self.done += self.per * turns
        self.turn, self.per, self.here = 0, 0, 0

    def add(self, ins):
        ins.then_inc(self.sem, 1)
        self.here += 1

    def settle(self, eng):
        eng.wait_ge(self.sem, self.turn * self.per + (self.done + self.here))

    def chain(self, eng, ins):
        self.add(ins)
        self.settle(eng)


def alibi_slopes():
    return np.power(np.float32(2.0), np.float32(8.0) * np.arange(0, -H, -1, dtype=np.float32) / np.float32(H)).astype(np.float32)


def build(nc, I, out, upto=(1, 2, 3, 4)):
    SL = [float(x) for x in alibi_slopes()]
    ctx = ExitStack()
    with ctx:
        def sem(name):
            return ctx.enter_context(nc.semaphore(name))

        def sb(name, shape, dt=F32, scope=ctx):
            return scope.enter_context(nc.sbuf_tensor(name, shape, dt))

        bank = [ctx.enter_context(nc.psum_tensor(f"bank{i}", [P, 512], F32)) for i in range(2)]
        pairA = ctx.enter_context(nc.psum_tensor("pairA", [P, 1024], F32))
        pairB = ctx.enter_context(nc.psum_tensor("pairB", [P, 1024], F32))
        pairC = ctx.enter_context(nc.psum_tensor("pairC", [P, 1024], F32))
        bank += [pairA[:, 0:512], pairA[:, 512:1024], pairB[:, 0:512], pairB[:, 512:1024],
                 pairC[:, 0:512], pairC[:, 512:1024]]
        bank[0], bank[1] = bank[0][:, :], bank[1][:, :]

        X = sb("X", [P, NT, P])
        ident = sb("ident", [P, P])
        w2r = sb("w2r", [P, EXPERTS * FC, P])
        b2r = sb("b2r", [EXPERTS, P])
        XN = sb("XN", [P, TPB, P])
        XTB = sb("XTB", [P, SEQ])
        stats = sb("stats", [P, TPB, 6])
        mv = sb("mv", [P, TPB, 2])
        rstd = sb("rstd", [P, TPB])
        rstd2 = sb("rstd2", [P, TPB])
        rall = sb("rall", [P, TPB])
        mhalf = sb("mhalf", [P, TPB])
        Wqa = sb("Wqa", [P, SLOTS, P])
        Wka = sb("Wka", [P, SLOTS, P])
        Wnat = sb("Wnat", [P, 4 * P])
        Wg1T = sb("Wg1T", [D, P])
        Wg2 = sb("Wg2", [D, P])
        Woa = sb("Woa", [P, P])
        gam = sb("gam", [P, P])
        bet = sb("bet", [P, P])
        Wqb = sb("Wqb", [P, SLOTS, P])
        Wkb = sb("Wkb", [P, SLOTS, P])
        Wvb = sb("Wvb", [P, P])
        Wob = sb("Wob", [P, P])
        qbias = sb("qbias", [P, SLOTS])
        kbias = sb("kbias", [P, SLOTS])
        vbias = sb("vbias", [P, P])
        obias = sb("obias", [P, P])
        negq = sb("negq", [P, 1])
        negk = sb("negk", [P, 1])
        lngT = sb("lngT", [P, 1])
        lnbT = sb("lnbT", [P, 1])
        Wab = sb("Wab", [P, P + EXPERTS])
        abias = sb("abias", [P, P + EXPERTS])
        b1T = sb("b1T", [P, EXPERTS * FC])
        mixa = sb("mixa", [P, P])
        mixn = sb("mixn", [P, P])
        mixb = sb("mixb", [P, 1])
        rank8 = sb("rank8", [P, EXPERTS])

        v_steps = Steps(sem("vector_steps"))
        g_steps = Steps(sem("gpsimd_steps"))
        x_loaded = sem("x_loaded")
        passed = sem("waits_passed")

        def pass_wait(e):
            e.sem_inc(passed, 1)

        w_loaded = sem("weights_loaded")
        gens_loaded = sem("gens_loaded")
        w2_loaded = sem("w2_loaded")
        out_stored = sem("out_stored")

        with ExitStack() as es:
            A = sb("A", [P, NROT, P], scope=es)
            AT = sb("AT", [P, NROT, P], scope=es)
            M = sb("M", [P, NROT, P], scope=es)
            MT = sb("MT", [P, NROT, P], scope=es)
            rot = sb("rot", [P, P], scope=es)
            rot12 = sb("rot12", [P, P], scope=es)
            w2T = sb("w2T", [P, EXPERTS, DF], scope=es)
            b2T = sb("b2T", [P, EXPERTS], scope=es)
            inv = sb("inv", [P, TAYLOR], scope=es)
            thr = sb("thr", [P, SQUARINGS, NROT], scope=es)
            norm = sb("norm", [P, NROT], scope=es)
            norms = sb("norms", [P, NROT], scope=es)
            act_f = sb("act_f", [P, SQUARINGS, NROT], scope=es)
            now_i = sb("now_i", [P, NROT], I32, scope=es)
            act_i = sb("act_i", [P, SQUARINGS, NROT], I32, scope=es)
            fac = sb("fac", [P, SQUARINGS, NROT], scope=es)
        norm_row = sem("norm_row")
        norm_all = sem("norm_all")
        exp_in = sem("exp_in")
        prod_done = Signal(sem("prod_done"), 2)
        next_done = Signal(sem("next_done"), 2)
        sq_done = Signal(sem("sq_done"), 2)
        sel_done = Signal(sem("sel_done"), 2)
        rot_done = sem("rot_done")
        rot_copied = sem("rot_copied")
        fold_done = sem("fold_done")
        fold_copied = sem("fold_copied")
        gate_w_done = sem("gate_w_done")
        gate_w_copied = sem("gate_w_copied")

        def expm_vector(e):
            e.wait_ge(gens_loaded, 16 * 5)
            e.tensor_reduce(norm[:, :], A[:, :, :], AX.X, ALU.add, apply_absolute_value=True).then_inc(norm_row, 1)
            e.wait_ge(norm_all, 1)
            v_steps.chain(e, e.tensor_tensor(act_f[:, :, :], norms[:, None, :].to_broadcast([P, SQUARINGS, NROT]),
                                             thr[:, :, :], ALU.is_gt))
            v_steps.add(e.tensor_copy(act_i[:, :, :], act_f[:, :, :]))
            v_steps.chain(e, e.tensor_scalar(fac[:, :, :], act_f[:, :, :], -0.5, 1.0, ALU.mult, ALU.add))
            n = SQUARINGS // 2
            while n:
                v_steps.chain(e, e.tensor_tensor(fac[:, 0:n, :], fac[:, 0:n, :], fac[:, n:2 * n, :], ALU.mult))
                n //= 2
            for m in (A, AT):
                v_steps.chain(e, e.tensor_tensor(m[:, :, :], m[:, :, :],
                                                 fac[:, 0, :].unsqueeze(2).to_broadcast([P, NROT, P]), ALU.mult))
            for m, last in ((M, False), (MT, True)):
                ins = e.tensor_copy(m[:, :, :], ident[:, None, :].to_broadcast([P, NROT, P]))
                ins.then_inc(exp_in, 1) if last else v_steps.chain(e, ins)
            next_done.prime(e)
            sel_done.prime(e)
            with e.Fori(0, TAYLOR) as i:
                for k, m in enumerate((M, MT)):
                    prod_done.wait(e, i, 1)
                    e.scalar_tensor_tensor(out=m[:, :, :], in0=bank[k][:, 0:NROT * P].rearrange("p (j n) -> p j n", n=P),
                                           scalar=inv[:, bass.ds(i, 1)],
                                           in1=ident[:, None, :].to_broadcast([P, NROT, P]),
                                           op0=ALU.mult, op1=ALU.add).then_inc(next_done.sem, 1)
            with e.Fori(0, SQUARINGS) as i:
                v_steps.loop(i, 1)
                sel_done.wait(e, i, -1)
                v_steps.chain(e, e.tensor_copy(now_i[:, :], act_i[:, bass.ds(i, 1), :].rearrange("p a j -> p (a j)")))
                for k, m in enumerate((M, MT)):
                    sq_done.wait(e, i, 1)
                    pass_wait(e)
                    e.copy_predicated(m[:, :, :], now_i[:, :].unsqueeze(2).to_broadcast([P, NROT, P]),
                                      bank[k][:, 0:NROT * P].rearrange("p (j n) -> p j n", n=P)).then_inc(sel_done.sem, 1)
            v_steps.end(SQUARINGS)
            for k, m in enumerate((rot12, rot)):
                e.wait_ge(rot_done, k + 1)
                e.tensor_copy(m[:, :], bank[0][:, 0:P]).then_inc(rot_copied, 1)
            for q in range(EXPERTS * FC // 4):
                e.wait_ge(fold_done, q + 1)
                e.tensor_copy(w2r[:, 4 * q:4 * q + 4, :].rearrange("p c n -> p (c n)"), bank[q % 2]).then_inc(fold_copied, 1)
            e.wait_ge(fold_done, EXPERTS + 1)
            e.tensor_copy(b2r[:, :], bank[0][0:EXPERTS, 0:P]).then_inc(fold_copied, 1)

        def expm_gpsimd(e):
            g_steps.chain(e, e.memset(mhalf[:, :], -0.5))
            e.wait_ge(norm_row, 1)
            e.partition_all_reduce(norms[:, :], norm[:, :], P, bass.bass_isa.ReduceOp.max).then_inc(norm_all, 1)

        def expm_tensor(e):
            e.wait_ge(w_loaded, 16 * N_WLOADS)
            e.matmul(bank[0][:, 0:P], Wg1T[:, :], Wg2[:, :], start=True, stop=True).then_inc(gate_w_done, 1)
            e.wait_ge(gate_w_copied, 1)
            e.wait_ge(exp_in, 1)
            prod_done.prime(e)
            sq_done.prime(e)

            def products(lefts, done):
                for k, (left, right) in enumerate(lefts):
                    for j in range(NROT):
                        last = e.matmul(bank[k][:, j * P:(j + 1) * P], left[:, j, :], right[:, j, :], start=True, stop=True)
                    last.then_inc(done.sem, 1)
            with e.Fori(0, TAYLOR) as i:
                next_done.wait(e, i, -1)
                products([(AT, M), (A, MT)], prod_done)
            next_done.wait(e, TAYLOR - 1, 1)
            with e.Fori(0, SQUARINGS) as i:
                sel_done.wait(e, i, -1)
                products([(MT, M), (M, MT)], sq_done)
            sel_done.wait(e, SQUARINGS - 1, 1)
            e.matmul(bank[0][:, 0:P], MT[:, 1, :], M[:, 2, :], start=True, stop=True).then_inc(rot_done, 1)
            e.wait_ge(rot_copied, 1)
            e.matmul(bank[0][:, 0:P], MT[:, 0, :], rot12[:, :], start=True, stop=True).then_inc(rot_done, 1)
            e.wait_ge(rot_copied, 2)
            e.wait_ge(w2_loaded, 32)
            for q in range(EXPERTS):
                if q >= 2:
                    e.wait_ge(fold_copied, q - 1)
                for c in range(FC):
                    last = e.matmul(bank[q % 2][:, c * P:(c + 1) * P], w2T[:, q, c * P:(c + 1) * P], rot[:, :], start=True, stop=True)
                last.then_inc(fold_done, 1)
            e.wait_ge(fold_copied, EXPERTS)
            e.matmul(bank[0][0:EXPERTS, 0:P], b2T[:, :], rot[:, :], start=True, stop=True).then_inc(fold_done, 1)

        def inverse_root(e, out, var):
            pass_wait(e)
            g_steps.chain(e, e.tensor_scalar(out, var, EPS, None, ALU.add))
            return e.tensor_tensor(out, out, mhalf[:, 0:out.shape[1]], ALU.pow)

        class Norm:

            def __init__(self, name, twice=False):
                self.twice = twice
                self.stats_ready = Signal(sem(name + "_stats_ready"), 1)
                self.rstd_ready = Signal(sem(name + "_rstd_ready"), 1)
                self.xn_ready = Signal(sem(name + "_xn_ready"), 2)

            def prime_vector(self, e):
                self.stats_ready.prime(e)
                self.xn_ready.prime(e)

            def prime_gpsimd(self, e):
                self.rstd_ready.prime(e)

            def vector(self, e, i, keep=None):
                for t in range(TPB):
                    v_steps.add(e.bn_stats(stats[:, t, :], X[:, bass.ds(i * TPB + t, 1), :].rearrange("p a d -> p (a d)")))
                v_steps.settle(e)
                pass_wait(e)
                for t in range(TPB):
                    ins = e.bn_aggr(mv[:, t, :], stats[:, t, :])
                    ins.then_inc(self.stats_ready.sem, 1) if t == TPB - 1 else v_steps.add(ins)
                self.rstd_ready.wait(e, i, 0)
                for t in range(TPB):
                    ins = e.tensor_scalar(XN[:, t, :], X[:, bass.ds(i * TPB + t, 1), :].rearrange("p a d -> p (a d)"),
                                          mv[:, t, 0:1], (rall if self.twice else rstd)[:, t:t + 1], ALU.subtract, ALU.mult)
                    ins.then_inc(self.xn_ready.sem, 1) if t % GROUP == GROUP - 1 else v_steps.add(ins)
                if keep is not None:
                    for t in range(TPB):
                        v_steps.add(e.tensor_scalar(keep[:, bass.ds(i * TPB + t, 1), :].rearrange("p a d -> p (a d)"),
                                                    X[:, bass.ds(i * TPB + t, 1), :].rearrange("p a d -> p (a d)"),
                                                    mv[:, t, 0:1], rstd[:, t:t + 1], ALU.subtract, ALU.mult))

            def gpsimd(self, e, i):
                self.stats_ready.wait(e, i, 0)
                var = mv[:, :, 1]
                if not self.twice:
                    inverse_root(e, rstd[:, :], var).then_inc(self.rstd_ready.sem, 1)
                    return
                g_steps.chain(e, inverse_root(e, rstd[:, :], var))
                g_steps.chain(e, e.tensor_tensor(rstd2[:, :], var, rstd[:, :], ALU.mult))
                g_steps.chain(e, e.tensor_tensor(rstd2[:, :], rstd2[:, :], rstd[:, :], ALU.mult))
                g_steps.chain(e, inverse_root(e, rstd2[:, :], rstd2[:, :]))
                e.tensor_tensor(rall[:, :], rstd[:, :], rstd2[:, :], ALU.mult).then_inc(self.rstd_ready.sem, 1)

            def transposes(self, e, i, half, to):
                self.xn_ready.wait(e, i, half)
                for j in range(GROUP):
                    last = e.transpose(to[:, j * P:(j + 1) * P], XN[:, GROUP * half + j, :], ident[:, :])
                return last

        att = ExitStack()
        Qpad = sb("Qpad", [P, SLOTS, R, SEQ], F32R, att)
        KA = sb("KA", [P, SLOTS, SEQ], F32R, att)
        T = sb("T", [P, 2, 512], scope=att)
        TH = sb("TH", [P, 2, 512], F32R, att)
        V9 = sb("V9", [P, TPB, H, D + 1], scope=att)
        TR = XTB

        zeroed = sem("zeroed")

        aa = ExitStack()
        QST = sb("QST", [P, 2, SEQ], F32R, aa)
        maskT = sb("maskT", [P, H, P], scope=aa)
        sel = sb("sel", [P, SLOTS, P], scope=aa)
        lamq = sb("lamq", [P, P], scope=aa)
        lamk = sb("lamk", [P, P], scope=aa)
        lamc = sb("lamc", [P, 1], scope=aa)
        blk = sb("blk", [P, P], scope=aa)
        KN = sb("KN", [P, TPB, P], scope=aa)
        GT = sb("GT", [P, TPB, P], scope=aa)
        GB = sb("GB", [P, TPB, P], scope=aa)
        QL = sb("QL", [P, TPB, P], scope=aa)
        PA = sb("PA", [P, 2, 512], scope=aa)
        OTS = sb("OTS", [P, 2, 512], scope=aa)
        KV = sb("KV", [P, 2, P], scope=aa)
        KVN = sb("KVN", [P, P], scope=aa)
        ONS = sb("ONS", [P, GROUP, P], scope=aa)
        aa.close()
        ab = ExitStack()
        KB = sb("KB", [P, SLOTS, SEQ], F32R, ab)
        EX = sb("EX", [P, 8, SEQ], scope=ab)
        over = sb("over", [P, P], scope=ab)
        overT = sb("overT", [P, P], scope=ab)
        OTB = T[:, :, :].rearrange("p a n -> p (a n)")
        MX = sb("MX", [P, PART], scope=ab)
        MXT = sb("MXT", [PART, P], F32R, ab)
        DEN = sb("DEN", [P, GROUP, R], scope=ab)
        ATT = XN
        qbs = sb("qbs", [P, SLOTS], scope=ab)
        ab.close()
        att.close()

        AJ = 30
        a_norm = Norm("a")
        a_job = Signal(sem("a_job_done"), AJ)
        a_evac = Signal(sem("a_job_evacuated"), AJ)
        a_split = Signal(sem("a_split_done"), 16)
        a_qpad = [Signal(sem(f"a_q_padded{s}"), 1, 16 * R) for s in range(SLOTS)]
        a_score = Signal(sem("a_scores_done"), 4 * TPB)
        a_masked = Signal(sem("a_masked"), 4 * TPB)
        a_pv = Signal(sem("a_pv_done"), 4 * TPB)
        a_ot = Signal(sem("a_ot_evacuated"), TPB)
        a_on = Signal(sem("a_o_natural"), TPB)
        a_onorm = Signal(sem("a_o_normed"), 2)
        a_ostat = Signal(sem("a_o_stats"), 2)
        a_orstd = Signal(sem("a_o_rstd"), 2)
        a_y = Signal(sem("a_y_ready"), 2)
        a_aux = Signal(sem("a_aux_done"), TPB - 1 + 2)
        a_auxr = Signal(sem("a_aux_read"), TPB - 1 + 2)
        a_kv = Signal(sem("a_state_ready"), TPB - 1)
        a_pool = Signal(sem("a_decayed"), 2)
        a_tables = sem("a_tables_loaded")
        ot_zero = sem("ot_zeroed")

        U7 = TPB - 1
        LAST = 4 * TPB + 8

        def aux_index(kind, n):
            order = [("kv", 0), ("kv", 1), ("kv", 2), ("kv", 3), ("kv", 4), ("kv", 5), ("y", 0), ("kv", 6), ("y", 1)]
            return order.index((kind, n))

        def a_steps(u):
            return {
                "score": u if u < 32 else None,
                "pv": u - 1 if 1 <= u <= 32 else None,
                "kv": (u - 2) // 4 if u % 4 == 2 and (u - 2) // 4 < U7 else None,
                "sel": (u - 6) // 4 if u >= 6 and u % 4 == 2 and (u - 6) // 4 < TPB else None,
                "ot": (u - 4) // 4 if u >= 4 and u % 4 == 0 and (u - 4) // 4 < TPB else None,
                "norm": {19: 0, 35: 1}.get(u),
                "turn": {23: 0, 36: 1}.get(u),
                "y": {25: 0, 37: 1}.get(u),
            }

        def attn_a_sync(e):
            for s in a_qpad:
                s.prime(e)
            e.wait_ge(zeroed, 1)
            with e.Fori(0, BATCH) as i:
                for s in range(SLOTS):
                    a_split.wait(e, i, 4 * s + 1)
                    pass_wait(e)
                    a_masked.wait(e, i, -1)
                    for r in range(R):
                        e.dma_start(Qpad[PART * r:PART * r + ROWS, s, r, :].bitcast(F32),
                                    QST[PART * r:PART * r + ROWS, s % 2, :].bitcast(F32)).then_inc(a_qpad[s].sem, 16)

        def attn_a_gpsimd(e):
            a_norm.prime_gpsimd(e)
            a_pool.prime(e)
            a_orstd.prime(e)
            a_y.prime(e)
            e.wait_ge(a_tables, 16 * 6)
            e.wait_ge(w_loaded, 16 * N_WLOADS)
            with e.Fori(0, BATCH) as i:
                g_steps.loop(i, 8)
                a_norm.gpsimd(e, i)
                a_evac.wait(e, i, 2 + 16 + 7)
                def rows(t):
                    return t[:, None, :].to_broadcast([P, TPB, P])
                g_steps.add(e.tensor_tensor(KN[:, :, :], KN[:, :, :], rows(lamk), ALU.mult))
                pass_wait(e)
                g_steps.chain(e, e.tensor_scalar(GT[:, :, :], GT[:, :, :], 0.5, 0.5, ALU.mult, ALU.add))
                g_steps.chain(e, e.tensor_tensor(GB[:, :, :], GT[:, :, :], rows(bet), ALU.mult))
                e.tensor_tensor(GT[:, :, :], GT[:, :, :], rows(gam), ALU.mult).then_inc(a_pool.sem, 1)
                a_evac.wait(e, i, 2 + 16 + 8 + 1)
                e.tensor_tensor(QL[:, :, :], QL[:, :, :], rows(lamq), ALU.mult).then_inc(a_pool.sem, 1)
                for g in range(2):
                    a_ostat.wait(e, i, g)
                    inverse_root(e, rstd2[:, 4 * g:4 * g + 4], mv[:, 4 * g:4 * g + 4, 1]).then_inc(a_orstd.sem, 1)
                    a_onorm.wait(e, i, g)
                    a_pool.wait(e, i, 1)
                    g_steps.chain(e, e.tensor_tensor(ONS[:, :, :], ONS[:, :, :], GT[:, 4 * g:4 * g + 4, :], ALU.mult))
                    e.tensor_tensor(ONS[:, :, :], ONS[:, :, :], GB[:, 4 * g:4 * g + 4, :], ALU.add).then_inc(a_y.sem, 1)
            g_steps.end(BATCH)

        def attn_a_scalar(e):
            a_evac.prime(e)
            a_ot.prime(e)
            with e.Fori(0, BATCH) as i:
                def job(n):
                    a_job.wait(e, i, n)
                    return bank[n % 2]
                for half in range(2):
                    e.activation(XTB[:, half * 512:(half + 1) * 512], job(half), ACT.Copy).then_inc(a_evac.sem, 1)
                for m in range(16):
                    a_split.wait(e, i, m - 2)
                    e.activation(T[:, m % 2, :], job(2 + m), ACT.Silu).then_inc(a_evac.sem, 1)
                for c in range(TPB):
                    b = job(18 + c)
                    e.activation(KN[:, c, :], b[:, 0:P], ACT.Silu)
                    e.activation(V9[:, c, :, 0:D], b[:, P:2 * P].rearrange("p (h d) -> p h d", d=D), ACT.Silu)
                    e.activation(GT[:, c, :], b[:, 2 * P:3 * P], ACT.Tanh, scale=0.5).then_inc(a_evac.sem, 1)
                for half in range(2):
                    e.activation(QL[:, 4 * half:4 * half + 4, :].rearrange("p c n -> p (c n)"), job(26 + half), ACT.Silu).then_inc(a_evac.sem, 1)
                for u in range(LAST):
                    w = a_steps(u)
                    if w["ot"] is not None:
                        c = w["ot"]
                        a_pv.wait(e, i, 4 * c + 3)
                        a_on.wait(e, i, c - 2)
                        e.activation(OTS[:, c % 2, :], bank[4 + c % 2], ACT.Copy).then_inc(a_ot.sem, 1)
                    if w["turn"] is not None:
                        g = w["turn"]
                        e.activation(TR[:, g * 512:(g + 1) * 512], job(28 + g), ACT.Copy).then_inc(a_evac.sem, 1)

        def attn_a_vector(e):
            a_norm.prime_vector(e)
            for s in (a_split, a_masked, a_onorm, a_ostat, a_auxr, a_kv):
                s.prime(e)
            e.wait_ge(gate_w_done, 1)
            e.tensor_copy(Wnat[:, 2 * P:3 * P], bank[0][:, 0:P]).then_inc(gate_w_copied, 1)

        def attn_a_vector_loop(e):
            e.memset(bank[4], 0.0).then_inc(ot_zero, 1)
            e.memset(bank[5], 0.0).then_inc(ot_zero, 1)
            e.wait_ge(a_tables, 16 * 6)
            with e.Fori(0, BATCH) as i:
                v_steps.loop(i, A_V)
                a_norm.vector(e, i)
                for m in range(16):
                    s, side, half = m // 4, (m // 2) % 2, m % 2
                    a_evac.wait(e, i, 2 + m)
                    if side == 0 and half == 0:
                        a_qpad[s - 2].wait(e, i, 0 if s >= 2 else -1)
                    v_steps.chain(e, e.tensor_copy(TH[:, m % 2, :], T[:, m % 2, :]))
                    to = (QST[:, s % 2, half * 512:(half + 1) * 512] if side == 0 else KA[:, s, half * 512:(half + 1) * 512])
                    e.scalar_tensor_tensor(out=to, in0=TH[:, m % 2, :].bitcast(F32), scalar=(negq if side == 0 else negk)[:, 0:1],
                                           in1=T[:, m % 2, :], op0=ALU.mult, op1=ALU.add).then_inc(a_split.sem, 1)
                for u in range(LAST):
                    w = a_steps(u)
                    if w["score"] is not None:
                        s = u % 4
                        a_score.wait(e, i, u)
                        a_pv.wait(e, i, u - 2)
                        e.tensor_tensor(PA[:, u % 2, :], bank[2 + u % 2], maskT[:, 4 * s:4 * s + 4, :].rearrange("p h n -> p (h n)"),
                                        ALU.mult).then_inc(a_masked.sem, 1)
                    if w["kv"] is not None:
                        c = w["kv"]
                        a_aux.wait(e, i, aux_index("kv", c))
                        e.tensor_tensor(KVN[:, :], bank[7][:, 0:P], blk[:, :], ALU.mult).then_inc(a_auxr.sem, 1)
                        a_auxr.wait(e, i, aux_index("kv", c))
                        to = KV[:, (c + 1) % 2, :]
                        if c == 0:
                            a_on.wait(e, i, -1)
                            e.tensor_copy(to, KVN[:, :]).then_inc(a_kv.sem, 1)
                        else:
                            a_on.wait(e, i, c - 1)
                            a_kv.wait(e, i, c - 1)
                            e.scalar_tensor_tensor(out=to, in0=KV[:, c % 2, :], scalar=lamc[:, 0:1], in1=KVN[:, :],
                                                   op0=ALU.mult, op1=ALU.add).then_inc(a_kv.sem, 1)
                    if w["norm"] is not None:
                        g = w["norm"]
                        a_on.wait(e, i, 4 * g + 3)
                        for j in range(4):
                            v_steps.add(e.bn_stats(stats[:, 4 * g + j, :], bank[6][:, j * P:(j + 1) * P]))
                        v_steps.settle(e)
                        pass_wait(e)
                        for j in range(4):
                            ins = e.bn_aggr(mv[:, 4 * g + j, :], stats[:, 4 * g + j, :])
                            ins.then_inc(a_ostat.sem, 1) if j == 3 else v_steps.add(ins)
                        a_orstd.wait(e, i, g)
                        if g == 1:
                            a_job.wait(e, i, 28)
                        else:
                            a_job.wait(e, i, -1)
                        for j in range(4):
                            ins = e.tensor_scalar(ONS[:, j, :], bank[6][:, j * P:(j + 1) * P], mv[:, 4 * g + j, 0:1],
                                                  rstd2[:, 4 * g + j:4 * g + j + 1], ALU.subtract, ALU.mult)
                            ins.then_inc(a_onorm.sem, 1) if j == 3 else v_steps.add(ins)
                    if w["y"] is not None:
                        g = w["y"]
                        a_aux.wait(e, i, aux_index("y", g))
                        xs = X[:, bass.ds(i * TPB + 4 * g, 4), :]
                        e.tensor_tensor(xs, bank[7].rearrange("p (t n) -> p t n", n=P), xs, ALU.add).then_inc(a_auxr.sem, 1)
                        a_auxr.wait(e, i, aux_index("y", g))
            v_steps.end(BATCH)

        A_V = 8 + 7 + 6 + 16 + 2 * (4 + 3 + 3)

        def attn_a_tensor(e):
            for s in (a_job, a_score, a_pv, a_on, a_aux):
                s.prime(e)
            e.wait_ge(ot_zero, 2)
            with e.Fori(0, BATCH) as i:
                def job(n):
                    a_evac.wait(e, i, n - 2)
                    return bank[n % 2]
                for half in range(2):
                    b = job(half)
                    a_norm.transposes(e, i, half, b).then_inc(a_job.sem, 1)
                a_evac.wait(e, i, 1)
                for m in range(16):
                    s, side, half = m // 4, (m // 2) % 2, m % 2
                    e.matmul(job(2 + m), (Wqa if side == 0 else Wka)[:, s, :], XTB[:, half * 512:(half + 1) * 512],
                             start=True, stop=True).then_inc(a_job.sem, 1)
                for c in range(TPB):
                    e.matmul(job(18 + c)[:, 0:3 * P], XTB[:, c * P:(c + 1) * P], Wnat[:, 0:3 * P], start=True, stop=True).then_inc(a_job.sem, 1)
                for half in range(2):
                    e.matmul(job(26 + half), Wnat[:, 3 * P:4 * P], XTB[:, half * 512:(half + 1) * 512], start=True, stop=True).then_inc(a_job.sem, 1)
                a_pool.wait(e, i, 1)
                for u in range(LAST):
                    w = a_steps(u)
                    if w["score"] is not None:
                        c, s = u // 4, u % 4
                        if c == 0:
                            a_split.wait(e, i, 4 * s + 3)
                            a_qpad[s].wait(e, i, 0)
                        a_masked.wait(e, i, u - 2)
                        e.matmul(bank[2 + u % 2].rearrange("p (r n) -> p r n", r=R), KA[:, s, c * P:(c + 1) * P],
                                 Qpad[:, s, :, c * P:(c + 1) * P], start=True, stop=True).then_inc(a_score.sem, 1)
                    if w["pv"] is not None:
                        v = w["pv"]
                        c, s = v // 4, v % 4
                        a_masked.wait(e, i, v)
                        if s == 0:
                            a_ot.wait(e, i, c - 2)
                        for r in range(R):
                            last = e.matmul(bank[4 + c % 2][PART * r:PART * r + D, s * P:(s + 1) * P], V9[:, c, 4 * s + r, 0:D],
                                            PA[:, v % 2, r * P:(r + 1) * P], start=True, stop=True)
                        last.then_inc(a_pv.sem, 1)
                    if w["kv"] is not None:
                        c = w["kv"]
                        a_auxr.wait(e, i, aux_index("kv", c) - 1)
                        e.matmul(bank[7][:, 0:P].rearrange("p (h d) -> p h d", d=D), KN[:, c, :], V9[:, c, :, 0:D],
                                 start=True, stop=True).then_inc(a_aux.sem, 1)
                    if w["sel"] is not None:
                        c = w["sel"]
                        a_ot.wait(e, i, c)
                        if c % 4 == 0:
                            a_onorm.wait(e, i, c // 4 - 1)
                        to = bank[6][:, (c % 4) * P:(c % 4 + 1) * P]
                        for s in range(SLOTS):
                            last = e.matmul(to, OTS[:, c % 2, s * P:(s + 1) * P], sel[:, s, :], start=(s == 0), stop=(s == 3 and c == 0))
                        if c:
                            a_kv.wait(e, i, c - 1)
                            last = e.matmul(to, QL[:, c, :], KV[:, c % 2, :], start=False, stop=True)
                        last.then_inc(a_on.sem, 1)
                    if w["turn"] is not None:
                        g = w["turn"]
                        b = job(28 + g)
                        a_y.wait(e, i, g)
                        for j in range(4):
                            last = e.transpose(b[:, j * P:(j + 1) * P], ONS[:, j, :], ident[:, :])
                        last.then_inc(a_job.sem, 1)
                    if w["y"] is not None:
                        g = w["y"]
                        a_evac.wait(e, i, 28 + g)
                        a_auxr.wait(e, i, aux_index("y", g) - 1)
                        for j in range(4):
                            last = e.matmul(bank[7][:, j * P:(j + 1) * P], TR[:, (4 * g + j) * P:(4 * g + j + 1) * P], Woa[:, :], start=True, stop=True)
                        last.then_inc(a_aux.sem, 1)

        BJ = 28
        DJ = 2 * SLOTS
        GROUPS = SLOTS * TPB
        UNITS = GROUPS * R
        b_norm = Norm("b")
        b_job = Signal(sem("b_job_done"), BJ)
        b_evac = Signal(sem("b_job_evacuated"), BJ)
        b_ojob = Signal(sem("b_o_natural"), DJ)
        b_onorm = Signal(sem("b_o_normalised"), DJ)
        b_split = Signal(sem("b_split_done"), 16)
        b_qpad = [Signal(sem(f"b_q_padded{s}"), 1, 16 * R) for s in range(SLOTS)]
        b_kpad = [Signal(sem(f"b_k_copied{s}"), 1, 16 * R) for s in range(SLOTS)]
        b_mscore = Signal(sem("b_max_scores_done"), GROUPS * R)
        b_mred = Signal(sem("b_max_reduced"), GROUPS * R)
        b_shift = [Signal(sem(f"b_shift_stored{s}"), 1, 16 * R) for s in range(SLOTS)]
        b_score = Signal(sem("b_scores_done"), UNITS)
        b_diag = Signal(sem("b_diagonal_done"), UNITS)
        b_exp = Signal(sem("b_exponentials_done"), UNITS)
        b_pv = Signal(sem("b_pv_done"), GROUPS)
        b_ot = Signal(sem("b_ot_copied"), SLOTS)
        b_vb = Signal(sem("b_v_bias_added"), 1)
        b_xb = Signal(sem("b_out_bias_added"), 1)
        b_yx = Signal(sem("b_y_added"), 2)
        b_y = Signal(sem("b_y_done"), 2)
        b_tables = sem("b_tables_loaded")
        b_rows = sem("b_rows_loaded")
        b_cleared = sem("b_cleared")
        b_begin = sem("b_may_begin")
        b_ones = sem("b_ones_set")

        QSTB = EX[:, 0:2, :]
        pairs = [pairA, pairB]

        def attn_b_sync(e):
            for s in b_qpad + b_kpad + b_shift:
                s.prime(e)
            e.wait_ge(b_begin, 1)
            for a, b in ((over, "over"), (overT, "overT")):
                e.dma_start(a[:, :], I[b]).then_inc(b_tables, 16)
            e.wait_ge(b_rows, 16 * 12)
            with e.Fori(0, BATCH) as i:
                for s in range(SLOTS):
                    b_split.wait(e, i, 4 * s + 1)
                    pass_wait(e)
                    b_score.wait(e, i, -1)
                    for r in range(R):
                        e.dma_start(Qpad[PART * r:PART * r + ROWS, s, r, :].bitcast(F32),
                                    QSTB[PART * r:PART * r + ROWS, s % 2, :]).then_inc(b_qpad[s].sem, 16)
                    b_split.wait(e, i, 4 * s + 3)
                    for r in range(R):
                        for m in (KA, KB):
                            e.dma_start(m[PART * r:PART * r + ROWS, s, :].bitcast(F32),
                                        KST[PART * r:PART * r + ROWS, s % 2, :]).then_inc(b_kpad[s].sem, 16)
                for s in range(SLOTS):
                    b_evac.wait(e, i, SJ[s])
                    for r in range(R):
                        e.dma_start(Qpad[PART * r + SHIFT:PART * r + SHIFT + 1, s, r, :].bitcast(F32).rearrange("a (t n) -> a t n", n=P),
                                    MXT[TPB * r:TPB * (r + 1), :].bitcast(F32)).then_inc(b_shift[s].sem, 16)

        KST = EX[:, 2:4, :]
        VJ = 18
        SJ = [26 + s for s in range(SLOTS)]
        OJ = 30
        BJ = 32
        for g in (b_job, b_evac):
            g.per = BJ
        for g in b_kpad:
            g.unit = 16 * 2 * R

        def job_order():
            order = [("a", n) for n in range(VJ + TPB)]
            for s in range(SLOTS):
                order.append(("a", SJ[s]))
                if s:
                    order += [("o", 2 * (s - 1)), ("o", 2 * (s - 1) + 1)]
            order += [("o", 6), ("o", 7), ("a", OJ), ("a", OJ + 1)]
            order += [("y", 0), ("y", 1)]
            assert len(order) % 2 == 0
            return order

        ORDER = job_order()
        READ_BY = {"a": b_evac, "o": b_onorm, "y": b_yx}

        def job_bank(kind, n):
            return bank[ORDER.index((kind, n)) % 2]

        def job_free(e, i, kind, n):
            at = ORDER.index((kind, n))
            k, m = ORDER[at - 2]
            g = READ_BY[k]
            g.wait(e, i, m if at >= 2 else m - g.per)
            return bank[at % 2]

        def attn_b_gpsimd(e):
            b_norm.prime_gpsimd(e)
            b_vb.prime(e)
            b_xb.prime(e)
            e.wait_ge(b_begin, 1)
            e.memset(Qpad[:, :, :, :].bitcast(F32), 0.0).then_inc(b_cleared, 1)
            e.memset(KA[:, :, :].bitcast(F32), 0.0).then_inc(b_cleared, 1)
            e.memset(KB[:, :, :].bitcast(F32), 0.0).then_inc(b_cleared, 1)
            e.memset(V9[:, :, :, :], 1.0).then_inc(b_ones, 1)
            e.wait_ge(b_cleared, 3)
            for r in range(R):
                at = PART * r + ROWS
                e.dma_start(Qpad[at:at + AUG, :, r, :], I["augq"][r]).then_inc(b_rows, 16)
                e.dma_start(KA[at:at + AUG + 1, :, :], I["auga"][r]).then_inc(b_rows, 16)
                e.dma_start(KB[at:at + AUG + 1, :, :], I["augb"][r]).then_inc(b_rows, 16)
            with e.Fori(0, BATCH) as i:
                g_steps.loop(i, 1)
                b_norm.gpsimd(e, i)
                xs = X[:, bass.ds(i * TPB, TPB), :]
                b_norm.xn_ready.wait(e, i, 1)
                e.tensor_tensor(xs, xs, obias[:, None, :].to_broadcast([P, TPB, P]), ALU.add).then_inc(b_xb.sem, 1)
                b_onorm.wait(e, i, DJ - 1)
                e.tensor_tensor(ATT[:, :, :], ATT[:, :, :], vbias[:, None, :].to_broadcast([P, TPB, P]), ALU.add).then_inc(b_vb.sem, 1)
            g_steps.end(BATCH)

        def attn_b_scalar(e):
            b_evac.prime(e)
            b_exp.prime(e)
            e.wait_ge(b_ones, 1)
            e.wait_ge(qb_ready, 1)
            with e.Fori(0, BATCH) as i:
                def job(n):
                    b_job.wait(e, i, n)
                    return job_bank("a", n)
                for half in range(2):
                    e.activation(XTB[:, half * 512:(half + 1) * 512], job(half), ACT.Copy).then_inc(b_evac.sem, 1)
                for m in range(16):
                    s, side = m // 4, (m // 2) % 2
                    b_split.wait(e, i, m - 2)
                    e.activation(T[:, m % 2, :], job(2 + m), ACT.Identity, bias=(qbs if side == 0 else kbias)[:, s:s + 1],
                                 scale=(QSCALE if side == 0 else 1.0)).then_inc(b_evac.sem, 1)
                for c in range(TPB):
                    e.activation(V9[:, c, :, 0:D], job(VJ + c)[:, 0:P].rearrange("p (h d) -> p h d", d=D), ACT.Copy).then_inc(b_evac.sem, 1)
                for g in b_qpad + b_kpad:
                    g.wait(e, i, 0)
                for s in range(SLOTS):
                    b = job(SJ[s])
                    b_shift[s - 1].wait(e, i, 0 if s else -1)
                    e.activation(MXT[:, :], b[0:PART, 0:P], ACT.Copy, scale=-1.0).then_inc(b_evac.sem, 1)
                    for n in range(s * TPB * R, (s + 1) * TPB * R):
                        b_diag.wait(e, i, n)
                        if n % R == 0:
                            b_pv.wait(e, i, n // R - 2)
                        e.activation(EX[:, n % 8, :], pairs[n % 2][:, :], ACT.Exp).then_inc(b_exp.sem, 1)
                for half in range(2):
                    e.activation(TR[:, half * 512:(half + 1) * 512], job(OJ + half), ACT.Copy).then_inc(b_evac.sem, 1)

        qb_ready = sem("q_bias_scaled")

        def attn_b_vector(e):
            b_norm.prime_vector(e)
            for g in (b_split, b_mred, b_diag, b_ot, b_onorm, b_yx):
                g.prime(e)
            e.wait_ge(b_begin, 1)
            e.tensor_scalar(qbs[:, :], qbias[:, :], QSCALE, None, ALU.mult).then_inc(qb_ready, 1)
            for b in (6, 7):
                v_steps.add(e.memset(bank[b], 0.0))
            v_steps.settle(e)
            v_cleared_ins = e.memset(MX[:, :], 0.0)
            v_cleared_ins.then_inc(b_otzero, 1)
            e.wait_ge(b_tables, 32)
            with e.Fori(0, BATCH) as i:
                v_steps.loop(i, B_V)
                b_norm.vector(e, i)
                for m in range(16):
                    s, side, half = m // 4, (m // 2) % 2, m % 2
                    b_evac.wait(e, i, 2 + m)
                    if side == 0 and half == 0:
                        if s < 2:
                            b_pv.wait(e, i, -1)
                        else:
                            b_qpad[s - 2].wait(e, i, 0)
                    if side == 1 and half == 0 and s >= 2:
                        b_kpad[s - 2].wait(e, i, 0)
                    v_steps.chain(e, e.tensor_copy(TH[:, m % 2, :], T[:, m % 2, :]))
                    to = (QSTB if side == 0 else KST)[:, s % 2, half * 512:(half + 1) * 512].bitcast(F32R)
                    e.scalar_tensor_tensor(out=to, in0=TH[:, m % 2, :].bitcast(F32), scalar=(negq if side == 0 else negk)[:, 0:1],
                                           in1=T[:, m % 2, :], op0=ALU.mult, op1=ALU.add).then_inc(b_split.sem, 1)

                def normalise(s):
                    for half in range(2):
                        b_ojob.wait(e, i, 2 * s + half)
                        b = job_bank("o", 2 * s + half).rearrange("p (t c n) -> p t c n", t=GROUP, c=R)
                        v_steps.chain(e, e.reciprocal(DEN[:, :, :], b[:, :, :, D]))
                        if s == 0 and half == 0:
                            b_job.wait(e, i, 1)
                        e.tensor_tensor(ATT[:, GROUP * half:GROUP * half + GROUP, R * D * s:R * D * (s + 1)].rearrange("p t (c d) -> p t c d", d=D),
                                        b[:, :, :, 0:D], DEN[:, :, :].unsqueeze(3).to_broadcast([P, GROUP, R, D]), ALU.mult).then_inc(b_onorm.sem, 1)
                        b_onorm.wait(e, i, 2 * s + half)

                def copy_ot(s):
                    b_pv.wait(e, i, TPB * (s + 1) - 1)
                    if s:
                        b_ojob.wait(e, i, 2 * s - 1)
                    e.tensor_copy(OTB, pairC[:, :]).then_inc(b_ot.sem, 1)

                for s in range(SLOTS):
                    for m in range(TPB * R):
                        q, r = m // R, m % R
                        n = s * TPB * R + m
                        b_mscore.wait(e, i, n)
                        b = pairs[m % 2]
                        v_steps.chain(e, e.scalar_tensor_tensor(out=b[:, q * P:(q + 1) * P], in0=overT[:, :], scalar=-2.0 * SL[R * s + r],
                                                                in1=b[:, q * P:(q + 1) * P], op0=ALU.mult, op1=ALU.add))
                        if m == 0:
                            b_job.wait(e, i, SJ[s - 1] if s else -1 - (BJ - 1 - SJ[3]))
                        e.tensor_reduce(MX[:, TPB * r + q:TPB * r + q + 1], b[:, :], AX.X, ALU.max).then_inc(b_mred.sem, 1)
                    for g in range(TPB):
                        if g == 1 and s:
                            normalise(s - 1)
                        for r in range(R):
                            n = (s * TPB + g) * R + r
                            b_score.wait(e, i, n)
                            b = pairs[n % 2]
                            e.scalar_tensor_tensor(out=b[:, g * P:(g + 1) * P], in0=over[:, :], scalar=-2.0 * SL[R * s + r],
                                                   in1=b[:, g * P:(g + 1) * P], op0=ALU.mult, op1=ALU.add).then_inc(b_diag.sem, 1)
                    copy_ot(s)
                normalise(SLOTS - 1)
                for g in range(2):
                    b_y.wait(e, i, g)
                    b_xb.wait(e, i, 0)
                    xs = X[:, bass.ds(i * TPB + 4 * g, 4), :]
                    e.tensor_tensor(xs, job_bank("y", g).rearrange("p (t n) -> p t n", n=P), xs, ALU.add).then_inc(b_yx.sem, 1)
                    b_yx.wait(e, i, g)
            v_steps.end(BATCH)

        B_V = 8 + 7 + 6 + 16 + 8 + GROUPS * R
        b_otzero = sem("b_ot_zeroed")

        def attn_b_tensor(e):
            for g in (b_job, b_ojob, b_mscore, b_score, b_pv, b_y):
                g.prime(e)
            e.wait_ge(b_otzero, 1)
            with e.Fori(0, BATCH) as i:
                for half in range(2):
                    b = job_free(e, i, "a", half)
                    b_norm.transposes(e, i, half, b).then_inc(b_job.sem, 1)
                b_evac.wait(e, i, 1)
                for m in range(16):
                    s, side, half = m // 4, (m // 2) % 2, m % 2
                    e.matmul(job_free(e, i, "a", 2 + m), (Wqb if side == 0 else Wkb)[:, s, :], XTB[:, half * 512:(half + 1) * 512],
                             start=True, stop=True).then_inc(b_job.sem, 1)
                for c in range(TPB):
                    e.matmul(job_free(e, i, "a", VJ + c)[:, 0:P], XTB[:, c * P:(c + 1) * P], Wvb[:, :], start=True, stop=True).then_inc(b_job.sem, 1)
                b_evac.wait(e, i, VJ + TPB - 1)

                def exp_scores(s, g, r):
                    n = (s * TPB + g) * R + r
                    b_exp.wait(e, i, n - 2)
                    b = pairs[n % 2]
                    for half in range(2):
                        lo, hi = 512 * half, 512 * (half + 1)
                        cut = min(max(g * P, lo), hi)
                        for m, a, z in ((KB, lo, cut), (KA, cut, hi)):
                            if a < z:
                                last = e.matmul(b[:, a:z], m[:, s, g * P:(g + 1) * P], Qpad[:, s, r, a:z], start=True, stop=True)
                    last.then_inc(b_score.sem, 1)

                def max_scores(s, q, r):
                    m = q * R + r
                    if m < 2:
                        b_exp.wait(e, i, s * TPB * R - 2 + m)
                    else:
                        b_mred.wait(e, i, s * TPB * R + m - 2)
                    b = pairs[m % 2]
                    for half in range(2):
                        lo, hi = 512 * half, 512 * (half + 1)
                        cut = min(max((q + 1) * P, lo), hi)
                        for k, a, z in ((KA, lo, cut), (KB, cut, hi)):
                            if a < z:
                                last = e.matmul(b[:, a:z], Qpad[:, s, r, q * P:(q + 1) * P], k[:, s, a:z], start=True, stop=True)
                    last.then_inc(b_mscore.sem, 1)

                def pv(s, g, half):
                    n = s * TPB + g
                    if half == 0:
                        b_exp.wait(e, i, R * n + R - 1)
                        if g == 0:
                            b_ot.wait(e, i, s - 1)
                    for r in range(R):
                        last = e.matmul(pairC[PART * r:PART * r + D + 1, 512 * half:512 * (half + 1)], V9[:, g, R * s + r, :],
                                        EX[:, (R * n + r) % 8, 512 * half:512 * (half + 1)], start=(g == 0), stop=(g == TPB - 1))
                    if half == 1:
                        last.then_inc(b_pv.sem, 1)

                def naturals(s):
                    b_ot.wait(e, i, s)
                    for half in range(2):
                        b = job_free(e, i, "o", 2 * s + half)
                        for j in range(GROUP):
                            last = e.transpose(b[:, j * P:(j + 1) * P], OTB[:, (GROUP * half + j) * P:(GROUP * half + j + 1) * P], ident[:, :])
                        last.then_inc(b_ojob.sem, 1)

                for s in range(SLOTS):
                    b_qpad[s].wait(e, i, 0)
                    b_kpad[s].wait(e, i, 0)
                    for q in range(TPB):
                        for r in range(R):
                            max_scores(s, q, r)
                    b_mred.wait(e, i, (s + 1) * TPB * R - 1)
                    e.transpose(job_free(e, i, "a", SJ[s])[0:PART, 0:P], MX[:, :], ident[:, :]).then_inc(b_job.sem, 1)
                    b_shift[s].wait(e, i, 0)
                    for g in range(TPB):
                        exp_scores(s, g, 0)
                        exp_scores(s, g, 1)
                        if g:
                            pv(s, g - 1, 0)
                        if g == 1 and s:
                            naturals(s - 1)
                        exp_scores(s, g, 2)
                        exp_scores(s, g, 3)
                        if g:
                            pv(s, g - 1, 1)
                    pv(s, TPB - 1, 0)
                    pv(s, TPB - 1, 1)
                naturals(SLOTS - 1)
                b_vb.wait(e, i, 0)
                for half in range(2):
                    b = job_free(e, i, "a", OJ + half)
                    for j in range(GROUP):
                        last = e.transpose(b[:, j * P:(j + 1) * P], ATT[:, GROUP * half + j, :], ident[:, :])
                    last.then_inc(b_job.sem, 1)
                for g in range(2):
                    b_evac.wait(e, i, OJ + g)
                    b = job_free(e, i, "y", g)
                    for j in range(GROUP):
                        last = e.matmul(b[:, j * P:(j + 1) * P], TR[:, (GROUP * g + j) * P:(GROUP * g + j + 1) * P], Wob[:, :], start=True, stop=True)
                    last.then_inc(b_y.sem, 1)

        ff = ExitStack()
        XT = sb("XT", [P, NT * P], scope=ff)
        S = sb("S", [P, NT, P], scope=ff)
        AB = sb("AB", [P, NT, P], scope=ff)
        ACC = sb("ACC", [P, NT, P], scope=ff)
        W1 = sb("W1", [P, EXPERTS, DF], scope=ff)
        HT = sb("HT", [P, 2, FC, 512], scope=ff)
        LG = sb("LG", [P, NT, EXPERTS], scope=ff)
        WD = sb("WD", [P, NT, EXPERTS], scope=ff)
        R1 = sb("R1", [P, NT, EXPERTS], scope=ff)
        R2 = sb("R2", [P, NT, EXPERTS], scope=ff)
        C1 = sb("C1", [P, NT], scope=ff)
        C2 = sb("C2", [P, NT], scope=ff)
        C3 = sb("C3", [P, NT], scope=ff)
        C4 = sb("C4", [P, NT], scope=ff)
        ZA = sb("ZA", [P, NT], scope=ff)
        ZN = sb("ZN", [P, NT], scope=ff)
        WT = sb("WT", [EXPERTS, NT * P], scope=ff)
        ff.close()

        class Ffn:
            def __init__(self, k, begin):
                q = f"f{k}_"
                self.begin = begin
                self.norm = Norm(q, twice=True)
                self.tjob, self.tevac = Signal(sem(q + "transposed"), 2), Signal(sem(q + "xt_ready"), 2)
                self.ajob, self.aread = Signal(sem(q + "abel_done"), 4), Signal(sem(q + "abel_read"), 4)
                self.copied = Signal(sem(q + "xt_copied"), 1, 16)
                self.gelu = Signal(sem(q + "abel_ready"), 1)
                self.mixed = Signal(sem(q + "abel_mixed"), 1)
                self.zred = Signal(sem(q + "abel_reduced"), 1)
                self.w1 = sem(q + "w1_loaded")
                self.gap, self.ex = sem(q + "gap_ready"), sem(q + "gap_exp")
                self.wd = sem(q + "weights_ready")
                self.wt, self.wtc = sem(q + "weights_turned"), sem(q + "weights_copied")
                self.bb, self.bbc = sem(q + "b2_done"), sem(q + "b2_copied")
                self.hjob, self.hevac = Signal(sem(q + "hidden_done"), EXPERTS * FC), Signal(sem(q + "hidden_ready"), EXPERTS * FC)
                self.yjob, self.yread = Signal(sem(q + "expert_done"), EXPERTS), Signal(sem(q + "expert_added"), EXPERTS)
                self.z, self.gate = sem(q + "z_ready"), sem(q + "gate_ready")
                self.srest = Signal(sem(q + "s_ready"), 1)

            def sync(self, e):
                self.copied.prime(e)
                e.wait_ge(self.begin, 1)
                for x in range(EXPERTS):
                    e.dma_start(W1[:, x, :], I["w1"][:, x, :]).then_inc(self.w1, 16)
                with e.Fori(0, BATCH) as i:
                    self.tevac.wait(e, i, 1)
                    e.dma_start(XT[:, bass.ds(i * SEQ, SEQ)], XTB[:, :]).then_inc(self.copied.sem, 16)

            def gpsimd(self, e):
                self.norm.prime_gpsimd(e)
                self.mixed.prime(e)
                self.srest.prime(e)
                e.wait_ge(self.begin, 1)
                with e.Fori(0, BATCH) as i:
                    g_steps.loop(i, 4 + 2 + 1)
                    self.norm.gpsimd(e, i)
                    ts = bass.ds(i * TPB, TPB)
                    self.gelu.wait(e, i, 0)
                    g_steps.chain(e, e.tensor_tensor(S[:, ts, :], S[:, ts, :], X[:, ts, :], ALU.add))
                    e.tensor_tensor(XN[:, :, :], AB[:, ts, :], mixa[:, None, :].to_broadcast([P, TPB, P]), ALU.mult).then_inc(self.mixed.sem, 1)
                    e.tensor_tensor(S[:, ts, :], S[:, ts, :], AB[:, ts, :], ALU.add).then_inc(self.srest.sem, 1)
                g_steps.end(BATCH)

            def scalar(self, e):
                self.tevac.prime(e)
                self.gelu.prime(e)
                self.hevac.prime(e)
                e.wait_ge(self.begin, 1)
                with e.Fori(0, BATCH) as i:
                    for half in range(2):
                        self.tjob.wait(e, i, half)
                        self.copied.wait(e, i, -1)
                        self.ajob.wait(e, i, -1)
                        e.activation(XTB[:, half * 512:(half + 1) * 512], bank[half], ACT.Identity,
                                     bias=lnbT[:, 0:1], scale=lngT[:, 0:1]).then_inc(self.tevac.sem, 1)
                    self.aread.wait(e, i, 3)
                    ab = AB[:, bass.ds(i * TPB, TPB), :]
                    e.activation(ab, ab, ACT.Gelu).then_inc(self.gelu.sem, 1)
                e.wait_ge(self.gap, 1)
                e.activation(C3[:, :], C3[:, :], ACT.Exp).then_inc(self.ex, 1)
                for g in range(NG):
                    e.wait_ge(self.wt, g + 1)
                    e.activation(WT[:, g * 512:(g + 1) * 512], bank[g % 2][0:EXPERTS, :], ACT.Copy).then_inc(self.wtc, 1)
                for g in range(NG):
                    e.wait_ge(self.bb, g + 1)
                    e.activation(ACC[:, GROUP * g:GROUP * (g + 1), :].rearrange("p t n -> p (t n)"), bank[2 + g % 2], ACT.Copy).then_inc(self.bbc, 1)
                with e.Fori(0, NG) as i:
                    for x in range(EXPERTS):
                        for c in range(FC):
                            n = x * FC + c
                            self.hjob.wait(e, i, n)
                            if c == 0:
                                self.yjob.wait(e, i, x - 2)
                            e.activation(HT[:, x % 2, c, :], bank[n % 4], ACT.Gelu, bias=b1T[:, n:n + 1]).then_inc(self.hevac.sem, 1)
                e.wait_ge(self.z, 1)
                e.activation(C1[:, :], C1[:, :], ACT.Sigmoid, bias=mixb[:, 0:1]).then_inc(self.gate, 1)

            def vector(self, e):
                self.norm.prime_vector(e)
                for g in (self.aread, self.zred, self.yread):
                    g.prime(e)
                with e.Fori(0, BATCH) as i:
                    v_steps.loop(i, 8 + 7 + 6 + 8 + 4)
                    self.norm.vector(e, i, keep=S)
                    ts = bass.ds(i * TPB, TPB)
                    for j in range(4):
                        self.ajob.wait(e, i, j)
                        b = bank[2 + j % 2][:, 0:2 * (P + EXPERTS)].rearrange("p (t n) -> p t n", t=2)
                        tt = bass.ds(i * TPB + 2 * j, 2)
                        v_steps.add(e.tensor_tensor(LG[:, tt, :], b[:, :, P:P + EXPERTS], abias[:, None, P:P + EXPERTS].to_broadcast([P, 2, EXPERTS]), ALU.add))
                        e.tensor_tensor(AB[:, tt, :], b[:, :, 0:P], abias[:, None, 0:P].to_broadcast([P, 2, P]), ALU.add).then_inc(self.aread.sem, 1)
                    self.mixed.wait(e, i, 0)
                    e.tensor_reduce(ZA[:, ts], XN[:, :, :], AX.X, ALU.add).then_inc(self.zred.sem, 1)
                    self.zred.wait(e, i, 0)
                    self.srest.wait(e, i, 0)
                v_steps.end(BATCH)
                v_steps.settle(e)

                def every(c):
                    return c[:, :].unsqueeze(2).to_broadcast([P, NT, EXPERTS])

                def one_hot(of, top, hot, rank):
                    v_steps.chain(e, e.tensor_reduce(top[:, :], of[:, :, :], AX.X, ALU.max))
                    v_steps.chain(e, e.tensor_tensor(hot[:, :, :], of[:, :, :], every(top), ALU.is_equal))
                    v_steps.chain(e, e.tensor_tensor(hot[:, :, :], hot[:, :, :], rank8[:, None, :].to_broadcast([P, NT, EXPERTS]), ALU.mult))
                    v_steps.chain(e, e.tensor_reduce(rank[:, :], hot[:, :, :], AX.X, ALU.max))
                    v_steps.chain(e, e.tensor_tensor(hot[:, :, :], hot[:, :, :], every(rank), ALU.is_equal))

                one_hot(LG, C1, R1, C4)
                v_steps.chain(e, e.scalar_tensor_tensor(out=LG[:, :, :], in0=R1[:, :, :], scalar=-3.0e38, in1=LG[:, :, :], op0=ALU.mult, op1=ALU.add))
                one_hot(LG, C2, R2, C4)
                e.tensor_tensor(C3[:, :], C2[:, :], C1[:, :], ALU.subtract).then_inc(self.gap, 1)
                e.wait_ge(self.ex, 1)
                v_steps.chain(e, e.tensor_scalar(C1[:, :], C3[:, :], 1.0, None, ALU.add))
                v_steps.chain(e, e.reciprocal(C1[:, :], C1[:, :]))
                v_steps.chain(e, e.tensor_tensor(C2[:, :], C3[:, :], C1[:, :], ALU.mult))
                v_steps.chain(e, e.tensor_tensor(R1[:, :, :], R1[:, :, :], every(C1), ALU.mult))
                v_steps.chain(e, e.tensor_tensor(R2[:, :, :], R2[:, :, :], every(C2), ALU.mult))
                e.tensor_tensor(WD[:, :, :], R1[:, :, :], R2[:, :, :], ALU.add).then_inc(self.wd, 1)
                e.wait_ge(self.wd, 1)

                e.wait_ge(self.bbc, NG)
                with e.Fori(0, NG) as i:
                    v_steps.loop(i, EXPERTS * 3 + 2)
                    for x in range(EXPERTS):
                        self.yjob.wait(e, i, x)
                        for j in range(GROUP):
                            acc = ACC[:, bass.ds(i * GROUP + j, 1), :].rearrange("p a n -> p (a n)")
                            if j == 0:
                                self.yread.wait(e, i, x - 1)
                            ins = e.scalar_tensor_tensor(out=acc, in0=bank[4 + x % 2][:, j * P:(j + 1) * P],
                                                         scalar=WD[:, bass.ds(i * GROUP + j, 1), x:x + 1].rearrange("p a n -> p (a n)"), in1=acc,
                                                         op0=ALU.mult, op1=ALU.add)
                            ins.then_inc(self.yread.sem, 1) if j == GROUP - 1 else v_steps.add(ins)
                    self.yread.wait(e, i, EXPERTS - 1)
                    v_steps.settle(e)
                    gs = bass.ds(i * GROUP, GROUP)
                    v_steps.chain(e, e.tensor_tensor(XN[:, 0:GROUP, :], ACC[:, gs, :], mixn[:, None, :].to_broadcast([P, GROUP, P]), ALU.mult))
                    v_steps.add(e.tensor_reduce(ZN[:, gs], XN[:, 0:GROUP, :], AX.X, ALU.add))
                    v_steps.settle(e)
                v_steps.end(NG)
                v_steps.settle(e)
                v_steps.chain(e, e.tensor_tensor(ACC[:, :, :], ACC[:, :, :], AB[:, :, :], ALU.subtract))
                e.tensor_tensor(C1[:, :], ZA[:, :], ZN[:, :], ALU.add).then_inc(self.z, 1)
                e.wait_ge(self.gate, 1)
                for t in range(NT):
                    v_steps.add(e.scalar_tensor_tensor(out=X[:, t, :], in0=ACC[:, t, :], scalar=C1[:, t:t + 1], in1=S[:, t, :],
                                                       op0=ALU.mult, op1=ALU.add))
                v_steps.settle(e)

            def tensor(self, e):
                for g in (self.tjob, self.ajob, self.hjob, self.yjob):
                    g.prime(e)
                e.wait_ge(self.begin, 1)
                with e.Fori(0, BATCH) as i:
                    for half in range(2):
                        self.tevac.wait(e, i, half - 2)
                        self.norm.transposes(e, i, half, bank[half]).then_inc(self.tjob.sem, 1)
                    for j in range(4):
                        self.tevac.wait(e, i, j // 2)
                        self.aread.wait(e, i, j - 2)
                        for t in (2 * j, 2 * j + 1):
                            last = e.matmul(bank[2 + j % 2][:, (t % 2) * (P + EXPERTS):(t % 2 + 1) * (P + EXPERTS)], XTB[:, t * P:(t + 1) * P],
                                            Wab[:, :], start=True, stop=True)
                        last.then_inc(self.ajob.sem, 1)
                e.wait_ge(self.wd, 1)
                self.tevac.wait(e, BATCH - 1, 1)
                for g in range(NG):
                    if g >= 2:
                        e.wait_ge(self.wtc, g - 1)
                    for j in range(GROUP):
                        last = e.transpose(bank[g % 2][0:EXPERTS, j * P:(j + 1) * P], WD[:, GROUP * g + j, :], ident[:, :])
                    last.then_inc(self.wt, 1)
                for g in range(NG):
                    e.wait_ge(self.wtc, g + 1)
                    if g >= 2:
                        e.wait_ge(self.bbc, g - 1)
                    for j in range(GROUP):
                        t = GROUP * g + j
                        last = e.matmul(bank[2 + g % 2][:, j * P:(j + 1) * P], WT[:, t * P:(t + 1) * P], b2r[:, :], start=True, stop=True)
                    last.then_inc(self.bb, 1)
                e.wait_ge(self.bbc, NG)
                e.wait_ge(self.w1, 16 * EXPERTS)
                self.copied.wait(e, BATCH - 1, 0)
                with e.Fori(0, NG) as i:
                    def hidden(x):
                        for c in range(FC):
                            n = x * FC + c
                            self.hevac.wait(e, i, n - 4)
                            e.matmul(bank[n % 4], W1[:, x, c * P:(c + 1) * P], XT[:, bass.ds(i * 512, 512)], start=True, stop=True).then_inc(self.hjob.sem, 1)

                    hidden(0)
                    for x in range(EXPERTS):
                        if x + 1 < EXPERTS:
                            hidden(x + 1)
                        self.hevac.wait(e, i, x * FC + FC - 1)
                        self.yread.wait(e, i, x - 2)
                        for j in range(GROUP):
                            for c in range(FC):
                                last = e.matmul(bank[4 + x % 2][:, j * P:(j + 1) * P], HT[:, x % 2, c, j * P:(j + 1) * P], w2r[:, x * FC + c, :],
                                                start=(c == 0), stop=(c == FC - 1))
                        last.then_inc(self.yjob.sem, 1)

        def rowb(ap):
            return ap.partition_broadcast(P)

        wloads = [
            (Wqa[:, :, :], I["Wqa"]), (Wka[:, :, :], I["Wka"]), (Wnat[:, 0:2 * P], I["Wkv"]), (Wnat[:, 3 * P:4 * P], I["Wqn"]),
            (Wg1T[:, :], I["Wg1T"]), (Wg2[:, :], I["Wg2"]), (Woa[:, :], I["Woa"]), (gam[:, :], rowb(I["gam"])), (bet[:, :], rowb(I["bet"])),
            (negq[:, :], I["negq"]), (negk[:, :], I["negk"]),
            (Wqb[:, :, :], I["Wqb"]), (Wkb[:, :, :], I["Wkb"]), (Wvb[:, :], I["Wvb"]), (Wob[:, :], I["Wob"]),
            (qbias[:, :], I["qbias"]), (kbias[:, :], I["kbias"]), (vbias[:, :], rowb(I["vbias"])), (obias[:, :], rowb(I["obias"])),
            (lngT[:, :], I["lngT"]), (lnbT[:, :], I["lnbT"]), (Wab[:, 0:P], I["abel_w"]), (Wab[:, P:P + EXPERTS], I["gate_w"]),
            (abias[:, 0:P], rowb(I["abel_b"])), (abias[:, P:P + EXPERTS], rowb(I["gate_b"])), (b1T[:, :], I["b1T"]),
            (mixa[:, :], rowb(I["mixa"])), (mixn[:, :], rowb(I["mixn"])), (mixb[:, :], rowb(I["mixb"])), (rank8[:, :], rowb(I["rank8"])),
        ]
        N_WLOADS = len(wloads)

        def loads_sync(e):
            for a, b in ((ident[:, :], I["ident"]), (A[:, :, :], I["gens"]), (AT[:, :, :], I["gensT"]), (inv[:, :], rowb(I["inv"])),
                         (thr[:, :, :].rearrange("p a b -> p (a b)"), rowb(I["thr"]))):
                e.dma_start(a, b).then_inc(gens_loaded, 16)
            for b in range(BATCH):
                e.dma_start(X[:, b * TPB:(b + 1) * TPB, :], I["x"][b].rearrange("(t p) d -> p t d", p=P)).then_inc(x_loaded, 16)
            e.dma_start(w2T[:, :, :], I["w2T"]).then_inc(w2_loaded, 16)
            e.dma_start(b2T[:, :], I["b2T"]).then_inc(w2_loaded, 16)

        def loads_scalar(e):
            for a, b in wloads:
                e.dma_start(a, b).then_inc(w_loaded, 16)

        def tables_sync(e):
            e.wait_ge(fold_copied, EXPERTS + 1)
            for a, b in ((maskT, "maskT"), (sel, "sel"), (lamq, "lamq"), (lamk, "lamk"), (lamc, "lamc"), (blk, "blk")):
                e.dma_start(a[tuple(slice(None) for _ in a.shape)], I[b]).then_inc(a_tables, 16)

        begins = [sem(f"phase{n}_may_begin") for n in range(2)]
        ffns = [Ffn(n, begins[n]) for n in range(2)]
        x_done = sem("x_done")
        block = ctx.enter_context(nc.Block())

        @block.sync
        def _(e):
            loads_sync(e)
            tables_sync(e)
            if 1 in upto:
                attn_a_sync(e)
            if 2 in upto:
                ffns[0].sync(e)
            if 3 in upto:
                attn_b_sync(e)
            if 4 in upto:
                ffns[1].sync(e)
            e.wait_ge(x_done, 1)
            for b in range(BATCH):
                e.dma_start(out[b].rearrange("(t p) d -> p t d", p=P), X[:, b * TPB:(b + 1) * TPB, :]).then_inc(out_stored, 16)
            e.wait_ge(out_stored, 16 * BATCH)

        @block.scalar
        def _(e):
            loads_scalar(e)
            if 1 in upto:
                attn_a_scalar(e)
            if 2 in upto:
                ffns[0].scalar(e)
            if 3 in upto:
                attn_b_scalar(e)
            if 4 in upto:
                ffns[1].scalar(e)

        @block.gpsimd
        def _(e):
            expm_gpsimd(e)
            e.wait_ge(fold_copied, EXPERTS + 1)
            e.memset(Qpad[:, :, :, :].bitcast(F32), 0.0).then_inc(zeroed, 1)
            if 1 in upto:
                attn_a_gpsimd(e)
            if 2 in upto:
                ffns[0].gpsimd(e)
            if 3 in upto:
                attn_b_gpsimd(e)
            if 4 in upto:
                ffns[1].gpsimd(e)

        @block.vector
        def _(e):
            attn_a_vector(e)
            expm_vector(e)
            e.wait_ge(x_loaded, 16 * BATCH)
            if 1 in upto:
                attn_a_vector_loop(e)
            e.wait_ge(zeroed, 1)
            e.wait_ge(a_tables, 96)
            if 2 in upto:
                e.memset(rstd2[:, :], 0.0).then_inc(begins[0], 1)
                e.wait_ge(begins[0], 1)
                ffns[0].vector(e)
            if 3 in upto:
                e.memset(rstd2[:, :], 0.0).then_inc(b_begin, 1)
                e.wait_ge(b_begin, 1)
                attn_b_vector(e)
            if 4 in upto:
                e.memset(rstd2[:, :], 0.0).then_inc(begins[1], 1)
                e.wait_ge(begins[1], 1)
                ffns[1].vector(e)
            e.memset(rstd2[:, :], 0.0).then_inc(x_done, 1)

        @block.tensor
        def _(e):
            expm_tensor(e)
            if 1 in upto:
                attn_a_tensor(e)
            if 2 in upto:
                ffns[0].tensor(e)
            if 3 in upto:
                attn_b_tensor(e)
            if 4 in upto:
                ffns[1].tensor(e)


def slot_columns(w):
    t = w.reshape(w.shape[0], SLOTS, R, 1, D)
    o = np.zeros((w.shape[0], SLOTS, R, PART), np.float32)
    o[..., :ROWS] = np.broadcast_to(t, (w.shape[0], SLOTS, R, 3, D)).reshape(w.shape[0], SLOTS, R, ROWS)
    return o.reshape(w.shape[0], SLOTS, P)


def constants():
    c = {}
    c["ident"] = np.eye(P, dtype=np.float32)
    start = 2.0 ** (-2.0 ** (-(np.log2(H) - 3)))
    s = np.array([start * start ** i for i in range(H)], dtype=np.float32)
    s = (s * (1.0 - 0 / 11 + 1e-05)).astype(np.float32)
    idx = np.arange(P, dtype=np.float32)
    diff = idx[None, :] - idx[:, None]
    m = np.where(diff >= 0, np.exp(-s[:, None, None] * np.maximum(diff, 0)), 0).astype(np.float32)
    c["maskT"] = np.ascontiguousarray(m.transpose(1, 0, 2))
    sh = np.repeat(s, D)
    c["lamq"] = np.exp(-sh[:, None] * (idx[None, :] + 1)).astype(np.float32)
    c["lamk"] = np.exp(-sh[None, :] * (P - 1.0 - idx[:, None])).astype(np.float32)
    c["lamc"] = np.exp(-sh * P).astype(np.float32)[:, None]
    h = np.arange(P) // D
    c["blk"] = (h[:, None] == h[None, :]).astype(np.float32)
    sel = np.zeros((P, SLOTS, P), np.float32)
    for q in range(SLOTS):
        for r in range(R):
            for d in range(D):
                sel[PART * r + d, q, (R * q + r) * D + d] = 1
    c["sel"] = sel
    row = np.arange(P) % PART
    c["negq"] = -((row >= 2 * D) & (row < 3 * D)).astype(np.float32)[:, None]
    c["negk"] = -((row >= D) & (row < 2 * D)).astype(np.float32)[:, None]
    c["inv"] = (1.0 / np.arange(TAYLOR, 0, -1)).astype(np.float32)
    c["thr"] = np.repeat(THETA * 2.0 ** np.arange(SQUARINGS), NROT).astype(np.float32)
    c["rank8"] = np.arange(EXPERTS, 0, -1).astype(np.float32)
    sl = alibi_slopes()
    hi = (sl.view(np.uint32) & np.uint32(0xFFFFF000)).view(np.float32)
    lo = (sl - hi).astype(np.float32)
    pos = np.arange(SEQ, dtype=np.float32)
    one = np.ones(SEQ, np.float32)
    aq = np.zeros((R, AUG, SLOTS, SEQ), np.float32)
    ak = np.zeros((R, AUG + 1, SLOTS, SEQ), np.float32)
    for q in range(SLOTS):
        for r in range(R):
            a, b = hi[R * q + r], lo[R * q + r]
            aq[r, :, q] = [-pos, a * one, -pos, b * one]
            ak[r, :AUG, q] = [a * one, pos, b * one, pos]
    c["augq"] = aq
    ak[:, AUG] = 1
    c["auga"] = ak
    akb = ak.copy()
    akb[:, :AUG] *= -1
    c["augb"] = akb
    k = np.arange(P)
    c["over"] = np.maximum(k[:, None] - k[None, :], 0).astype(np.float32)
    c["overT"] = np.ascontiguousarray(c["over"].T)
    return c


def layouts(a):
    g = lambda n: np.asarray(a[n])
    L = {"x": g("L0_attn_a_x")}
    L["Wqa"] = slot_columns(g("L0_attn_a_Wq"))
    L["Wka"] = slot_columns(g("L0_attn_a_Wk"))
    L["Wkv"] = np.concatenate([g("L0_attn_a_Wk"), g("L0_attn_a_Wv")], axis=1)
    L["Wqn"] = g("L0_attn_a_Wq")
    L["Wg1T"] = g("L0_attn_a_Wg1").T
    L["Wg2"] = g("L0_attn_a_Wg2")
    L["Woa"] = g("L0_attn_a_Wo")
    L["gam"], L["bet"] = g("L0_attn_a_gamma"), g("L0_attn_a_beta")
    W, B = g("L0_attn_b_W_qkv"), g("L0_attn_b_b_qkv")
    L["Wqb"], L["Wkb"] = slot_columns(W[:P].T), slot_columns(W[P:2 * P].T)
    L["Wvb"] = W[2 * P:].T
    L["Wob"] = g("L0_attn_b_W_out").T
    L["qbias"] = slot_columns(B[None, :P])[0].T
    L["kbias"] = slot_columns(B[None, P:2 * P])[0].T
    L["vbias"], L["obias"] = B[2 * P:], g("L0_attn_b_b_out")
    L["lngT"], L["lnbT"] = g("L0_ffn_ln_g")[:, None], g("L0_ffn_ln_b")[:, None]
    L["abel_w"], L["gate_w"] = g("L0_ffn_abel_w"), g("L0_ffn_gate_w_moe")
    L["abel_b"], L["gate_b"] = g("L0_ffn_abel_b"), g("L0_ffn_gate_b_moe")
    L["w1"] = g("L0_ffn_w1").transpose(1, 0, 2)
    L["b1T"] = g("L0_ffn_b1").reshape(EXPERTS * FC, P).T
    L["w2T"] = g("L0_ffn_w2").transpose(2, 0, 1)
    L["b2T"] = g("L0_ffn_b2").T
    L["gens"] = g("L0_ffn_gens").transpose(1, 0, 2)
    L["gensT"] = g("L0_ffn_gens").transpose(2, 0, 1)
    mix = g("L0_ffn_mix_w").reshape(2 * P)
    L["mixa"], L["mixn"], L["mixb"] = mix[:P], mix[P:], g("L0_ffn_mix_b")
    L.update(constants())
    return L


def kernel(**inputs):
    import numpy as _np
    import concourse.bacc as _bacc
    from concourse import mybir as _mybir
    from concourse.bass_utils import run_bass_kernel_spmd as _run

    nc = _bacc.Bacc("TRN2", target_bir_lowering=False, num_devices=1)
    arrays, args = {}, {}
    for name, a in layouts(inputs).items():
        a = _np.ascontiguousarray(a)
        arrays[f"in_{name}_dram"] = a
        args[name] = nc.dram_tensor(f"in_{name}_dram", a.shape, _mybir.dt.from_np(a.dtype), kind="ExternalInput").ap()
    out = nc.dram_tensor("out_0_dram", (BATCH, SEQ, P), _mybir.dt.from_np(_np.dtype("float32")), kind="ExternalOutput").ap()
    build(nc, args, out)
    r = _run(nc, [arrays], core_ids=[0])
    return r.results[0]["out_0_dram"]
```

```python
from contextlib import ExitStack

import numpy as np

import concourse.bass as bass
from concourse import mybir

ALU = mybir.AluOpType
ACT = mybir.ActivationFunctionType
AX = mybir.AxisListType
F32 = mybir.dt.float32
F32R = mybir.dt.float32r
I32 = mybir.dt.int32

P = 128
BATCH, SEQ = 4, 1024
H, D = 16, 8
TPB = SEQ // P
NT = BATCH * TPB
SLOTS, R = 4, 4
PART = 32
ROWS = 3 * D
BIAS = R * ROWS
AUG = 4
SHIFT = BIAS + R * AUG
EXPERTS, DF = 8, 512
FC = DF // P
GROUP = 4
NG = NT // GROUP
EPS = 1e-5
NROT = 3
TAYLOR = 14
THETA = 2.0
SQUARINGS = 16
QSCALE = float(D) ** -0.5
SAFE = 64.0


class Signal:

    def __init__(self, sem, per, unit=1):
        self.sem, self.per, self.unit = sem, per, unit

    def prime(self, eng):
        eng.sem_inc(self.sem, self.per * self.unit)

    def wait(self, eng, i, k):
        assert -self.per <= k < self.per
        eng.wait_ge(self.sem, (i + 1) * (self.per * self.unit) + (k + 1) * self.unit)


class Steps:

    def __init__(self, sem):
        self.sem, self.done, self.here, self.turn, self.per = sem, 0, 0, 0, 0

    def loop(self, i, per):
        self.done += self.here
        self.turn, self.per, self.here = i, per, 0

    def end(self, turns):
        assert self.here == self.per, (self.here, self.per)
        self.done += self.per * turns
        self.turn, self.per, self.here = 0, 0, 0

    def add(self, ins):
        ins.then_inc(self.sem, 1)
        self.here += 1

    def settle(self, eng):
        eng.wait_ge(self.sem, self.turn * self.per + (self.done + self.here))

    def chain(self, eng, ins):
        self.add(ins)
        self.settle(eng)


def alibi_slopes():
    return np.power(np.float32(2.0), np.float32(8.0) * np.arange(0, -H, -1, dtype=np.float32) / np.float32(H)).astype(np.float32)


def build(nc, I, out, upto=(1, 2, 3, 4)):
    SL = [float(x) for x in alibi_slopes()]
    ctx = ExitStack()
    with ctx:
        def sem(name):
            return ctx.enter_context(nc.semaphore(name))

        def sb(name, shape, dt=F32, scope=ctx):
            return scope.enter_context(nc.sbuf_tensor(name, shape, dt))

        pairJ = ctx.enter_context(nc.psum_tensor("pairJ", [P, 1024], F32))
        pairA = ctx.enter_context(nc.psum_tensor("pairA", [P, 1024], F32))
        pairB = ctx.enter_context(nc.psum_tensor("pairB", [P, 1024], F32))
        pairC = ctx.enter_context(nc.psum_tensor("pairC", [P, 1024], F32))
        bank = [pairJ[:, 0:512], pairJ[:, 512:1024], pairA[:, 0:512], pairA[:, 512:1024], pairB[:, 0:512], pairB[:, 512:1024],
                 pairC[:, 0:512], pairC[:, 512:1024]]

        X = sb("X", [P, NT, P])
        ident = sb("ident", [P, P])
        w2r = sb("w2r", [P, EXPERTS * FC, P])
        b2r = sb("b2r", [EXPERTS, P])
        XN = sb("XN", [P, TPB, P])
        XTB = sb("XTB", [P, SEQ])
        stats = sb("stats", [P, TPB, 6])
        mv = sb("mv", [P, TPB, 2])
        rstd = sb("rstd", [P, TPB])
        rstd2 = sb("rstd2", [P, TPB])
        rall = sb("rall", [P, TPB])
        mhalf = sb("mhalf", [P, TPB])
        Wqa = sb("Wqa", [P, SLOTS, P])
        Wka = sb("Wka", [P, SLOTS, P])
        Wnat = sb("Wnat", [P, 4 * P])
        Wg1T = sb("Wg1T", [D, P])
        Wg2 = sb("Wg2", [D, P])
        Woa = sb("Woa", [P, P])
        gam = sb("gam", [P, P])
        bet = sb("bet", [P, P])
        Wqb = sb("Wqb", [P, SLOTS, BIAS])
        Wkb = sb("Wkb", [P, SLOTS, BIAS])
        Wvb = sb("Wvb", [P, P])
        Wob = sb("Wob", [P, P])
        qbias = sb("qbias", [P, SLOTS])
        kbias = sb("kbias", [P, SLOTS])
        vbias = sb("vbias", [P, P])
        obias = sb("obias", [P, P])
        negq = sb("negq", [P, 1])
        negk = sb("negk", [P, 1])
        negqb = sb("negqb", [P, 1])
        negkb = sb("negkb", [P, 1])
        lngT = sb("lngT", [P, 1])
        lnbT = sb("lnbT", [P, 1])
        Wab = sb("Wab", [P, P + EXPERTS])
        abias = sb("abias", [P, P + EXPERTS])
        b1T = sb("b1T", [P, EXPERTS * FC])
        mixa = sb("mixa", [P, P])
        mixn = sb("mixn", [P, P])
        mixb = sb("mixb", [P, 1])
        rank8 = sb("rank8", [P, EXPERTS])

        v_steps = Steps(sem("vector_steps"))
        g_steps = Steps(sem("gpsimd_steps"))
        x_loaded = sem("x_loaded")
        passed = sem("waits_passed")

        def pass_wait(e):
            e.sem_inc(passed, 1)

        w_loaded = sem("weights_loaded")
        gens_loaded = sem("gens_loaded")
        w2_loaded = sem("w2_loaded")
        out_stored = sem("out_stored")

        with ExitStack() as es:
            A = sb("A", [P, NROT, P], scope=es)
            AT = sb("AT", [P, NROT, P], scope=es)
            M = sb("M", [P, NROT, P], scope=es)
            MT = sb("MT", [P, NROT, P], scope=es)
            rot = sb("rot", [P, P], scope=es)
            rot12 = sb("rot12", [P, P], scope=es)
            w2T = sb("w2T", [P, EXPERTS, DF], scope=es)
            b2T = sb("b2T", [P, EXPERTS], scope=es)
            inv = sb("inv", [P, TAYLOR], scope=es)
            thr = sb("thr", [P, SQUARINGS, NROT], scope=es)
            norm = sb("norm", [P, NROT], scope=es)
            norms = sb("norms", [P, NROT], scope=es)
            act_f = sb("act_f", [P, SQUARINGS, NROT], scope=es)
            now_i = sb("now_i", [P, NROT], I32, scope=es)
            act_i = sb("act_i", [P, SQUARINGS, NROT], I32, scope=es)
            fac = sb("fac", [P, SQUARINGS, NROT], scope=es)
        norm_row = sem("norm_row")
        norm_all = sem("norm_all")
        exp_in = sem("exp_in")
        prod_done = Signal(sem("prod_done"), 2)
        next_done = Signal(sem("next_done"), 2)
        sq_done = Signal(sem("sq_done"), 2)
        sel_done = Signal(sem("sel_done"), 2)
        rot_done = sem("rot_done")
        rot_copied = sem("rot_copied")
        fold_done = sem("fold_done")
        fold_copied = sem("fold_copied")
        gate_w_done = sem("gate_w_done")
        gate_w_copied = sem("gate_w_copied")

        def expm_vector(e):
            e.wait_ge(gens_loaded, 16 * 5)
            e.tensor_reduce(norm[:, :], A[:, :, :], AX.X, ALU.add, apply_absolute_value=True).then_inc(norm_row, 1)
            e.wait_ge(norm_all, 1)
            v_steps.chain(e, e.tensor_tensor(act_f[:, :, :], norms[:, None, :].to_broadcast([P, SQUARINGS, NROT]),
                                             thr[:, :, :], ALU.is_gt))
            v_steps.add(e.tensor_copy(act_i[:, :, :], act_f[:, :, :]))
            v_steps.chain(e, e.tensor_scalar(fac[:, :, :], act_f[:, :, :], -0.5, 1.0, ALU.mult, ALU.add))
            n = SQUARINGS // 2
            while n:
                v_steps.chain(e, e.tensor_tensor(fac[:, 0:n, :], fac[:, 0:n, :], fac[:, n:2 * n, :], ALU.mult))
                n //= 2
            for m in (A, AT):
                v_steps.chain(e, e.tensor_tensor(m[:, :, :], m[:, :, :],
                                                 fac[:, 0, :].unsqueeze(2).to_broadcast([P, NROT, P]), ALU.mult))
            for m, last in ((M, False), (MT, True)):
                ins = e.tensor_copy(m[:, :, :], ident[:, None, :].to_broadcast([P, NROT, P]))
                ins.then_inc(exp_in, 1) if last else v_steps.chain(e, ins)
            next_done.prime(e)
            sel_done.prime(e)
            with e.Fori(0, TAYLOR) as i:
                for k, m in enumerate((M, MT)):
                    prod_done.wait(e, i, 1)
                    e.scalar_tensor_tensor(out=m[:, :, :], in0=bank[k][:, 0:NROT * P].rearrange("p (j n) -> p j n", n=P),
                                           scalar=inv[:, bass.ds(i, 1)],
                                           in1=ident[:, None, :].to_broadcast([P, NROT, P]),
                                           op0=ALU.mult, op1=ALU.add).then_inc(next_done.sem, 1)
            with e.Fori(0, SQUARINGS) as i:
                v_steps.loop(i, 1)
                sel_done.wait(e, i, -1)
                v_steps.chain(e, e.tensor_copy(now_i[:, :], act_i[:, bass.ds(i, 1), :].rearrange("p a j -> p (a j)")))
                for k, m in enumerate((M, MT)):
                    sq_done.wait(e, i, 1)
                    pass_wait(e)
                    e.copy_predicated(m[:, :, :], now_i[:, :].unsqueeze(2).to_broadcast([P, NROT, P]),
                                      bank[k][:, 0:NROT * P].rearrange("p (j n) -> p j n", n=P)).then_inc(sel_done.sem, 1)
            v_steps.end(SQUARINGS)
            for k, m in enumerate((rot12, rot)):
                e.wait_ge(rot_done, k + 1)
                e.tensor_copy(m[:, :], bank[0][:, 0:P]).then_inc(rot_copied, 1)
            for q in range(EXPERTS * FC // 4):
                e.wait_ge(fold_done, q + 1)
                e.tensor_copy(w2r[:, 4 * q:4 * q + 4, :].rearrange("p c n -> p (c n)"), bank[q % 2]).then_inc(fold_copied, 1)
            e.wait_ge(fold_done, EXPERTS + 1)
            e.tensor_copy(b2r[:, :], bank[0][0:EXPERTS, 0:P]).then_inc(fold_copied, 1)

        def expm_gpsimd(e):
            g_steps.chain(e, e.memset(mhalf[:, :], -0.5))
            e.wait_ge(norm_row, 1)
            e.partition_all_reduce(norms[:, :], norm[:, :], P, bass.bass_isa.ReduceOp.max).then_inc(norm_all, 1)

        def expm_tensor(e):
            e.wait_ge(w_loaded, 16 * N_WLOADS)
            e.matmul(bank[0][:, 0:P], Wg1T[:, :], Wg2[:, :], start=True, stop=True).then_inc(gate_w_done, 1)
            e.wait_ge(gate_w_copied, 1)
            e.wait_ge(exp_in, 1)
            prod_done.prime(e)
            sq_done.prime(e)

            def products(lefts, done):
                for k, (left, right) in enumerate(lefts):
                    for j in range(NROT):
                        last = e.matmul(bank[k][:, j * P:(j + 1) * P], left[:, j, :], right[:, j, :], start=True, stop=True)
                    last.then_inc(done.sem, 1)
            with e.Fori(0, TAYLOR) as i:
                next_done.wait(e, i, -1)
                products([(AT, M), (A, MT)], prod_done)
            next_done.wait(e, TAYLOR - 1, 1)
            with e.Fori(0, SQUARINGS) as i:
                sel_done.wait(e, i, -1)
                products([(MT, M), (M, MT)], sq_done)
            sel_done.wait(e, SQUARINGS - 1, 1)
            e.matmul(bank[0][:, 0:P], MT[:, 1, :], M[:, 2, :], start=True, stop=True).then_inc(rot_done, 1)
            e.wait_ge(rot_copied, 1)
            e.matmul(bank[0][:, 0:P], MT[:, 0, :], rot12[:, :], start=True, stop=True).then_inc(rot_done, 1)
            e.wait_ge(rot_copied, 2)
            e.wait_ge(w2_loaded, 32)
            for q in range(EXPERTS):
                if q >= 2:
                    e.wait_ge(fold_copied, q - 1)
                for c in range(FC):
                    last = e.matmul(bank[q % 2][:, c * P:(c + 1) * P], w2T[:, q, c * P:(c + 1) * P], rot[:, :], start=True, stop=True)
                last.then_inc(fold_done, 1)
            e.wait_ge(fold_copied, EXPERTS)
            e.matmul(bank[0][0:EXPERTS, 0:P], b2T[:, :], rot[:, :], start=True, stop=True).then_inc(fold_done, 1)

        def inverse_root(e, out, var):
            pass_wait(e)
            g_steps.chain(e, e.tensor_scalar(out, var, EPS, None, ALU.add))
            return e.tensor_tensor(out, out, mhalf[:, 0:out.shape[1]], ALU.pow)

        class Norm:

            def __init__(self, name, twice=False):
                self.twice = twice
                self.stats_ready = Signal(sem(name + "_stats_ready"), 1)
                self.rstd_ready = Signal(sem(name + "_rstd_ready"), 1)
                self.xn_ready = Signal(sem(name + "_xn_ready"), 2)

            def prime_vector(self, e):
                self.stats_ready.prime(e)
                self.xn_ready.prime(e)

            def prime_gpsimd(self, e):
                self.rstd_ready.prime(e)

            def vector(self, e, i, keep=None):
                for t in range(TPB):
                    v_steps.add(e.bn_stats(stats[:, t, :], X[:, bass.ds(i * TPB + t, 1), :].rearrange("p a d -> p (a d)")))
                v_steps.settle(e)
                pass_wait(e)
                for t in range(TPB):
                    ins = e.bn_aggr(mv[:, t, :], stats[:, t, :])
                    ins.then_inc(self.stats_ready.sem, 1) if t == TPB - 1 else v_steps.add(ins)
                self.rstd_ready.wait(e, i, 0)
                for t in range(TPB):
                    ins = e.tensor_scalar(XN[:, t, :], X[:, bass.ds(i * TPB + t, 1), :].rearrange("p a d -> p (a d)"),
                                          mv[:, t, 0:1], (rall if self.twice else rstd)[:, t:t + 1], ALU.subtract, ALU.mult)
                    ins.then_inc(self.xn_ready.sem, 1) if t % GROUP == GROUP - 1 else v_steps.add(ins)
                if keep is not None:
                    for t in range(TPB):
                        v_steps.add(e.tensor_scalar(keep[:, bass.ds(i * TPB + t, 1), :].rearrange("p a d -> p (a d)"),
                                                    X[:, bass.ds(i * TPB + t, 1), :].rearrange("p a d -> p (a d)"),
                                                    mv[:, t, 0:1], rstd[:, t:t + 1], ALU.subtract, ALU.mult))

            def gpsimd(self, e, i):
                self.stats_ready.wait(e, i, 0)
                var = mv[:, :, 1]
                if not self.twice:
                    inverse_root(e, rstd[:, :], var).then_inc(self.rstd_ready.sem, 1)
                    return
                g_steps.chain(e, inverse_root(e, rstd[:, :], var))
                g_steps.chain(e, e.tensor_tensor(rstd2[:, :], var, rstd[:, :], ALU.mult))
                g_steps.chain(e, e.tensor_tensor(rstd2[:, :], rstd2[:, :], rstd[:, :], ALU.mult))
                g_steps.chain(e, inverse_root(e, rstd2[:, :], rstd2[:, :]))
                e.tensor_tensor(rall[:, :], rstd[:, :], rstd2[:, :], ALU.mult).then_inc(self.rstd_ready.sem, 1)

            def transposes(self, e, i, half, to):
                self.xn_ready.wait(e, i, half)
                for j in range(GROUP):
                    last = e.transpose(to[:, j * P:(j + 1) * P], XN[:, GROUP * half + j, :], ident[:, :])
                return last

        att = ExitStack()
        Qpad = sb("Qpad", [P, SLOTS, R, SEQ], F32R, att)
        KA = sb("KA", [P, SLOTS, SEQ], F32R, att)
        T = sb("T", [P, 2, 512], scope=att)
        TH = sb("TH", [P, 2, 512], F32R, att)
        V9 = sb("V9", [P, TPB, H, D + 1], scope=att)
        TR = XTB

        zeroed = sem("zeroed")

        aa = ExitStack()
        QST = sb("QST", [P, 2, SEQ], F32R, aa)
        maskT = sb("maskT", [P, H, P], scope=aa)
        sel = sb("sel", [P, SLOTS, P], scope=aa)
        lamq = sb("lamq", [P, P], scope=aa)
        lamk = sb("lamk", [P, P], scope=aa)
        lamc = sb("lamc", [P, 1], scope=aa)
        blk = sb("blk", [P, P], scope=aa)
        KN = sb("KN", [P, TPB, P], scope=aa)
        GT = sb("GT", [P, TPB, P], scope=aa)
        GB = sb("GB", [P, TPB, P], scope=aa)
        QL = sb("QL", [P, TPB, P], scope=aa)
        PA = sb("PA", [P, 2, 512], scope=aa)
        OTS = sb("OTS", [P, 2, 512], scope=aa)
        KV = sb("KV", [P, 2, P], scope=aa)
        KVN = sb("KVN", [P, P], scope=aa)
        ONS = sb("ONS", [P, GROUP, P], scope=aa)
        aa.close()
        ab = ExitStack()
        KB = sb("KB", [P, SLOTS, SEQ], F32R, ab)
        EX = sb("EX", [P, 8, SEQ], scope=ab)
        over = sb("over", [P, P], scope=ab)
        overT = sb("overT", [P, P], scope=ab)
        OTB = T[:, :, :].rearrange("p a n -> p (a n)")
        MX = sb("MX", [P, H * TPB], scope=ab)
        MXT = sb("MXT", [P, P], F32R, ab)
        Wqkn = sb("Wqkn", [P, 2, P], scope=ab)
        nbias = sb("nbias", [P, 2], scope=ab)
        top = sb("top", [P, 4], scope=ab)
        bound = sb("bound", [P, 2], scope=ab)
        blkb = sb("blkb", [P, P], scope=ab)
        large = sb("large", [1, 1], scope=ab)
        flag = sb("flag", [1, 1], I32, ab)
        DEN = sb("DEN", [P, GROUP, R], scope=ab)
        ATT = XN
        qbs = sb("qbs", [P, SLOTS], scope=ab)
        ab.close()
        att.close()

        AJ = 30
        a_norm = Norm("a")
        a_job = Signal(sem("a_job_done"), AJ)
        a_evac = Signal(sem("a_job_evacuated"), AJ)
        a_split = Signal(sem("a_split_done"), 16)
        a_qpad = [Signal(sem(f"a_q_padded{s}"), 1, 16 * R) for s in range(SLOTS)]
        a_score = Signal(sem("a_scores_done"), 4 * TPB)
        a_masked = Signal(sem("a_masked"), 4 * TPB)
        a_pv = Signal(sem("a_pv_done"), 4 * TPB)
        a_ot = Signal(sem("a_ot_evacuated"), TPB)
        a_on = Signal(sem("a_o_natural"), TPB)
        a_onorm = Signal(sem("a_o_normed"), 2)
        a_ostat = Signal(sem("a_o_stats"), 2)
        a_orstd = Signal(sem("a_o_rstd"), 2)
        a_y = Signal(sem("a_y_ready"), 2)
        a_aux = Signal(sem("a_aux_done"), TPB - 1 + 2)
        a_auxr = Signal(sem("a_aux_read"), TPB - 1 + 2)
        a_kv = Signal(sem("a_state_ready"), TPB - 1)
        a_pool = Signal(sem("a_decayed"), 2)
        a_tables = sem("a_tables_loaded")
        ot_zero = sem("ot_zeroed")

        U7 = TPB - 1
        LAST = 4 * TPB + 8

        def aux_index(kind, n):
            order = [("kv", 0), ("kv", 1), ("kv", 2), ("kv", 3), ("kv", 4), ("kv", 5), ("y", 0), ("kv", 6), ("y", 1)]
            return order.index((kind, n))

        def a_steps(u):
            return {
                "score": u if u < 32 else None,
                "pv": u - 1 if 1 <= u <= 32 else None,
                "kv": (u - 2) // 4 if u % 4 == 2 and (u - 2) // 4 < U7 else None,
                "sel": (u - 6) // 4 if u >= 6 and u % 4 == 2 and (u - 6) // 4 < TPB else None,
                "ot": (u - 4) // 4 if u >= 4 and u % 4 == 0 and (u - 4) // 4 < TPB else None,
                "norm": {19: 0, 35: 1}.get(u),
                "turn": {23: 0, 36: 1}.get(u),
                "y": {25: 0, 37: 1}.get(u),
            }

        def attn_a_sync(e):
            for s in a_qpad:
                s.prime(e)
            e.wait_ge(zeroed, 1)
            with e.Fori(0, BATCH) as i:
                for s in range(SLOTS):
                    a_split.wait(e, i, 4 * s + 1)
                    pass_wait(e)
                    a_masked.wait(e, i, -1)
                    for r in range(R):
                        e.dma_start(Qpad[PART * r:PART * r + ROWS, s, r, :].bitcast(F32),
                                    QST[PART * r:PART * r + ROWS, s % 2, :].bitcast(F32)).then_inc(a_qpad[s].sem, 16)

        def attn_a_gpsimd(e):
            a_norm.prime_gpsimd(e)
            a_pool.prime(e)
            a_orstd.prime(e)
            a_y.prime(e)
            e.wait_ge(a_tables, 16 * 6)
            e.wait_ge(w_loaded, 16 * N_WLOADS)
            with e.Fori(0, BATCH) as i:
                g_steps.loop(i, 8)
                a_norm.gpsimd(e, i)
                a_evac.wait(e, i, 2 + 16 + 7)
                def rows(t):
                    return t[:, None, :].to_broadcast([P, TPB, P])
                g_steps.add(e.tensor_tensor(KN[:, :, :], KN[:, :, :], rows(lamk), ALU.mult))
                pass_wait(e)
                g_steps.chain(e, e.tensor_scalar(GT[:, :, :], GT[:, :, :], 0.5, 0.5, ALU.mult, ALU.add))
                g_steps.chain(e, e.tensor_tensor(GB[:, :, :], GT[:, :, :], rows(bet), ALU.mult))
                e.tensor_tensor(GT[:, :, :], GT[:, :, :], rows(gam), ALU.mult).then_inc(a_pool.sem, 1)
                a_evac.wait(e, i, 2 + 16 + 8 + 1)
                e.tensor_tensor(QL[:, :, :], QL[:, :, :], rows(lamq), ALU.mult).then_inc(a_pool.sem, 1)
                for g in range(2):
                    a_ostat.wait(e, i, g)
                    inverse_root(e, rstd2[:, 4 * g:4 * g + 4], mv[:, 4 * g:4 * g + 4, 1]).then_inc(a_orstd.sem, 1)
                    a_onorm.wait(e, i, g)
                    a_pool.wait(e, i, 1)
                    g_steps.chain(e, e.tensor_tensor(ONS[:, :, :], ONS[:, :, :], GT[:, 4 * g:4 * g + 4, :], ALU.mult))
                    e.tensor_tensor(ONS[:, :, :], ONS[:, :, :], GB[:, 4 * g:4 * g + 4, :], ALU.add).then_inc(a_y.sem, 1)
            g_steps.end(BATCH)

        def attn_a_scalar(e):
            a_evac.prime(e)
            a_ot.prime(e)
            with e.Fori(0, BATCH) as i:
                def job(n):
                    a_job.wait(e, i, n)
                    return bank[n % 2]
                for half in range(2):
                    e.activation(XTB[:, half * 512:(half + 1) * 512], job(half), ACT.Copy).then_inc(a_evac.sem, 1)
                for m in range(16):
                    a_split.wait(e, i, m - 2)
                    e.activation(T[:, m % 2, :], job(2 + m), ACT.Silu).then_inc(a_evac.sem, 1)
                for c in range(TPB):
                    b = job(18 + c)
                    e.activation(KN[:, c, :], b[:, 0:P], ACT.Silu)
                    e.activation(V9[:, c, :, 0:D], b[:, P:2 * P].rearrange("p (h d) -> p h d", d=D), ACT.Silu)
                    e.activation(GT[:, c, :], b[:, 2 * P:3 * P], ACT.Tanh, scale=0.5).then_inc(a_evac.sem, 1)
                for half in range(2):
                    e.activation(QL[:, 4 * half:4 * half + 4, :].rearrange("p c n -> p (c n)"), job(26 + half), ACT.Silu).then_inc(a_evac.sem, 1)
                for u in range(LAST):
                    w = a_steps(u)
                    if w["ot"] is not None:
                        c = w["ot"]
                        a_pv.wait(e, i, 4 * c + 3)
                        a_on.wait(e, i, c - 2)
                        e.activation(OTS[:, c % 2, :], bank[4 + c % 2], ACT.Copy).then_inc(a_ot.sem, 1)
                    if w["turn"] is not None:
                        g = w["turn"]
                        e.activation(TR[:, g * 512:(g + 1) * 512], job(28 + g), ACT.Copy).then_inc(a_evac.sem, 1)

        def attn_a_vector(e):
            a_norm.prime_vector(e)
            for s in (a_split, a_masked, a_onorm, a_ostat, a_auxr, a_kv):
                s.prime(e)
            e.wait_ge(gate_w_done, 1)
            e.tensor_copy(Wnat[:, 2 * P:3 * P], bank[0][:, 0:P]).then_inc(gate_w_copied, 1)

        def attn_a_vector_loop(e):
            e.memset(bank[4], 0.0).then_inc(ot_zero, 1)
            e.memset(bank[5], 0.0).then_inc(ot_zero, 1)
            e.wait_ge(a_tables, 16 * 6)
            with e.Fori(0, BATCH) as i:
                v_steps.loop(i, A_V)
                a_norm.vector(e, i)
                for m in range(16):
                    s, side, half = m // 4, (m // 2) % 2, m % 2
                    a_evac.wait(e, i, 2 + m)
                    if side == 0 and half == 0:
                        a_qpad[s - 2].wait(e, i, 0 if s >= 2 else -1)
                    v_steps.chain(e, e.tensor_copy(TH[:, m % 2, :], T[:, m % 2, :]))
                    to = (QST[:, s % 2, half * 512:(half + 1) * 512] if side == 0 else KA[:, s, half * 512:(half + 1) * 512])
                    e.scalar_tensor_tensor(out=to, in0=TH[:, m % 2, :].bitcast(F32), scalar=(negq if side == 0 else negk)[:, 0:1],
                                           in1=T[:, m % 2, :], op0=ALU.mult, op1=ALU.add).then_inc(a_split.sem, 1)
                for u in range(LAST):
                    w = a_steps(u)
                    if w["score"] is not None:
                        s = u % 4
                        a_score.wait(e, i, u)
                        a_pv.wait(e, i, u - 2)
                        e.tensor_tensor(PA[:, u % 2, :], bank[2 + u % 2], maskT[:, 4 * s:4 * s + 4, :].rearrange("p h n -> p (h n)"),
                                        ALU.mult).then_inc(a_masked.sem, 1)
                    if w["kv"] is not None:
                        c = w["kv"]
                        a_aux.wait(e, i, aux_index("kv", c))
                        e.tensor_tensor(KVN[:, :], bank[7][:, 0:P], blk[:, :], ALU.mult).then_inc(a_auxr.sem, 1)
                        a_auxr.wait(e, i, aux_index("kv", c))
                        to = KV[:, (c + 1) % 2, :]
                        if c == 0:
                            a_on.wait(e, i, -1)
                            e.tensor_copy(to, KVN[:, :]).then_inc(a_kv.sem, 1)
                        else:
                            a_on.wait(e, i, c - 1)
                            a_kv.wait(e, i, c - 1)
                            e.scalar_tensor_tensor(out=to, in0=KV[:, c % 2, :], scalar=lamc[:, 0:1], in1=KVN[:, :],
                                                   op0=ALU.mult, op1=ALU.add).then_inc(a_kv.sem, 1)
                    if w["norm"] is not None:
                        g = w["norm"]
                        a_on.wait(e, i, 4 * g + 3)
                        for j in range(4):
                            v_steps.add(e.bn_stats(stats[:, 4 * g + j, :], bank[6][:, j * P:(j + 1) * P]))
                        v_steps.settle(e)
                        pass_wait(e)
                        for j in range(4):
                            ins = e.bn_aggr(mv[:, 4 * g + j, :], stats[:, 4 * g + j, :])
                            ins.then_inc(a_ostat.sem, 1) if j == 3 else v_steps.add(ins)
                        a_orstd.wait(e, i, g)
                        if g == 1:
                            a_job.wait(e, i, 28)
                        else:
                            a_job.wait(e, i, -1)
                        for j in range(4):
                            ins = e.tensor_scalar(ONS[:, j, :], bank[6][:, j * P:(j + 1) * P], mv[:, 4 * g + j, 0:1],
                                                  rstd2[:, 4 * g + j:4 * g + j + 1], ALU.subtract, ALU.mult)
                            ins.then_inc(a_onorm.sem, 1) if j == 3 else v_steps.add(ins)
                    if w["y"] is not None:
                        g = w["y"]
                        a_aux.wait(e, i, aux_index("y", g))
                        xs = X[:, bass.ds(i * TPB + 4 * g, 4), :]
                        e.tensor_tensor(xs, bank[7].rearrange("p (t n) -> p t n", n=P), xs, ALU.add).then_inc(a_auxr.sem, 1)
                        a_auxr.wait(e, i, aux_index("y", g))
            v_steps.end(BATCH)

        A_V = 8 + 7 + 6 + 16 + 2 * (4 + 3 + 3)

        def attn_a_tensor(e):
            for s in (a_job, a_score, a_pv, a_on, a_aux):
                s.prime(e)
            e.wait_ge(ot_zero, 2)
            with e.Fori(0, BATCH) as i:
                def job(n):
                    a_evac.wait(e, i, n - 2)
                    return bank[n % 2]
                for half in range(2):
                    b = job(half)
                    a_norm.transposes(e, i, half, b).then_inc(a_job.sem, 1)
                a_evac.wait(e, i, 1)
                for m in range(16):
                    s, side, half = m // 4, (m // 2) % 2, m % 2
                    e.matmul(job(2 + m), (Wqa if side == 0 else Wka)[:, s, :], XTB[:, half * 512:(half + 1) * 512],
                             start=True, stop=True).then_inc(a_job.sem, 1)
                for c in range(TPB):
                    e.matmul(job(18 + c)[:, 0:3 * P], XTB[:, c * P:(c + 1) * P], Wnat[:, 0:3 * P], start=True, stop=True).then_inc(a_job.sem, 1)
                for half in range(2):
                    e.matmul(job(26 + half), Wnat[:, 3 * P:4 * P], XTB[:, half * 512:(half + 1) * 512], start=True, stop=True).then_inc(a_job.sem, 1)
                a_pool.wait(e, i, 1)
                for u in range(LAST):
                    w = a_steps(u)
                    if w["score"] is not None:
                        c, s = u // 4, u % 4
                        if c == 0:
                            a_split.wait(e, i, 4 * s + 3)
                            a_qpad[s].wait(e, i, 0)
                        a_masked.wait(e, i, u - 2)
                        e.matmul(bank[2 + u % 2].rearrange("p (r n) -> p r n", r=R), KA[:, s, c * P:(c + 1) * P],
                                 Qpad[:, s, :, c * P:(c + 1) * P], start=True, stop=True).then_inc(a_score.sem, 1)
                    if w["pv"] is not None:
                        v = w["pv"]
                        c, s = v // 4, v % 4
                        a_masked.wait(e, i, v)
                        if s == 0:
                            a_ot.wait(e, i, c - 2)
                        for r in range(R):
                            last = e.matmul(bank[4 + c % 2][PART * r:PART * r + D, s * P:(s + 1) * P], V9[:, c, 4 * s + r, 0:D],
                                            PA[:, v % 2, r * P:(r + 1) * P], start=True, stop=True)
                        last.then_inc(a_pv.sem, 1)
                    if w["kv"] is not None:
                        c = w["kv"]
                        a_auxr.wait(e, i, aux_index("kv", c) - 1)
                        e.matmul(bank[7][:, 0:P].rearrange("p (h d) -> p h d", d=D), KN[:, c, :], V9[:, c, :, 0:D],
                                 start=True, stop=True).then_inc(a_aux.sem, 1)
                    if w["sel"] is not None:
                        c = w["sel"]
                        a_ot.wait(e, i, c)
                        if c % 4 == 0:
                            a_onorm.wait(e, i, c // 4 - 1)
                        to = bank[6][:, (c % 4) * P:(c % 4 + 1) * P]
                        for s in range(SLOTS):
                            last = e.matmul(to, OTS[:, c % 2, s * P:(s + 1) * P], sel[:, s, :], start=(s == 0), stop=(s == 3 and c == 0))
                        if c:
                            a_kv.wait(e, i, c - 1)
                            last = e.matmul(to, QL[:, c, :], KV[:, c % 2, :], start=False, stop=True)
                        last.then_inc(a_on.sem, 1)
                    if w["turn"] is not None:
                        g = w["turn"]
                        b = job(28 + g)
                        a_y.wait(e, i, g)
                        for j in range(4):
                            last = e.transpose(b[:, j * P:(j + 1) * P], ONS[:, j, :], ident[:, :])
                        last.then_inc(a_job.sem, 1)
                    if w["y"] is not None:
                        g = w["y"]
                        a_evac.wait(e, i, 28 + g)
                        a_auxr.wait(e, i, aux_index("y", g) - 1)
                        for j in range(4):
                            last = e.matmul(bank[7][:, j * P:(j + 1) * P], TR[:, (4 * g + j) * P:(4 * g + j + 1) * P], Woa[:, :], start=True, stop=True)
                        last.then_inc(a_aux.sem, 1)

        BJ = 28
        DJ = 2 * SLOTS
        GROUPS = SLOTS * TPB
        UNITS = GROUPS * R
        b_norm = Norm("b")
        b_job = Signal(sem("b_job_done"), BJ)
        b_evac = Signal(sem("b_job_evacuated"), BJ)
        b_ojob = Signal(sem("b_o_natural"), DJ)
        b_onorm = Signal(sem("b_o_normalised"), DJ)
        b_split = Signal(sem("b_split_done"), 16)
        b_qpad = [Signal(sem(f"b_q_padded{s}"), 1, 16 * R) for s in range(SLOTS)]
        b_kpad = [Signal(sem(f"b_k_copied{s}"), 1, 16) for s in range(SLOTS)]
        b_mscore = Signal(sem("b_max_scores_done"), GROUPS * R)
        b_mred = Signal(sem("b_max_reduced"), GROUPS * R)
        b_shift = Signal(sem("b_shift_stored"), 1, 16)
        b_mjob = Signal(sem("b_natural_done"), 4)
        b_mread = Signal(sem("b_natural_read"), 4)
        b_bound = Signal(sem("b_bound_ready"), 1)
        b_sum = Signal(sem("b_bound_summed"), 1)
        b_sumread = Signal(sem("b_bound_read"), 1)
        b_flag = Signal(sem("b_flag_ready"), 1)
        b_score = Signal(sem("b_scores_done"), UNITS)
        b_diag = Signal(sem("b_diagonal_done"), UNITS)
        b_exp = Signal(sem("b_exponentials_done"), UNITS)
        b_pv = Signal(sem("b_pv_done"), GROUPS)
        b_ot = Signal(sem("b_ot_copied"), SLOTS)
        b_vb = Signal(sem("b_v_bias_added"), 1)
        b_xb = Signal(sem("b_out_bias_added"), 1)
        b_yx = Signal(sem("b_y_added"), 2)
        b_y = Signal(sem("b_y_done"), 2)
        b_tables = sem("b_tables_loaded")
        b_rows = sem("b_rows_loaded")
        b_cleared = sem("b_cleared")
        b_begin = sem("b_may_begin")
        b_ones = sem("b_ones_set")

        QSTB = EX[:, 0:2, :]
        pairs = [pairA, pairB]

        def attn_b_sync(e):
            for s in b_qpad + b_kpad + [b_shift]:
                s.prime(e)
            e.wait_ge(b_begin, 1)
            for a, b in ((over, "over"), (overT, "overT"), (blkb, "blk"), (nbias, "nbias")):
                e.dma_start(a[:, :], I[b]).then_inc(b_tables, 16)
            e.dma_start(Wqkn[:, :, :], I["Wqkn"]).then_inc(b_tables, 16)
            e.wait_ge(b_rows, 16 * (R + 2))
            with e.Fori(0, BATCH) as i:
                for s in range(SLOTS):
                    b_split.wait(e, i, 4 * s + 1)
                    pass_wait(e)
                    b_score.wait(e, i, -1)
                    for r in range(R):
                        e.dma_start(Qpad[ROWS * r:ROWS * (r + 1), s, r, :].bitcast(F32),
                                    QSTB[ROWS * r:ROWS * (r + 1), s % 2, :]).then_inc(b_qpad[s].sem, 16)
                    b_split.wait(e, i, 4 * s + 3)
                    e.dma_start(KB[0:BIAS, s, :].bitcast(F32), KA[0:BIAS, s, :].bitcast(F32)).then_inc(b_kpad[s].sem, 16)
                b_evac.wait(e, i, SJ)
                e.dma_start(Qpad[SHIFT:SHIFT + 1, :, :, :].bitcast(F32).rearrange("a s r (t n) -> a (s r t) n", n=P),
                            MXT[:, :].bitcast(F32)).then_inc(b_shift.sem, 16)

        SQ = EX[:, 4:6, :].rearrange("p a (h n) -> p (a h) n", h=2)
        SQJ = 2
        QJ = 6
        VJ = 22
        SJ = 30
        OJ = 31
        BJ = 33
        for g in (b_job, b_evac):
            g.per = BJ

        def job_order():
            order = [("a", n) for n in range(QJ + 4)] + [("m", n) for n in range(4)]
            order += [("a", n) for n in range(QJ + 4, VJ + TPB)] + [("s", 0), ("a", SJ)]
            order += [("a", OJ), ("a", OJ + 1)]
            order += [("y", 0), ("y", 1)]
            assert len(order) % 2 == 0
            return order

        ORDER = job_order()
        READ_BY = {"a": b_evac, "y": b_yx, "m": b_mread, "s": b_sumread}

        def job_bank(kind, n):
            return bank[ORDER.index((kind, n)) % 2]

        def job_free(e, i, kind, n):
            at = ORDER.index((kind, n))
            k, m = ORDER[at - 2]
            g = READ_BY[k]
            g.wait(e, i, m if at >= 2 else m - g.per)
            return bank[at % 2]

        def ring_order():
            order = []
            for s in range(SLOTS):
                for g in range(TPB):
                    order += [("u", (s * TPB + g) * R), ("u", (s * TPB + g) * R + 1)]
                    if s and g == 2:
                        order.append(("o", s - 1))
                    order += [("u", (s * TPB + g) * R + 2), ("u", (s * TPB + g) * R + 3)]
            return order + [("o", SLOTS - 1)]

        RING = ring_order()
        pairs3 = [pairA, pairB, pairJ]

        def ring_pair(kind, n):
            return pairs3[RING.index((kind, n)) % 3]

        def ring_free(e, i, kind, n):
            at = RING.index((kind, n))
            if at == 2:
                b_evac.wait(e, i, SJ)
                b_sumread.wait(e, i, 0)
            elif at > 2:
                k, m = RING[at - 3]
                if k == "u":
                    b_exp.wait(e, i, m)
                else:
                    b_onorm.wait(e, i, 2 * m + 1)
            else:
                b_exp.wait(e, i, at - 2)
            return pairs3[at % 3]

        def attn_b_gpsimd(e):
            b_norm.prime_gpsimd(e)
            b_vb.prime(e)
            b_xb.prime(e)
            e.wait_ge(b_begin, 1)
            e.memset(Qpad[:, :, :, :].bitcast(F32), 0.0).then_inc(b_cleared, 1)
            e.memset(KA[:, :, :].bitcast(F32), 0.0).then_inc(b_cleared, 1)
            e.memset(KB[:, :, :].bitcast(F32), 0.0).then_inc(b_cleared, 1)
            e.memset(V9[:, :, :, :], 1.0).then_inc(b_ones, 1)
            e.wait_ge(b_cleared, 3)
            for r in range(R):
                e.dma_start(Qpad[BIAS + AUG * r:BIAS + AUG * (r + 1), :, r, :], I["augq"][r]).then_inc(b_rows, 16)
            e.dma_start(KA[BIAS:SHIFT + 1, :, :], I["auga"]).then_inc(b_rows, 16)
            e.dma_start(KB[BIAS:SHIFT + 1, :, :], I["augb"]).then_inc(b_rows, 16)
            with e.Fori(0, BATCH) as i:
                g_steps.loop(i, 1)
                b_norm.gpsimd(e, i)
                xs = X[:, bass.ds(i * TPB, TPB), :]
                b_norm.xn_ready.wait(e, i, 1)
                e.tensor_tensor(xs, xs, obias[:, None, :].to_broadcast([P, TPB, P]), ALU.add).then_inc(b_xb.sem, 1)
                b_onorm.wait(e, i, DJ - 1)
                e.tensor_tensor(ATT[:, :, :], ATT[:, :, :], vbias[:, None, :].to_broadcast([P, TPB, P]), ALU.add).then_inc(b_vb.sem, 1)
            g_steps.end(BATCH)

        def attn_b_scalar(e):
            b_evac.prime(e)
            b_exp.prime(e)
            e.wait_ge(b_ones, 1)
            e.wait_ge(qb_ready, 1)
            e.wait_ge(b_tables, 16 * 5)
            with e.Fori(0, BATCH) as i:
                def job(n):
                    b_job.wait(e, i, n)
                    return job_bank("a", n)
                for half in range(2):
                    e.activation(XTB[:, half * 512:(half + 1) * 512], job(half), ACT.Copy).then_inc(b_evac.sem, 1)
                b_pv.wait(e, i, -1)
                for n in range(4):
                    e.activation(SQ[:, n, :], job(SQJ + n), ACT.Square, bias=nbias[:, n // 2:n // 2 + 1]).then_inc(b_evac.sem, 1)
                for m in range(16):
                    s, side = m // 4, (m // 2) % 2
                    b_split.wait(e, i, m - 2)
                    e.activation(T[0:BIAS, m % 2, :], job(QJ + m)[0:BIAS, :], ACT.Identity, bias=(qbs if side == 0 else kbias)[0:BIAS, s:s + 1],
                                 scale=(QSCALE if side == 0 else 1.0)).then_inc(b_evac.sem, 1)
                for c in range(TPB):
                    e.activation(V9[:, c, :, 0:D], job(VJ + c)[:, 0:P].rearrange("p (h d) -> p h d", d=D), ACT.Copy).then_inc(b_evac.sem, 1)
                for g in b_qpad + b_kpad:
                    g.wait(e, i, 0)
                b = job(SJ)
                b_shift.wait(e, i, -1)
                e.activation(MXT[:, :], b[:, 0:P], ACT.Copy, scale=-1.0).then_inc(b_evac.sem, 1)
                for s in range(SLOTS):
                    for n in range(s * TPB * R, (s + 1) * TPB * R):
                        b_diag.wait(e, i, n)
                        if n % R == 0:
                            b_pv.wait(e, i, n // R - 2)
                        e.activation(EX[:, n % 8, :], ring_pair("u", n)[:, :], ACT.Exp).then_inc(b_exp.sem, 1)
                for half in range(2):
                    e.activation(TR[:, half * 512:(half + 1) * 512], job(OJ + half), ACT.Copy).then_inc(b_evac.sem, 1)

        qb_ready = sem("q_bias_scaled")

        def attn_b_vector(e):
            b_norm.prime_vector(e)
            for g in (b_split, b_mred, b_diag, b_ot, b_onorm, b_yx, b_mread, b_bound, b_sumread, b_flag):
                g.prime(e)
            e.wait_ge(b_begin, 1)
            e.tensor_scalar(qbs[0:BIAS, :], qbias[0:BIAS, :], QSCALE, None, ALU.mult).then_inc(qb_ready, 1)
            for b in (6, 7):
                v_steps.add(e.memset(bank[b], 0.0))
            v_steps.settle(e)
            e.memset(MX[:, :], 0.0).then_inc(b_otzero, 1)
            e.wait_ge(b_tables, 16 * 5)
            with e.Fori(0, BATCH) as i:
                v_steps.loop(i, B_V)
                b_norm.vector(e, i)
                for m in range(16):
                    s, side, half = m // 4, (m // 2) % 2, m % 2
                    b_evac.wait(e, i, QJ + m)
                    if side == 0 and half == 0:
                        if s < 2:
                            b_pv.wait(e, i, -1)
                        else:
                            b_qpad[s - 2].wait(e, i, 0)
                    v_steps.chain(e, e.tensor_copy(TH[0:BIAS, m % 2, :], T[0:BIAS, m % 2, :]))
                    if side:
                        b_kpad[s].wait(e, i, -1)
                    to = (QSTB[0:BIAS, s % 2, half * 512:(half + 1) * 512].bitcast(F32R) if side == 0
                          else KA[0:BIAS, s, half * 512:(half + 1) * 512])
                    e.scalar_tensor_tensor(out=to, in0=TH[0:BIAS, m % 2, :].bitcast(F32), scalar=(negqb if side == 0 else negkb)[0:BIAS, 0:1],
                                           in1=T[0:BIAS, m % 2, :], op0=ALU.mult, op1=ALU.add).then_inc(b_split.sem, 1)
                    if m == 3:
                        for n in range(4):
                            b_mjob.wait(e, i, n)
                            e.tensor_reduce(top[:, n:n + 1], job_bank("m", n), AX.X, ALU.max).then_inc(b_mread.sem, 1)
                        b_mread.wait(e, i, 3)
                        v_steps.add(e.tensor_tensor(bound[:, 0:1], top[:, 0:1], top[:, 1:2], ALU.max))
                        v_steps.chain(e, e.tensor_tensor(bound[:, 1:2], top[:, 2:3], top[:, 3:4], ALU.max))
                        b_sum.wait(e, i, -1)
                        e.tensor_tensor(top[:, 0:1], bound[:, 0:1], bound[:, 1:2], ALU.mult).then_inc(b_bound.sem, 1)

                def normalise(s):
                    for half in range(2):
                        b_ojob.wait(e, i, 2 * s + half)
                        b = ring_pair("o", s)[:, 512 * half:512 * (half + 1)].rearrange("p (t c n) -> p t c n", t=GROUP, c=R)
                        v_steps.chain(e, e.reciprocal(DEN[:, :, :], b[:, :, :, D]))
                        if s == 0 and half == 0:
                            b_job.wait(e, i, 1)
                        e.tensor_tensor(ATT[:, GROUP * half:GROUP * half + GROUP, R * D * s:R * D * (s + 1)].rearrange("p t (c d) -> p t c d", d=D),
                                        b[:, :, :, 0:D], DEN[:, :, :].unsqueeze(3).to_broadcast([P, GROUP, R, D]), ALU.mult).then_inc(b_onorm.sem, 1)
                        b_onorm.wait(e, i, 2 * s + half)

                def copy_ot(s):
                    b_pv.wait(e, i, TPB * (s + 1) - 1)
                    if s:
                        b_ojob.wait(e, i, 2 * s - 1)
                    e.tensor_copy(OTB, pairC[:, :]).then_inc(b_ot.sem, 1)

                b_sum.wait(e, i, 0)
                e.tensor_reduce(large[:, :], job_bank("s", 0)[0:1, 0:P], AX.X, ALU.max).then_inc(b_sumread.sem, 1)
                b_sumread.wait(e, i, 0)
                e.tensor_scalar(flag[:, :], large[:, :], (SAFE / QSCALE) ** 2, None, ALU.is_gt).then_inc(b_flag.sem, 1)
                b_flag.wait(e, i, 0)
                b_job.wait(e, i, SJ - BJ)
                pass_wait(e)
                needed = e.value_load(flag[0:1, 0:1], min_val=0, max_val=1)
                with e.If(needed > 0):
                    for n in range(UNITS):
                        s, q, r = n // (TPB * R), n // R % TPB, n % R
                        b_mscore.wait(e, i, n)
                        b = pairs[n % 2]
                        v_steps.chain(e, e.scalar_tensor_tensor(out=b[:, q * P:(q + 1) * P], in0=overT[:, :], scalar=-2.0 * SL[R * s + r],
                                                                in1=b[:, q * P:(q + 1) * P], op0=ALU.mult, op1=ALU.add))
                        at = TPB * (R * s + r) + q
                        e.tensor_reduce(MX[:, at:at + 1], b[:, :], AX.X, ALU.max).then_inc(b_mred.sem, 1)
                with e.Else():
                    e.memset(MX[:, :], 0.0).then_inc(b_mred.sem, 1)
                    e.sem_inc(b_mred.sem, UNITS - 1)
                    e.sem_inc(v_steps.sem, UNITS)
                for s in range(SLOTS):
                    for g in range(TPB):
                        for r in range(R):
                            if g == 2 and r == 2 and s:
                                normalise(s - 1)
                            n = (s * TPB + g) * R + r
                            b_score.wait(e, i, n)
                            b = ring_pair("u", n)
                            e.scalar_tensor_tensor(out=b[:, g * P:(g + 1) * P], in0=over[:, :], scalar=-2.0 * SL[R * s + r],
                                                   in1=b[:, g * P:(g + 1) * P], op0=ALU.mult, op1=ALU.add).then_inc(b_diag.sem, 1)
                        if g == 0 and s:
                            copy_ot(s - 1)
                copy_ot(SLOTS - 1)
                normalise(SLOTS - 1)
                for g in range(2):
                    b_y.wait(e, i, g)
                    b_xb.wait(e, i, 0)
                    xs = X[:, bass.ds(i * TPB + 4 * g, 4), :]
                    e.tensor_tensor(xs, job_bank("y", g).rearrange("p (t n) -> p t n", n=P), xs, ALU.add).then_inc(b_yx.sem, 1)
                    b_yx.wait(e, i, g)
            v_steps.end(BATCH)

        B_V = 8 + 7 + 6 + 2 + 16 + 8 + GROUPS * R
        b_otzero = sem("b_ot_zeroed")

        def attn_b_tensor(e):
            for g in (b_job, b_ojob, b_mscore, b_score, b_pv, b_y, b_mjob, b_sum):
                g.prime(e)
            e.wait_ge(b_otzero, 1)
            e.wait_ge(b_tables, 16 * 5)
            with e.Fori(0, BATCH) as i:
                for half in range(2):
                    b = job_free(e, i, "a", half)
                    b_norm.transposes(e, i, half, b).then_inc(b_job.sem, 1)
                b_evac.wait(e, i, 1)
                for n in range(4):
                    e.matmul(job_free(e, i, "a", SQJ + n), Wqkn[:, n // 2, :], XTB[:, (n % 2) * 512:(n % 2 + 1) * 512],
                             start=True, stop=True).then_inc(b_job.sem, 1)
                for m in range(16):
                    s, side, half = m // 4, (m // 2) % 2, m % 2
                    e.matmul(job_free(e, i, "a", QJ + m)[0:BIAS, :], (Wqb if side == 0 else Wkb)[:, s, :], XTB[:, half * 512:(half + 1) * 512],
                             start=True, stop=True).then_inc(b_job.sem, 1)
                    if m == 3:
                        for n in range(4):
                            b_evac.wait(e, i, SQJ + n)
                            e.matmul(job_free(e, i, "m", n), blkb[:, :], SQ[:, n, :], start=True, stop=True).then_inc(b_mjob.sem, 1)
                for c in range(TPB):
                    e.matmul(job_free(e, i, "a", VJ + c)[:, 0:P], XTB[:, c * P:(c + 1) * P], Wvb[:, :], start=True, stop=True).then_inc(b_job.sem, 1)
                b_bound.wait(e, i, 0)
                e.matmul(job_free(e, i, "s", 0)[0:1, 0:P], top[:, 0:1], ident[:, :], start=True, stop=True).then_inc(b_sum.sem, 1)
                b_evac.wait(e, i, VJ + TPB - 1)

                def exp_scores(s, g, r):
                    n = (s * TPB + g) * R + r
                    b = ring_free(e, i, "u", n)
                    for half in range(2):
                        lo, hi = 512 * half, 512 * (half + 1)
                        cut = min(max(g * P, lo), hi)
                        for m, a, z in ((KB, lo, cut), (KA, cut, hi)):
                            if a < z:
                                last = e.matmul(b[:, a:z], m[:, s, g * P:(g + 1) * P], Qpad[:, s, r, a:z], start=True, stop=True)
                    last.then_inc(b_score.sem, 1)

                def max_scores(s, q, r):
                    n = (s * TPB + q) * R + r
                    if n < 2:
                        b_exp.wait(e, i, n - 2)
                    else:
                        b_mred.wait(e, i, n - 2)
                    b = pairs[n % 2]
                    for half in range(2):
                        lo, hi = 512 * half, 512 * (half + 1)
                        cut = min(max((q + 1) * P, lo), hi)
                        for k, a, z in ((KA, lo, cut), (KB, cut, hi)):
                            if a < z:
                                last = e.matmul(b[:, a:z], Qpad[:, s, r, q * P:(q + 1) * P], k[:, s, a:z], start=True, stop=True)
                    last.then_inc(b_mscore.sem, 1)

                def pv(s, g, half):
                    n = s * TPB + g
                    if half == 0:
                        b_exp.wait(e, i, R * n + R - 1)
                        if g == 0:
                            b_ot.wait(e, i, s - 1)
                    for r in range(R):
                        last = e.matmul(pairC[PART * r:PART * r + D + 1, 512 * half:512 * (half + 1)], V9[:, g, R * s + r, :],
                                        EX[:, (R * n + r) % 8, 512 * half:512 * (half + 1)], start=(g == 0), stop=(g == TPB - 1))
                    if half == 1:
                        last.then_inc(b_pv.sem, 1)

                def naturals(s):
                    b_ot.wait(e, i, s)
                    pair = ring_free(e, i, "o", s)
                    for half in range(2):
                        b = pair[:, 512 * half:512 * (half + 1)]
                        for j in range(GROUP):
                            last = e.transpose(b[:, j * P:(j + 1) * P], OTB[:, (GROUP * half + j) * P:(GROUP * half + j + 1) * P], ident[:, :])
                        last.then_inc(b_ojob.sem, 1)

                for s in range(SLOTS):
                    b_qpad[s].wait(e, i, 0)
                    b_kpad[s].wait(e, i, 0)
                b_flag.wait(e, i, 0)
                pass_wait(e)
                needed = e.value_load(flag[0:1, 0:1], min_val=0, max_val=1)
                with e.If(needed > 0):
                    for n in range(UNITS):
                        max_scores(n // (TPB * R), n // R % TPB, n % R)
                with e.Else():
                    e.sem_inc(b_mscore.sem, UNITS)
                b_mred.wait(e, i, UNITS - 1)
                e.transpose(job_free(e, i, "a", SJ)[:, 0:P], MX[:, :], ident[:, :]).then_inc(b_job.sem, 1)
                b_shift.wait(e, i, 0)
                for s in range(SLOTS):
                    for g in range(TPB):
                        exp_scores(s, g, 0)
                        exp_scores(s, g, 1)
                        before = s * TPB + g - 1
                        if before >= 0:
                            pv(before // TPB, before % TPB, 0)
                        if g == 2 and s:
                            naturals(s - 1)
                        exp_scores(s, g, 2)
                        exp_scores(s, g, 3)
                        if before >= 0:
                            pv(before // TPB, before % TPB, 1)
                pv(SLOTS - 1, TPB - 1, 0)
                pv(SLOTS - 1, TPB - 1, 1)
                naturals(SLOTS - 1)
                b_vb.wait(e, i, 0)
                for half in range(2):
                    b = job_free(e, i, "a", OJ + half)
                    for j in range(GROUP):
                        last = e.transpose(b[:, j * P:(j + 1) * P], ATT[:, GROUP * half + j, :], ident[:, :])
                    last.then_inc(b_job.sem, 1)
                for g in range(2):
                    b_evac.wait(e, i, OJ + g)
                    b = job_free(e, i, "y", g)
                    for j in range(GROUP):
                        last = e.matmul(b[:, j * P:(j + 1) * P], TR[:, (GROUP * g + j) * P:(GROUP * g + j + 1) * P], Wob[:, :], start=True, stop=True)
                    last.then_inc(b_y.sem, 1)

        ff = ExitStack()
        XT = sb("XT", [P, NT * P], scope=ff)
        S = sb("S", [P, NT, P], scope=ff)
        AB = sb("AB", [P, NT, P], scope=ff)
        ACC = sb("ACC", [P, NT, P], scope=ff)
        W1 = sb("W1", [P, EXPERTS, DF], scope=ff)
        HT = sb("HT", [P, 2, FC, 512], scope=ff)
        LG = sb("LG", [P, NT, EXPERTS], scope=ff)
        WD = sb("WD", [P, NT, EXPERTS], scope=ff)
        R1 = sb("R1", [P, NT, EXPERTS], scope=ff)
        R2 = sb("R2", [P, NT, EXPERTS], scope=ff)
        C1 = sb("C1", [P, NT], scope=ff)
        C2 = sb("C2", [P, NT], scope=ff)
        C3 = sb("C3", [P, NT], scope=ff)
        C4 = sb("C4", [P, NT], scope=ff)
        ZA = sb("ZA", [P, NT], scope=ff)
        ZN = sb("ZN", [P, NT], scope=ff)
        WT = sb("WT", [EXPERTS, NT * P], scope=ff)
        ff.close()

        class Ffn:
            def __init__(self, k, begin):
                q = f"f{k}_"
                self.begin = begin
                self.norm = Norm(q, twice=True)
                self.tjob, self.tevac = Signal(sem(q + "transposed"), 2), Signal(sem(q + "xt_ready"), 2)
                self.ajob, self.aread = Signal(sem(q + "abel_done"), 4), Signal(sem(q + "abel_read"), 4)
                self.copied = Signal(sem(q + "xt_copied"), 1, 16)
                self.gelu = Signal(sem(q + "abel_ready"), 1)
                self.mixed = Signal(sem(q + "abel_mixed"), 1)
                self.zred = Signal(sem(q + "abel_reduced"), 1)
                self.w1 = sem(q + "w1_loaded")
                self.gap, self.ex = sem(q + "gap_ready"), sem(q + "gap_exp")
                self.wd = sem(q + "weights_ready")
                self.wt, self.wtc = sem(q + "weights_turned"), sem(q + "weights_copied")
                self.bb, self.bbc = sem(q + "b2_done"), sem(q + "b2_copied")
                self.hjob, self.hevac = Signal(sem(q + "hidden_done"), EXPERTS * FC), Signal(sem(q + "hidden_ready"), EXPERTS * FC)
                self.yjob, self.yread = Signal(sem(q + "expert_done"), EXPERTS), Signal(sem(q + "expert_added"), EXPERTS)
                self.z, self.gate = sem(q + "z_ready"), sem(q + "gate_ready")
                self.srest = Signal(sem(q + "s_ready"), 1)

            def sync(self, e):
                self.copied.prime(e)
                e.wait_ge(self.begin, 1)
                for x in range(EXPERTS):
                    e.dma_start(W1[:, x, :], I["w1"][:, x, :]).then_inc(self.w1, 16)
                with e.Fori(0, BATCH) as i:
                    self.tevac.wait(e, i, 1)
                    e.dma_start(XT[:, bass.ds(i * SEQ, SEQ)], XTB[:, :]).then_inc(self.copied.sem, 16)

            def gpsimd(self, e):
                self.norm.prime_gpsimd(e)
                self.mixed.prime(e)
                self.srest.prime(e)
                e.wait_ge(self.begin, 1)
                with e.Fori(0, BATCH) as i:
                    g_steps.loop(i, 4 + 2 + 1)
                    self.norm.gpsimd(e, i)
                    ts = bass.ds(i * TPB, TPB)
                    self.gelu.wait(e, i, 0)
                    g_steps.chain(e, e.tensor_tensor(S[:, ts, :], S[:, ts, :], X[:, ts, :], ALU.add))
                    e.tensor_tensor(XN[:, :, :], AB[:, ts, :], mixa[:, None, :].to_broadcast([P, TPB, P]), ALU.mult).then_inc(self.mixed.sem, 1)
                    e.tensor_tensor(S[:, ts, :], S[:, ts, :], AB[:, ts, :], ALU.add).then_inc(self.srest.sem, 1)
                g_steps.end(BATCH)

            def scalar(self, e):
                self.tevac.prime(e)
                self.gelu.prime(e)
                self.hevac.prime(e)
                e.wait_ge(self.begin, 1)
                with e.Fori(0, BATCH) as i:
                    for half in range(2):
                        self.tjob.wait(e, i, half)
                        self.copied.wait(e, i, -1)
                        self.ajob.wait(e, i, -1)
                        e.activation(XTB[:, half * 512:(half + 1) * 512], bank[half], ACT.Identity,
                                     bias=lnbT[:, 0:1], scale=lngT[:, 0:1]).then_inc(self.tevac.sem, 1)
                    self.aread.wait(e, i, 3)
                    ab = AB[:, bass.ds(i * TPB, TPB), :]
                    e.activation(ab, ab, ACT.Gelu).then_inc(self.gelu.sem, 1)
                e.wait_ge(self.gap, 1)
                e.activation(C3[:, :], C3[:, :], ACT.Exp).then_inc(self.ex, 1)
                for g in range(NG):
                    e.wait_ge(self.wt, g + 1)
                    e.activation(WT[:, g * 512:(g + 1) * 512], bank[g % 2][0:EXPERTS, :], ACT.Copy).then_inc(self.wtc, 1)
                for g in range(NG):
                    e.wait_ge(self.bb, g + 1)
                    e.activation(ACC[:, GROUP * g:GROUP * (g + 1), :].rearrange("p t n -> p (t n)"), bank[2 + g % 2], ACT.Copy).then_inc(self.bbc, 1)
                with e.Fori(0, NG) as i:
                    for x in range(EXPERTS):
                        for c in range(FC):
                            n = x * FC + c
                            self.hjob.wait(e, i, n)
                            if c == 0:
                                self.yjob.wait(e, i, x - 2)
                            e.activation(HT[:, x % 2, c, :], bank[n % 4], ACT.Gelu, bias=b1T[:, n:n + 1]).then_inc(self.hevac.sem, 1)
                e.wait_ge(self.z, 1)
                e.activation(C1[:, :], C1[:, :], ACT.Sigmoid, bias=mixb[:, 0:1]).then_inc(self.gate, 1)

            def vector(self, e):
                self.norm.prime_vector(e)
                for g in (self.aread, self.zred, self.yread):
                    g.prime(e)
                with e.Fori(0, BATCH) as i:
                    v_steps.loop(i, 8 + 7 + 6 + 8 + 4)
                    self.norm.vector(e, i, keep=S)
                    ts = bass.ds(i * TPB, TPB)
                    for j in range(4):
                        self.ajob.wait(e, i, j)
                        b = bank[2 + j % 2][:, 0:2 * (P + EXPERTS)].rearrange("p (t n) -> p t n", t=2)
                        tt = bass.ds(i * TPB + 2 * j, 2)
                        v_steps.add(e.tensor_tensor(LG[:, tt, :], b[:, :, P:P + EXPERTS], abias[:, None, P:P + EXPERTS].to_broadcast([P, 2, EXPERTS]), ALU.add))
                        e.tensor_tensor(AB[:, tt, :], b[:, :, 0:P], abias[:, None, 0:P].to_broadcast([P, 2, P]), ALU.add).then_inc(self.aread.sem, 1)
                    self.mixed.wait(e, i, 0)
                    e.tensor_reduce(ZA[:, ts], XN[:, :, :], AX.X, ALU.add).then_inc(self.zred.sem, 1)
                    self.zred.wait(e, i, 0)
                    self.srest.wait(e, i, 0)
                v_steps.end(BATCH)
                v_steps.settle(e)

                def every(c):
                    return c[:, :].unsqueeze(2).to_broadcast([P, NT, EXPERTS])

                def one_hot(of, top, hot, rank):
                    v_steps.chain(e, e.tensor_reduce(top[:, :], of[:, :, :], AX.X, ALU.max))
                    v_steps.chain(e, e.tensor_tensor(hot[:, :, :], of[:, :, :], every(top), ALU.is_equal))
                    v_steps.chain(e, e.tensor_tensor(hot[:, :, :], hot[:, :, :], rank8[:, None, :].to_broadcast([P, NT, EXPERTS]), ALU.mult))
                    v_steps.chain(e, e.tensor_reduce(rank[:, :], hot[:, :, :], AX.X, ALU.max))
                    v_steps.chain(e, e.tensor_tensor(hot[:, :, :], hot[:, :, :], every(rank), ALU.is_equal))

                one_hot(LG, C1, R1, C4)
                v_steps.chain(e, e.scalar_tensor_tensor(out=LG[:, :, :], in0=R1[:, :, :], scalar=-3.0e38, in1=LG[:, :, :], op0=ALU.mult, op1=ALU.add))
                one_hot(LG, C2, R2, C4)
                e.tensor_tensor(C3[:, :], C2[:, :], C1[:, :], ALU.subtract).then_inc(self.gap, 1)
                e.wait_ge(self.ex, 1)
                v_steps.chain(e, e.tensor_scalar(C1[:, :], C3[:, :], 1.0, None, ALU.add))
                v_steps.chain(e, e.reciprocal(C1[:, :], C1[:, :]))
                v_steps.chain(e, e.tensor_tensor(C2[:, :], C3[:, :], C1[:, :], ALU.mult))
                v_steps.chain(e, e.tensor_tensor(R1[:, :, :], R1[:, :, :], every(C1), ALU.mult))
                v_steps.chain(e, e.tensor_tensor(R2[:, :, :], R2[:, :, :], every(C2), ALU.mult))
                e.tensor_tensor(WD[:, :, :], R1[:, :, :], R2[:, :, :], ALU.add).then_inc(self.wd, 1)
                e.wait_ge(self.wd, 1)

                e.wait_ge(self.bbc, NG)
                with e.Fori(0, NG) as i:
                    v_steps.loop(i, EXPERTS * 3 + 2)
                    for x in range(EXPERTS):
                        self.yjob.wait(e, i, x)
                        for j in range(GROUP):
                            acc = ACC[:, bass.ds(i * GROUP + j, 1), :].rearrange("p a n -> p (a n)")
                            if j == 0:
                                self.yread.wait(e, i, x - 1)
                            ins = e.scalar_tensor_tensor(out=acc, in0=bank[4 + x % 2][:, j * P:(j + 1) * P],
                                                         scalar=WD[:, bass.ds(i * GROUP + j, 1), x:x + 1].rearrange("p a n -> p (a n)"), in1=acc,
                                                         op0=ALU.mult, op1=ALU.add)
                            ins.then_inc(self.yread.sem, 1) if j == GROUP - 1 else v_steps.add(ins)
                    self.yread.wait(e, i, EXPERTS - 1)
                    v_steps.settle(e)
                    gs = bass.ds(i * GROUP, GROUP)
                    v_steps.chain(e, e.tensor_tensor(XN[:, 0:GROUP, :], ACC[:, gs, :], mixn[:, None, :].to_broadcast([P, GROUP, P]), ALU.mult))
                    v_steps.add(e.tensor_reduce(ZN[:, gs], XN[:, 0:GROUP, :], AX.X, ALU.add))
                    v_steps.settle(e)
                v_steps.end(NG)
                v_steps.settle(e)
                v_steps.chain(e, e.tensor_tensor(ACC[:, :, :], ACC[:, :, :], AB[:, :, :], ALU.subtract))
                e.tensor_tensor(C1[:, :], ZA[:, :], ZN[:, :], ALU.add).then_inc(self.z, 1)
                e.wait_ge(self.gate, 1)
                for t in range(NT):
                    v_steps.add(e.scalar_tensor_tensor(out=X[:, t, :], in0=ACC[:, t, :], scalar=C1[:, t:t + 1], in1=S[:, t, :],
                                                       op0=ALU.mult, op1=ALU.add))
                v_steps.settle(e)

            def tensor(self, e):
                for g in (self.tjob, self.ajob, self.hjob, self.yjob):
                    g.prime(e)
                e.wait_ge(self.begin, 1)
                with e.Fori(0, BATCH) as i:
                    for half in range(2):
                        self.tevac.wait(e, i, half - 2)
                        self.norm.transposes(e, i, half, bank[half]).then_inc(self.tjob.sem, 1)
                    for j in range(4):
                        self.tevac.wait(e, i, j // 2)
                        self.aread.wait(e, i, j - 2)
                        for t in (2 * j, 2 * j + 1):
                            last = e.matmul(bank[2 + j % 2][:, (t % 2) * (P + EXPERTS):(t % 2 + 1) * (P + EXPERTS)], XTB[:, t * P:(t + 1) * P],
                                            Wab[:, :], start=True, stop=True)
                        last.then_inc(self.ajob.sem, 1)
                e.wait_ge(self.wd, 1)
                self.tevac.wait(e, BATCH - 1, 1)
                for g in range(NG):
                    if g >= 2:
                        e.wait_ge(self.wtc, g - 1)
                    for j in range(GROUP):
                        last = e.transpose(bank[g % 2][0:EXPERTS, j * P:(j + 1) * P], WD[:, GROUP * g + j, :], ident[:, :])
                    last.then_inc(self.wt, 1)
                for g in range(NG):
                    e.wait_ge(self.wtc, g + 1)
                    if g >= 2:
                        e.wait_ge(self.bbc, g - 1)
                    for j in range(GROUP):
                        t = GROUP * g + j
                        last = e.matmul(bank[2 + g % 2][:, j * P:(j + 1) * P], WT[:, t * P:(t + 1) * P], b2r[:, :], start=True, stop=True)
                    last.then_inc(self.bb, 1)
                e.wait_ge(self.bbc, NG)
                e.wait_ge(self.w1, 16 * EXPERTS)
                self.copied.wait(e, BATCH - 1, 0)
                with e.Fori(0, NG) as i:
                    def hidden(x):
                        for c in range(FC):
                            n = x * FC + c
                            self.hevac.wait(e, i, n - 4)
                            e.matmul(bank[n % 4], W1[:, x, c * P:(c + 1) * P], XT[:, bass.ds(i * 512, 512)], start=True, stop=True).then_inc(self.hjob.sem, 1)

                    hidden(0)
                    for x in range(EXPERTS):
                        if x + 1 < EXPERTS:
                            hidden(x + 1)
                        self.hevac.wait(e, i, x * FC + FC - 1)
                        self.yread.wait(e, i, x - 2)
                        for j in range(GROUP):
                            for c in range(FC):
                                last = e.matmul(bank[4 + x % 2][:, j * P:(j + 1) * P], HT[:, x % 2, c, j * P:(j + 1) * P], w2r[:, x * FC + c, :],
                                                start=(c == 0), stop=(c == FC - 1))
                        last.then_inc(self.yjob.sem, 1)

        def rowb(ap):
            return ap.partition_broadcast(P)

        wloads = [
            (Wqa[:, :, :], I["Wqa"]), (Wka[:, :, :], I["Wka"]), (Wnat[:, 0:2 * P], I["Wkv"]), (Wnat[:, 3 * P:4 * P], I["Wqn"]),
            (Wg1T[:, :], I["Wg1T"]), (Wg2[:, :], I["Wg2"]), (Woa[:, :], I["Woa"]), (gam[:, :], rowb(I["gam"])), (bet[:, :], rowb(I["bet"])),
            (negq[:, :], I["negq"]), (negk[:, :], I["negk"]),
            (negqb[:, :], I["negqb"]), (negkb[:, :], I["negkb"]),
            (Wqb[:, :, :], I["Wqb"]), (Wkb[:, :, :], I["Wkb"]), (Wvb[:, :], I["Wvb"]), (Wob[:, :], I["Wob"]),
            (qbias[0:BIAS, :], I["qbias"]), (kbias[0:BIAS, :], I["kbias"]), (vbias[:, :], rowb(I["vbias"])), (obias[:, :], rowb(I["obias"])),
            (lngT[:, :], I["lngT"]), (lnbT[:, :], I["lnbT"]), (Wab[:, 0:P], I["abel_w"]), (Wab[:, P:P + EXPERTS], I["gate_w"]),
            (abias[:, 0:P], rowb(I["abel_b"])), (abias[:, P:P + EXPERTS], rowb(I["gate_b"])), (b1T[:, :], I["b1T"]),
            (mixa[:, :], rowb(I["mixa"])), (mixn[:, :], rowb(I["mixn"])), (mixb[:, :], rowb(I["mixb"])), (rank8[:, :], rowb(I["rank8"])),
        ]
        N_WLOADS = len(wloads)

        def loads_sync(e):
            for a, b in ((ident[:, :], I["ident"]), (A[:, :, :], I["gens"]), (AT[:, :, :], I["gensT"]), (inv[:, :], rowb(I["inv"])),
                         (thr[:, :, :].rearrange("p a b -> p (a b)"), rowb(I["thr"]))):
                e.dma_start(a, b).then_inc(gens_loaded, 16)
            for b in range(BATCH):
                e.dma_start(X[:, b * TPB:(b + 1) * TPB, :], I["x"][b].rearrange("(t p) d -> p t d", p=P)).then_inc(x_loaded, 16)
            e.dma_start(w2T[:, :, :], I["w2T"]).then_inc(w2_loaded, 16)
            e.dma_start(b2T[:, :], I["b2T"]).then_inc(w2_loaded, 16)

        def loads_scalar(e):
            for a, b in wloads:
                e.dma_start(a, b).then_inc(w_loaded, 16)

        def tables_sync(e):
            e.wait_ge(fold_copied, EXPERTS + 1)
            for a, b in ((maskT, "maskT"), (sel, "sel"), (lamq, "lamq"), (lamk, "lamk"), (lamc, "lamc"), (blk, "blk")):
                e.dma_start(a[tuple(slice(None) for _ in a.shape)], I[b]).then_inc(a_tables, 16)

        begins = [sem(f"phase{n}_may_begin") for n in range(2)]
        ffns = [Ffn(n, begins[n]) for n in range(2)]
        x_done = sem("x_done")
        block = ctx.enter_context(nc.Block())

        @block.sync
        def _(e):
            loads_sync(e)
            tables_sync(e)
            if 1 in upto:
                attn_a_sync(e)
            if 2 in upto:
                ffns[0].sync(e)
            if 3 in upto:
                attn_b_sync(e)
            if 4 in upto:
                ffns[1].sync(e)
            e.wait_ge(x_done, 1)
            for b in range(BATCH):
                e.dma_start(out[b].rearrange("(t p) d -> p t d", p=P), X[:, b * TPB:(b + 1) * TPB, :]).then_inc(out_stored, 16)
            e.wait_ge(out_stored, 16 * BATCH)

        @block.scalar
        def _(e):
            loads_scalar(e)
            if 1 in upto:
                attn_a_scalar(e)
            if 2 in upto:
                ffns[0].scalar(e)
            if 3 in upto:
                attn_b_scalar(e)
            if 4 in upto:
                ffns[1].scalar(e)

        @block.gpsimd
        def _(e):
            expm_gpsimd(e)
            e.wait_ge(fold_copied, EXPERTS + 1)
            e.memset(Qpad[:, :, :, :].bitcast(F32), 0.0).then_inc(zeroed, 1)
            if 1 in upto:
                attn_a_gpsimd(e)
            if 2 in upto:
                ffns[0].gpsimd(e)
            if 3 in upto:
                attn_b_gpsimd(e)
            if 4 in upto:
                ffns[1].gpsimd(e)

        @block.vector
        def _(e):
            attn_a_vector(e)
            expm_vector(e)
            e.wait_ge(x_loaded, 16 * BATCH)
            if 1 in upto:
                attn_a_vector_loop(e)
            e.wait_ge(zeroed, 1)
            e.wait_ge(a_tables, 96)
            if 2 in upto:
                e.memset(rstd2[:, :], 0.0).then_inc(begins[0], 1)
                e.wait_ge(begins[0], 1)
                ffns[0].vector(e)
            if 3 in upto:
                e.memset(rstd2[:, :], 0.0).then_inc(b_begin, 1)
                e.wait_ge(b_begin, 1)
                attn_b_vector(e)
            if 4 in upto:
                e.memset(rstd2[:, :], 0.0).then_inc(begins[1], 1)
                e.wait_ge(begins[1], 1)
                ffns[1].vector(e)
            e.memset(rstd2[:, :], 0.0).then_inc(x_done, 1)

        @block.tensor
        def _(e):
            expm_tensor(e)
            if 1 in upto:
                attn_a_tensor(e)
            if 2 in upto:
                ffns[0].tensor(e)
            if 3 in upto:
                attn_b_tensor(e)
            if 4 in upto:
                ffns[1].tensor(e)


def slot_columns(w):
    t = w.reshape(w.shape[0], SLOTS, R, 1, D)
    o = np.zeros((w.shape[0], SLOTS, R, PART), np.float32)
    o[..., :ROWS] = np.broadcast_to(t, (w.shape[0], SLOTS, R, 3, D)).reshape(w.shape[0], SLOTS, R, ROWS)
    return o.reshape(w.shape[0], SLOTS, P)


def packed_columns(w):
    t = w.reshape(w.shape[0], SLOTS, R, 1, D)
    return np.broadcast_to(t, (w.shape[0], SLOTS, R, 3, D)).reshape(w.shape[0], SLOTS, BIAS)


def constants():
    c = {}
    c["ident"] = np.eye(P, dtype=np.float32)
    start = 2.0 ** (-2.0 ** (-(np.log2(H) - 3)))
    s = np.array([start * start ** i for i in range(H)], dtype=np.float32)
    s = (s * (1.0 - 0 / 11 + 1e-05)).astype(np.float32)
    idx = np.arange(P, dtype=np.float32)
    diff = idx[None, :] - idx[:, None]
    m = np.where(diff >= 0, np.exp(-s[:, None, None] * np.maximum(diff, 0)), 0).astype(np.float32)
    c["maskT"] = np.ascontiguousarray(m.transpose(1, 0, 2))
    sh = np.repeat(s, D)
    c["lamq"] = np.exp(-sh[:, None] * (idx[None, :] + 1)).astype(np.float32)
    c["lamk"] = np.exp(-sh[None, :] * (P - 1.0 - idx[:, None])).astype(np.float32)
    c["lamc"] = np.exp(-sh * P).astype(np.float32)[:, None]
    h = np.arange(P) // D
    c["blk"] = (h[:, None] == h[None, :]).astype(np.float32)
    sel = np.zeros((P, SLOTS, P), np.float32)
    for q in range(SLOTS):
        for r in range(R):
            for d in range(D):
                sel[PART * r + d, q, (R * q + r) * D + d] = 1
    c["sel"] = sel
    row = np.arange(P) % PART
    c["negq"] = -((row >= 2 * D) & (row < 3 * D)).astype(np.float32)[:, None]
    c["negk"] = -((row >= D) & (row < 2 * D)).astype(np.float32)[:, None]
    part = np.arange(P) % ROWS // D
    c["negqb"] = -(part == 2).astype(np.float32)[:, None]
    c["negkb"] = -(part == 1).astype(np.float32)[:, None]
    c["inv"] = (1.0 / np.arange(TAYLOR, 0, -1)).astype(np.float32)
    c["thr"] = np.repeat(THETA * 2.0 ** np.arange(SQUARINGS), NROT).astype(np.float32)
    c["rank8"] = np.arange(EXPERTS, 0, -1).astype(np.float32)
    sl = alibi_slopes()
    hi = (sl.view(np.uint32) & np.uint32(0xFFFFF000)).view(np.float32)
    lo = (sl - hi).astype(np.float32)
    pos = np.arange(SEQ, dtype=np.float32)
    one = np.ones(SEQ, np.float32)
    aq = np.zeros((R, AUG, SLOTS, SEQ), np.float32)
    ak = np.zeros((R, AUG, SLOTS, SEQ), np.float32)
    for q in range(SLOTS):
        for r in range(R):
            a, b = hi[R * q + r], lo[R * q + r]
            aq[r, :, q] = [-pos, a * one, -pos, b * one]
            ak[r, :, q] = [a * one, pos, b * one, pos]
    c["augq"] = aq
    ones = np.ones((1, SLOTS, SEQ), np.float32)
    c["auga"] = np.concatenate([ak.reshape(R * AUG, SLOTS, SEQ), ones])
    c["augb"] = np.concatenate([-ak.reshape(R * AUG, SLOTS, SEQ), ones])
    k = np.arange(P)
    c["over"] = np.maximum(k[:, None] - k[None, :], 0).astype(np.float32)
    c["overT"] = np.ascontiguousarray(c["over"].T)
    return c


def layouts(a):
    g = lambda n: np.asarray(a[n])
    L = {"x": g("L0_attn_a_x")}
    L["Wqa"] = slot_columns(g("L0_attn_a_Wq"))
    L["Wka"] = slot_columns(g("L0_attn_a_Wk"))
    L["Wkv"] = np.concatenate([g("L0_attn_a_Wk"), g("L0_attn_a_Wv")], axis=1)
    L["Wqn"] = g("L0_attn_a_Wq")
    L["Wg1T"] = g("L0_attn_a_Wg1").T
    L["Wg2"] = g("L0_attn_a_Wg2")
    L["Woa"] = g("L0_attn_a_Wo")
    L["gam"], L["bet"] = g("L0_attn_a_gamma"), g("L0_attn_a_beta")
    W, B = g("L0_attn_b_W_qkv"), g("L0_attn_b_b_qkv")
    L["Wqb"], L["Wkb"] = packed_columns(W[:P].T), packed_columns(W[P:2 * P].T)
    L["Wvb"] = W[2 * P:].T
    L["Wob"] = g("L0_attn_b_W_out").T
    L["Wqkn"] = W[:2 * P].reshape(2, P, P).transpose(2, 0, 1)
    L["nbias"] = B[:2 * P].reshape(2, P).T
    L["qbias"] = packed_columns(B[None, :P])[0].T
    L["kbias"] = packed_columns(B[None, P:2 * P])[0].T
    L["vbias"], L["obias"] = B[2 * P:], g("L0_attn_b_b_out")
    L["lngT"], L["lnbT"] = g("L0_ffn_ln_g")[:, None], g("L0_ffn_ln_b")[:, None]
    L["abel_w"], L["gate_w"] = g("L0_ffn_abel_w"), g("L0_ffn_gate_w_moe")
    L["abel_b"], L["gate_b"] = g("L0_ffn_abel_b"), g("L0_ffn_gate_b_moe")
    L["w1"] = g("L0_ffn_w1").transpose(1, 0, 2)
    L["b1T"] = g("L0_ffn_b1").reshape(EXPERTS * FC, P).T
    L["w2T"] = g("L0_ffn_w2").transpose(2, 0, 1)
    L["b2T"] = g("L0_ffn_b2").T
    L["gens"] = g("L0_ffn_gens").transpose(1, 0, 2)
    L["gensT"] = g("L0_ffn_gens").transpose(2, 0, 1)
    mix = g("L0_ffn_mix_w").reshape(2 * P)
    L["mixa"], L["mixn"], L["mixb"] = mix[:P], mix[P:], g("L0_ffn_mix_b")
    L.update(constants())
    return L


def kernel(**inputs):
    import numpy as _np
    import concourse.bacc as _bacc
    from concourse import mybir as _mybir
    from concourse.bass_utils import run_bass_kernel_spmd as _run

    nc = _bacc.Bacc("TRN2", target_bir_lowering=False, num_devices=1)
    arrays, args = {}, {}
    for name, a in layouts(inputs).items():
        a = _np.ascontiguousarray(a)
        arrays[f"in_{name}_dram"] = a
        args[name] = nc.dram_tensor(f"in_{name}_dram", a.shape, _mybir.dt.from_np(a.dtype), kind="ExternalInput").ap()
    out = nc.dram_tensor("out_0_dram", (BATCH, SEQ, P), _mybir.dt.from_np(_np.dtype("float32")), kind="ExternalOutput").ap()
    build(nc, args, out)
    r = _run(nc, [arrays], core_ids=[0])
    return r.results[0]["out_0_dram"]
```

```python
from contextlib import ExitStack

import numpy as np

import concourse.bass as bass
from concourse import mybir

ALU = mybir.AluOpType
ACT = mybir.ActivationFunctionType
AX = mybir.AxisListType
F32 = mybir.dt.float32
F32R = mybir.dt.float32r
I32 = mybir.dt.int32

P = 128
BATCH, SEQ = 4, 1024
H, D = 16, 8
TPB = SEQ // P
NT = BATCH * TPB
SLOTS, R = 4, 4
PART = 32
ROWS = 3 * D
BIAS = R * ROWS
AUG = 4
SHIFT = BIAS + R * AUG
EXPERTS, DF = 8, 512
FC = DF // P
GROUP = 4
TILE = 2 * P
MAXT = NT * P // TILE
NTILES = 2 * MAXT + EXPERTS - 1
DEPTH = 3
ROW = P + EXPERTS
REGION = NT * P + TILE
SPARE = (EXPERTS - 1) * TILE
T_BASE = 0
T_FULL = T_BASE + EXPERTS + 1
T_TILE = T_FULL + MAXT
T_NAME = T_TILE + NTILES
TAB = T_NAME + EXPERTS + 1
EPS = 1e-5
NROT = 3
TAYLOR = 14
THETA = 2.0
SQUARINGS = 16
QSCALE = float(D) ** -0.5
SAFE = 64.0


class Signal:

    def __init__(self, sem, per, unit=1, base=0):
        self.sem, self.per, self.unit, self.base = sem, per, unit, base

    def prime(self, eng):
        eng.sem_inc(self.sem, self.per * self.unit)

    def wait(self, eng, i, k):
        assert -self.per <= k < self.per
        eng.wait_ge(self.sem, (i + 1) * (self.per * self.unit) + ((k + 1) * self.unit + self.base))


class Mark:

    def __init__(self, sem, base):
        self.sem, self.base = sem, base

    def wait(self, eng, n):
        eng.wait_ge(self.sem, self.base + n)


class Count:

    def __init__(self, sem, unit, base):
        self.sem, self.unit, self.base = sem, unit, base

    def wait(self, eng, i):
        eng.wait_ge(self.sem, i * self.unit + (self.base + 1) * self.unit)


class Steps:

    def __init__(self, sem):
        self.sem, self.done, self.here, self.turn, self.per = sem, 0, 0, 0, 0

    def loop(self, i, per):
        self.done += self.here
        self.turn, self.per, self.here = i, per, 0

    def end(self, turns):
        assert self.here == self.per, (self.here, self.per)
        self.done += self.per * turns
        self.turn, self.per, self.here = 0, 0, 0

    def add(self, ins):
        ins.then_inc(self.sem, 1)
        self.here += 1

    def settle(self, eng):
        eng.wait_ge(self.sem, self.turn * self.per + (self.done + self.here))

    def chain(self, eng, ins):
        self.add(ins)
        self.settle(eng)


def alibi_slopes():
    return np.power(np.float32(2.0), np.float32(8.0) * np.arange(0, -H, -1, dtype=np.float32) / np.float32(H)).astype(np.float32)


def build(nc, I, out):
    SL = [float(x) for x in alibi_slopes()]
    ctx = ExitStack()
    with ctx:
        def sem(name):
            return ctx.enter_context(nc.semaphore(name))

        def sb(name, shape, dt=F32, scope=ctx):
            return scope.enter_context(nc.sbuf_tensor(name, shape, dt))

        pairJ = ctx.enter_context(nc.psum_tensor("pairJ", [P, 1024], F32))
        pairA = ctx.enter_context(nc.psum_tensor("pairA", [P, 1024], F32))
        pairB = ctx.enter_context(nc.psum_tensor("pairB", [P, 1024], F32))
        pairC = ctx.enter_context(nc.psum_tensor("pairC", [P, 1024], F32))
        bank = [pairJ[:, 0:512], pairJ[:, 512:1024], pairA[:, 0:512], pairA[:, 512:1024], pairB[:, 0:512], pairB[:, 512:1024],
                 pairC[:, 0:512], pairC[:, 512:1024]]

        X = sb("X", [P, NT, P])
        ident = sb("ident", [P, P])
        w2r = sb("w2r", [P, EXPERTS * FC, P])
        b2r = sb("b2r", [EXPERTS, P])
        routed = nc.dram_tensor("routed", [EXPERTS * REGION + SPARE, ROW], F32).ap()
        placed = nc.dram_tensor("placed", [2 * NT * P + EXPERTS * TILE + SPARE, P], F32).ap()
        XN = sb("XN", [P, TPB, P])
        XTB = sb("XTB", [P, SEQ])
        stats = sb("stats", [P, TPB, 6])
        mv = sb("mv", [P, TPB, 2])
        rstd = sb("rstd", [P, TPB])
        rstd2 = sb("rstd2", [P, TPB])
        mhalf = sb("mhalf", [P, TPB])
        Wqa = sb("Wqa", [P, SLOTS, P])
        Wka = sb("Wka", [P, SLOTS, P])
        Wnat = sb("Wnat", [P, 4 * P])
        Wg1T = sb("Wg1T", [D, P])
        Wg2 = sb("Wg2", [D, P])
        Woa = sb("Woa", [P, P])
        gam = sb("gam", [P, P])
        bet = sb("bet", [P, P])
        Wqb = sb("Wqb", [P, SLOTS, BIAS])
        Wkb = sb("Wkb", [P, SLOTS, BIAS])
        Wvb = sb("Wvb", [P, P])
        Wob = sb("Wob", [P, P])
        qbias = sb("qbias", [P, SLOTS])
        kbias = sb("kbias", [P, SLOTS])
        vbias = sb("vbias", [P, P])
        obias = sb("obias", [P, P])
        negq = sb("negq", [P, 1])
        negk = sb("negk", [P, 1])
        negqb = sb("negqb", [P, 1])
        negkb = sb("negkb", [P, 1])
        lngT = sb("lngT", [P, 1])
        lnbT = sb("lnbT", [P, 1])
        Wab = sb("Wab", [P, P + EXPERTS])
        abias = sb("abias", [P, P + EXPERTS])
        mixa = sb("mixa", [P, P])
        mixn = sb("mixn", [P, P])
        mixb = sb("mixb", [P, 1])
        rank8 = sb("rank8", [P, EXPERTS])

        v_steps = Steps(sem("vector_steps"))
        g_steps = Steps(sem("gpsimd_steps"))
        x_loaded = sem("x_loaded")
        passed = sem("waits_passed")

        def pass_wait(e):
            e.sem_inc(passed, 1)

        w_loaded = sem("weights_loaded")
        w_late = sem("later_weights_loaded")
        gens_loaded = sem("gens_loaded")
        w2_loaded = sem("w2_loaded")
        out_stored = sem("out_stored")

        A = sb("A", [P, NROT, P])
        AT = sb("AT", [P, NROT, P])
        M = sb("M", [P, NROT, P])
        MT = sb("MT", [P, NROT, P])
        rot = sb("rot", [P, P])
        rot12 = sb("rot12", [P, P])
        b2T = sb("b2T", [P, EXPERTS])
        inv = sb("inv", [P, TAYLOR])
        thr = sb("thr", [P, SQUARINGS, NROT])
        norm = sb("norm", [P, NROT])
        norms = sb("norms", [P, NROT])
        act_f = sb("act_f", [P, SQUARINGS, NROT])
        now_i = sb("now_i", [P, NROT], I32)
        act_i = sb("act_i", [P, SQUARINGS, NROT], I32)
        fac = sb("fac", [P, SQUARINGS, NROT])
        norm_row = sem("norm_row")
        norm_all = sem("norm_all")
        exp_in = sem("exp_in")
        prod_done = Signal(sem("prod_done"), 2)
        next_done = Signal(sem("next_done"), 2)
        sq_done = Signal(sem("sq_done"), 2)
        sel_done = Signal(sem("sel_done"), 2)
        rot_done = sem("rot_done")
        rot_copied = sem("rot_copied")
        fold_done = sem("fold_done")
        fold_copied = sem("fold_copied")
        gate_w_done = sem("gate_w_done")
        gate_w_copied = sem("gate_w_copied")

        def expm_vector(e):
            e.wait_ge(gens_loaded, 16 * 5)
            e.tensor_reduce(norm[:, :], A[:, :, :], AX.X, ALU.add, apply_absolute_value=True).then_inc(norm_row, 1)
            e.wait_ge(norm_all, 1)
            v_steps.chain(e, e.tensor_tensor(act_f[:, :, :], norms[:, None, :].to_broadcast([P, SQUARINGS, NROT]),
                                             thr[:, :, :], ALU.is_gt))
            v_steps.add(e.tensor_copy(act_i[:, :, :], act_f[:, :, :]))
            v_steps.chain(e, e.tensor_scalar(fac[:, :, :], act_f[:, :, :], -0.5, 1.0, ALU.mult, ALU.add))
            n = SQUARINGS // 2
            while n:
                v_steps.chain(e, e.tensor_tensor(fac[:, 0:n, :], fac[:, 0:n, :], fac[:, n:2 * n, :], ALU.mult))
                n //= 2
            for m in (A, AT):
                v_steps.chain(e, e.tensor_tensor(m[:, :, :], m[:, :, :],
                                                 fac[:, 0, :].unsqueeze(2).to_broadcast([P, NROT, P]), ALU.mult))
            for m, last in ((M, False), (MT, True)):
                ins = e.tensor_copy(m[:, :, :], ident[:, None, :].to_broadcast([P, NROT, P]))
                ins.then_inc(exp_in, 1) if last else v_steps.chain(e, ins)
            next_done.prime(e)
            sel_done.prime(e)

        EXPM_STEPS = [TAYLOR // 2, SQUARINGS // 2]

        def expm_at(part, u):
            return (u - 1) // 3 if u >= 1 and u % 3 == 1 and (u - 1) // 3 < EXPM_STEPS[part] else None

        def expm_vector_step(e, part, turn, n):
            step = turn * EXPM_STEPS[part] + n
            if part == 1:
                sel_done.wait(e, step, -1)
                v_steps.chain(e, e.tensor_copy(now_i[:, :], act_i[:, bass.ds(step, 1), :].rearrange("p a j -> p (a j)")))
            for k, m in enumerate((M, MT)):
                b = bank[k][:, 0:NROT * P].rearrange("p (j n) -> p j n", n=P)
                if part == 0:
                    prod_done.wait(e, step, 1)
                    e.scalar_tensor_tensor(out=m[:, :, :], in0=b, scalar=inv[:, bass.ds(step, 1)],
                                           in1=ident[:, None, :].to_broadcast([P, NROT, P]),
                                           op0=ALU.mult, op1=ALU.add).then_inc(next_done.sem, 1)
                else:
                    sq_done.wait(e, step, 1)
                    pass_wait(e)
                    e.copy_predicated(m[:, :, :], now_i[:, :].unsqueeze(2).to_broadcast([P, NROT, P]), b).then_inc(sel_done.sem, 1)

        def fold_scalar(e):
            for k, m in enumerate((rot12, rot)):
                e.wait_ge(rot_done, k + 1)
                e.activation(m[:, :], bank[0][:, 0:P], ACT.Copy).then_inc(rot_copied, 1)
            for q in range(EXPERTS * FC // 4):
                e.wait_ge(fold_done, q + 1)
                e.activation(w2r[:, 4 * q:4 * q + 4, :].rearrange("p c n -> p (c n)"), bank[q % 2], ACT.Copy).then_inc(fold_copied, 1)
            e.wait_ge(fold_done, EXPERTS + 1)
            e.activation(b2r[:, :], bank[0][0:EXPERTS, 0:P], ACT.Copy).then_inc(fold_copied, 1)
            e.wait_ge(fold_copied, EXPERTS + 1)

        def expm_gpsimd(e):
            g_steps.chain(e, e.memset(mhalf[:, :], -0.5))
            e.wait_ge(norm_row, 1)
            e.partition_all_reduce(norms[:, :], norm[:, :], P, bass.bass_isa.ReduceOp.max).then_inc(norm_all, 1)

        def expm_tensor(e):
            e.wait_ge(w_loaded, 16 * N_WLOADS)
            e.matmul(bank[0][:, 0:P], Wg1T[:, :], Wg2[:, :], start=True, stop=True).then_inc(gate_w_done, 1)
            e.wait_ge(gate_w_copied, 1)
            e.wait_ge(exp_in, 1)
            prod_done.prime(e)
            sq_done.prime(e)

        def expm_tensor_step(e, part, turn, n):
            step = turn * EXPM_STEPS[part] + n
            (next_done, sel_done)[part].wait(e, step, -1)
            done, sides = ((prod_done, [(AT, M), (A, MT)]), (sq_done, [(MT, M), (M, MT)]))[part]
            for k, (left, right) in enumerate(sides):
                for x in range(NROT):
                    last = e.matmul(bank[k][:, x * P:(x + 1) * P], left[:, x, :], right[:, x, :], start=True, stop=True)
                last.then_inc(done.sem, 1)

        def fold_tensor(e):
            e.matmul(bank[0][:, 0:P], MT[:, 1, :], M[:, 2, :], start=True, stop=True).then_inc(rot_done, 1)
            e.wait_ge(rot_copied, 1)
            e.matmul(bank[0][:, 0:P], MT[:, 0, :], rot12[:, :], start=True, stop=True).then_inc(rot_done, 1)
            e.wait_ge(rot_copied, 2)
            e.wait_ge(w2_loaded, 32)
            for q in range(EXPERTS):
                if q >= 2:
                    e.wait_ge(fold_copied, q - 1)
                for c in range(FC):
                    last = e.matmul(bank[q % 2][:, c * P:(c + 1) * P], w2r[:, q * FC + c, :], rot[:, :], start=True, stop=True)
                last.then_inc(fold_done, 1)
            e.wait_ge(fold_copied, EXPERTS)
            e.matmul(bank[0][0:EXPERTS, 0:P], b2T[:, :], rot[:, :], start=True, stop=True).then_inc(fold_done, 1)

        def inverse_root(e, out, var):
            pass_wait(e)
            g_steps.chain(e, e.tensor_scalar(out, var, EPS, None, ALU.add))
            return e.tensor_tensor(out, out, mhalf[:, 0:out.shape[1]], ALU.pow)

        class Norm:

            def __init__(self, name):
                self.stats_ready = Signal(sem(name + "_stats_ready"), 1)
                self.rstd_ready = Signal(sem(name + "_rstd_ready"), 1)
                self.xn_ready = Signal(sem(name + "_xn_ready"), 2)

            def prime_vector(self, e):
                self.stats_ready.prime(e)
                self.xn_ready.prime(e)

            def prime_gpsimd(self, e):
                self.rstd_ready.prime(e)

            def x_tile(self, i, t):
                return X[:, bass.ds(i * TPB + t, 1), :].rearrange("p a d -> p (a d)")

            def tile_statistics(self, e, i, t):
                v_steps.add(e.bn_stats(stats[:, t, :], self.x_tile(i, t)))

            def turn_variances(self, e):
                v_steps.settle(e)
                pass_wait(e)
                for t in range(TPB):
                    ins = e.bn_aggr(mv[:, t, :], stats[:, t, :])
                    ins.then_inc(self.stats_ready.sem, 1) if t == TPB - 1 else v_steps.add(ins)

            def normalise_tile(self, e, i, t):
                if t == 0:
                    self.rstd_ready.wait(e, i, 0)
                ins = e.tensor_scalar(XN[:, t, :], self.x_tile(i, t), mv[:, t, 0:1], rstd[:, t:t + 1], ALU.subtract, ALU.mult)
                ins.then_inc(self.xn_ready.sem, 1) if t % GROUP == GROUP - 1 else v_steps.add(ins)

            def vector(self, e, i):
                for t in range(TPB):
                    self.tile_statistics(e, i, t)
                self.turn_variances(e)
                for t in range(TPB):
                    self.normalise_tile(e, i, t)

            def gpsimd(self, e, i):
                self.stats_ready.wait(e, i, 0)
                inverse_root(e, rstd[:, :], mv[:, :, 1]).then_inc(self.rstd_ready.sem, 1)

            def transposes(self, e, i, half, to):
                self.xn_ready.wait(e, i, half)
                for j in range(GROUP):
                    last = e.transpose(to[:, j * P:(j + 1) * P], XN[:, GROUP * half + j, :], ident[:, :])
                return last

        att = ExitStack()
        Qpad = sb("Qpad", [P, SLOTS, R, SEQ], F32R, att)
        KA = sb("KA", [P, SLOTS, SEQ], F32R, att)
        T = sb("T", [P, 2, 512], scope=att)
        TH = sb("TH", [P, 2, 512], F32R, att)
        V9 = sb("V9", [P, TPB, H, D + 1], scope=att)
        TR = XTB

        zeroed = sem("zeroed")

        aa = ExitStack()
        QST = sb("QST", [P, 2, SEQ], F32R, aa)
        maskT = sb("maskT", [P, H, P], scope=aa)
        sel = sb("sel", [P, SLOTS, P], scope=aa)
        lamq = sb("lamq", [P, P], scope=aa)
        lamk = sb("lamk", [P, P], scope=aa)
        lamc = sb("lamc", [P, 1], scope=aa)
        blk = sb("blk", [P, P], scope=aa)
        KN = sb("KN", [P, TPB, P], scope=aa)
        GT = sb("GT", [P, TPB, P], scope=aa)
        GB = sb("GB", [P, TPB, P], scope=aa)
        QL = sb("QL", [P, TPB, P], scope=aa)
        PA = sb("PA", [P, 3, 512], scope=aa)
        OTS = sb("OTS", [P, 2, 512], scope=aa)
        KV = sb("KV", [P, 2, P], scope=aa)
        KVN = sb("KVN", [P, P], scope=aa)
        ONS = sb("ONS", [P, GROUP, P], scope=aa)
        aa.close()
        ab = ExitStack()
        KB = sb("KB", [P, SLOTS, SEQ], F32R, ab)
        EX = sb("EX", [P, 8, SEQ], scope=ab)
        over = AT[:, 0, :]
        overT = AT[:, 1, :]
        OTB = T[:, :, :].rearrange("p a n -> p (a n)")
        MX = sb("MX", [P, H * TPB], scope=ab)
        MXT = sb("MXT", [P, P], F32R, ab)
        Wqkn = A[:, 0:2, :]
        nbias = sb("nbias", [P, 2], scope=ab)
        top = sb("top", [P, 4], scope=ab)
        bound = sb("bound", [P, 2], scope=ab)
        blkb = A[:, 2, :]
        large = sb("large", [1, 1], scope=ab)
        flag = sb("flag", [1, 1], I32, ab)
        DEN = sb("DEN", [P, GROUP, R], scope=ab)
        ATT = XTB[:, :].rearrange("p (t n) -> p t n", n=P)
        TRB = EX[:, 0, :]
        qbs = sb("qbs", [P, SLOTS], scope=ab)
        ab.close()
        att.close()

        AJ = 30
        a_norm = Norm("a")
        a_job = Signal(sem("a_job_done"), AJ)
        a_evac = Signal(sem("a_job_evacuated"), AJ)
        a_split = Signal(sem("a_split_done"), 16)
        a_qpad = [Signal(sem(f"a_q_padded{s}"), 1, 16 * R) for s in range(SLOTS)]
        a_score = Signal(sem("a_scores_done"), 4 * TPB)
        a_masked = Signal(sem("a_masked"), 4 * TPB)
        a_pv = Signal(sem("a_pv_done"), 4 * TPB)
        a_ot = Signal(sem("a_ot_evacuated"), TPB)
        a_on = Signal(sem("a_o_natural"), TPB)
        a_onorm = Signal(sem("a_o_normed"), 2)
        a_ostat = Signal(sem("a_o_stats"), 2)
        a_orstd = Signal(sem("a_o_rstd"), 2)
        a_y = Signal(sem("a_y_ready"), 2)
        a_aux = Signal(sem("a_aux_done"), TPB - 1 + 2)
        a_auxr = Signal(sem("a_aux_read"), TPB - 1 + 2)
        a_kv = Signal(sem("a_state_ready"), TPB - 1)
        a_pool = Signal(sem("a_decayed"), 3)
        a_gate = Signal(sem("a_gate_ready"), 1)
        a_tables = sem("a_tables_loaded")
        ot_zero = sem("ot_zeroed")

        U7 = TPB - 1
        LAST = 4 * TPB + 8

        def aux_index(kind, n):
            order = [("kv", 0), ("kv", 1), ("kv", 2), ("kv", 3), ("kv", 4), ("kv", 5), ("kv", 6), ("y", 0), ("y", 1)]
            return order.index((kind, n))

        def a_steps(u):
            return {
                "score": u if u < 32 else None,
                "pv": u - 2 if 2 <= u <= 33 else None,
                "kv": (u - 2) // 4 if u % 4 == 2 and (u - 2) // 4 < U7 else None,
                "sel": (u - 7) // 4 if u >= 7 and u % 4 == 3 and (u - 7) // 4 < TPB else None,
                "ot": (u - 6) // 4 if u >= 6 and u % 4 == 2 and (u - 6) // 4 < TPB else None,
                "norm": {20: 0, 36: 1}.get(u),
                "turn": {24: 0, 37: 1}.get(u),
                "y": {27: 0, 38: 1}.get(u),
            }

        def attn_a_sync(e):
            for s in a_qpad:
                s.prime(e)
            e.wait_ge(zeroed, 1)
            with e.Fori(0, BATCH) as i:
                for s in range(SLOTS):
                    a_split.wait(e, i, 4 * s + 1)
                    pass_wait(e)
                    a_masked.wait(e, i, -1)
                    for r in range(R):
                        e.dma_start(Qpad[PART * r:PART * r + ROWS, s, r, :].bitcast(F32),
                                    QST[PART * r:PART * r + ROWS, s % 2, :].bitcast(F32)).then_inc(a_qpad[s].sem, 16)

        def attn_a_gpsimd(e):
            a_norm.prime_gpsimd(e)
            a_pool.prime(e)
            a_orstd.prime(e)
            a_y.prime(e)
            e.wait_ge(a_tables, 16 * 6)
            e.wait_ge(w_loaded, 16 * N_WLOADS)
            a_norm.gpsimd(e, 0)
            with e.Fori(0, BATCH - 1) as i:
                g_steps.loop(i, 7)
                attn_a_gpsimd_turn(e, i, True)
            g_steps.end(BATCH - 1)
            attn_a_gpsimd_turn(e, BATCH - 1, False)

        def attn_a_gpsimd_turn(e, i, more):
            a_evac.wait(e, i, 2 + 16 + 7)
            def rows(t):
                return t[:, None, :].to_broadcast([P, TPB, P])
            e.tensor_tensor(KN[:, :, :], KN[:, :, :], rows(lamk), ALU.mult).then_inc(a_pool.sem, 1)
            a_evac.wait(e, i, 2 + 16 + 8 + 1)
            e.tensor_tensor(QL[:, :, :], QL[:, :, :], rows(lamq), ALU.mult).then_inc(a_pool.sem, 1)
            a_gate.wait(e, i, 0)
            pass_wait(e)
            g_steps.chain(e, e.tensor_scalar(GT[:, :, :], GT[:, :, :], 0.5, 0.5, ALU.mult, ALU.add))
            g_steps.chain(e, e.tensor_tensor(GB[:, :, :], GT[:, :, :], rows(bet), ALU.mult))
            e.tensor_tensor(GT[:, :, :], GT[:, :, :], rows(gam), ALU.mult).then_inc(a_pool.sem, 1)
            for g in range(2):
                if g == 1 and more:
                    a_norm.gpsimd(e, i + 1)
                a_ostat.wait(e, i, g)
                inverse_root(e, rstd2[:, 4 * g:4 * g + 4], mv[:, 4 * g:4 * g + 4, 1]).then_inc(a_orstd.sem, 1)
                a_onorm.wait(e, i, g)
                a_pool.wait(e, i, 2)
                g_steps.chain(e, e.tensor_tensor(ONS[:, :, :], ONS[:, :, :], GT[:, 4 * g:4 * g + 4, :], ALU.mult))
                e.tensor_tensor(ONS[:, :, :], ONS[:, :, :], GB[:, 4 * g:4 * g + 4, :], ALU.add).then_inc(a_y.sem, 1)

        def attn_a_scalar(e):
            a_evac.prime(e)
            a_ot.prime(e)
            a_gate.prime(e)
            with e.Fori(0, BATCH) as i:
                def job(n):
                    a_job.wait(e, i, n)
                    return bank[n % 2]
                for half in range(2):
                    e.activation(XTB[:, half * 512:(half + 1) * 512], job(half), ACT.Copy).then_inc(a_evac.sem, 1)
                for m in range(16):
                    a_split.wait(e, i, m - 2)
                    if m // 2 % 2:
                        e.activation(TH[:, m % 2, :], job(2 + m), ACT.Silu)
                    e.activation(T[:, m % 2, :], job(2 + m), ACT.Silu).then_inc(a_evac.sem, 1)
                for c in range(TPB):
                    b = job(18 + c)
                    e.activation(KN[:, c, :], b[:, 0:P], ACT.Silu)
                    e.activation(V9[:, c, :, 0:D], b[:, P:2 * P].rearrange("p (h d) -> p h d", d=D), ACT.Silu)
                    if c == 0:
                        a_y.wait(e, i, -1)
                    e.activation(GT[:, c, :], b[:, 2 * P:3 * P], ACT.Copy).then_inc(a_evac.sem, 1)
                for half in range(2):
                    e.activation(QL[:, 4 * half:4 * half + 4, :].rearrange("p c n -> p (c n)"), job(26 + half), ACT.Silu).then_inc(a_evac.sem, 1)
                a_evac.wait(e, i, 25)
                e.activation(GT[:, :, :], GT[:, :, :], ACT.Tanh, scale=0.5).then_inc(a_gate.sem, 1)
                for u in range(LAST):
                    w = a_steps(u)
                    if w["ot"] is not None:
                        c = w["ot"]
                        a_pv.wait(e, i, 4 * c + 3)
                        a_on.wait(e, i, c - 2)
                        e.activation(OTS[:, c % 2, :], bank[4 + c % 2], ACT.Copy).then_inc(a_ot.sem, 1)
                    if w["turn"] is not None:
                        g = w["turn"]
                        e.activation(TR[:, g * 512:(g + 1) * 512], job(28 + g), ACT.Copy).then_inc(a_evac.sem, 1)

        def attn_a_vector(e):
            a_norm.prime_vector(e)
            for s in (a_split, a_masked, a_onorm, a_ostat, a_auxr, a_kv):
                s.prime(e)

        def attn_a_vector_loop(e):
            e.wait_ge(gate_w_done, 1)
            e.tensor_copy(Wnat[:, 2 * P:3 * P], bank[0][:, 0:P]).then_inc(gate_w_copied, 1)
            e.memset(bank[4], 0.0).then_inc(ot_zero, 1)
            e.memset(bank[5], 0.0).then_inc(ot_zero, 1)
            e.wait_ge(a_tables, 16 * 6)
            a_norm.vector(e, 0)
            with e.Fori(0, BATCH // 2) as turn:
                v_steps.loop(turn, A_V)
                attn_a_vector_turn(e, 0, turn, turn, True)
            v_steps.end(BATCH // 2)
            for turn in range(BATCH // 2):
                attn_a_vector_turn(e, 1, turn, turn + BATCH // 2, turn == 0)

        def attn_a_vector_turn(e, part, turn, i, more):
            for m in range(16):
                s, side, half = m // 4, (m // 2) % 2, m % 2
                a_evac.wait(e, i, 2 + m)
                if side == 0 and half == 0:
                    a_qpad[s - 2].wait(e, i, 0 if s >= 2 else -1)
                if side == 0:
                    v_steps.chain(e, e.tensor_copy(TH[:, m % 2, :], T[:, m % 2, :]))
                to = (QST[:, s % 2, half * 512:(half + 1) * 512] if side == 0 else KA[:, s, half * 512:(half + 1) * 512])
                e.scalar_tensor_tensor(out=to, in0=TH[:, m % 2, :].bitcast(F32), scalar=(negq if side == 0 else negk)[:, 0:1],
                                       in1=T[:, m % 2, :], op0=ALU.mult, op1=ALU.add).then_inc(a_split.sem, 1)
            for u in range(LAST):
                w = a_steps(u)
                if more and 24 <= u < 24 + TPB:
                    a_norm.tile_statistics(e, i + 1, u - 24)
                if more and u == 32:
                    a_norm.turn_variances(e)
                if more and u == 34:
                    for t in range(TPB):
                        a_norm.normalise_tile(e, i + 1, t)
                if expm_at(part, u - 1) is not None:
                    expm_vector_step(e, part, turn, expm_at(part, u - 1))
                if w["score"] is not None:
                    s = u % 4
                    a_score.wait(e, i, u)
                    a_pv.wait(e, i, u - 3 if u >= 3 else -1)
                    e.tensor_tensor(PA[:, u % 3, :], bank[2 + u % 2], maskT[:, 4 * s:4 * s + 4, :].rearrange("p h n -> p (h n)"),
                                    ALU.mult).then_inc(a_masked.sem, 1)
                if w["kv"] is not None:
                    c = w["kv"]
                    a_aux.wait(e, i, aux_index("kv", c))
                    e.tensor_tensor(KVN[:, :], bank[7][:, 0:P], blk[:, :], ALU.mult).then_inc(a_auxr.sem, 1)
                    a_auxr.wait(e, i, aux_index("kv", c))
                    to = KV[:, (c + 1) % 2, :]
                    if c == 0:
                        a_on.wait(e, i, -1)
                        e.tensor_copy(to, KVN[:, :]).then_inc(a_kv.sem, 1)
                    else:
                        a_on.wait(e, i, c - 1)
                        a_kv.wait(e, i, c - 1)
                        e.scalar_tensor_tensor(out=to, in0=KV[:, c % 2, :], scalar=lamc[:, 0:1], in1=KVN[:, :],
                                               op0=ALU.mult, op1=ALU.add).then_inc(a_kv.sem, 1)
                if w["norm"] is not None:
                    g = w["norm"]
                    a_on.wait(e, i, 4 * g + 3)
                    for j in range(4):
                        v_steps.add(e.bn_stats(stats[:, 4 * g + j, :], bank[6][:, j * P:(j + 1) * P]))
                    v_steps.settle(e)
                    pass_wait(e)
                    for j in range(4):
                        ins = e.bn_aggr(mv[:, 4 * g + j, :], stats[:, 4 * g + j, :])
                        ins.then_inc(a_ostat.sem, 1) if j == 3 else v_steps.add(ins)
                    a_orstd.wait(e, i, g)
                    if g == 1:
                        a_job.wait(e, i, 28)
                    else:
                        a_job.wait(e, i, -1)
                    for j in range(4):
                        ins = e.tensor_scalar(ONS[:, j, :], bank[6][:, j * P:(j + 1) * P], mv[:, 4 * g + j, 0:1],
                                              rstd2[:, 4 * g + j:4 * g + j + 1], ALU.subtract, ALU.mult)
                        ins.then_inc(a_onorm.sem, 1) if j == 3 else v_steps.add(ins)
                if w["y"] is not None:
                    g = w["y"]
                    a_aux.wait(e, i, aux_index("y", g))
                    xs = X[:, bass.ds(i * TPB + 4 * g, 4), :]
                    e.tensor_tensor(xs, bank[7].rearrange("p (t n) -> p t n", n=P), xs, ALU.add).then_inc(a_auxr.sem, 1)
                    a_auxr.wait(e, i, aux_index("y", g))

        A_V = 8 + 7 + 6 + 8 + 2 * (4 + 3 + 3)

        def attn_a_tensor(e):
            for s in (a_job, a_score, a_pv, a_on, a_aux):
                s.prime(e)
            e.wait_ge(ot_zero, 2)
            for part in range(2):
                with e.Fori(0, BATCH // 2) as turn:
                    i = turn + part * (BATCH // 2)
                    def job(n):
                        a_evac.wait(e, i, n - 2)
                        return bank[n % 2]
                    for half in range(2):
                        b = job(half)
                        a_norm.transposes(e, i, half, b).then_inc(a_job.sem, 1)
                    a_evac.wait(e, i, 1)
                    for m in range(16):
                        s, side, half = m // 4, (m // 2) % 2, m % 2
                        e.matmul(job(2 + m), (Wqa if side == 0 else Wka)[:, s, :], XTB[:, half * 512:(half + 1) * 512],
                                 start=True, stop=True).then_inc(a_job.sem, 1)
                    for c in range(TPB):
                        e.matmul(job(18 + c)[:, 0:3 * P], XTB[:, c * P:(c + 1) * P], Wnat[:, 0:3 * P], start=True, stop=True).then_inc(a_job.sem, 1)
                    for half in range(2):
                        e.matmul(job(26 + half), Wnat[:, 3 * P:4 * P], XTB[:, half * 512:(half + 1) * 512], start=True, stop=True).then_inc(a_job.sem, 1)
                    a_evac.wait(e, i, 2 + 16 + 7)
                    for u in range(LAST):
                        w = a_steps(u)
                        if expm_at(part, u) is not None:
                            if u == 1:
                                a_evac.wait(e, i, 27)
                            expm_tensor_step(e, part, turn, expm_at(part, u))
                        if w["score"] is not None:
                            c, s = u // 4, u % 4
                            if c == 0:
                                a_split.wait(e, i, 4 * s + 3)
                                a_qpad[s].wait(e, i, 0)
                            a_masked.wait(e, i, u - 2)
                            e.matmul(bank[2 + u % 2].rearrange("p (r n) -> p r n", r=R), KA[:, s, c * P:(c + 1) * P],
                                     Qpad[:, s, :, c * P:(c + 1) * P], start=True, stop=True).then_inc(a_score.sem, 1)
                        if w["pv"] is not None:
                            v = w["pv"]
                            c, s = v // 4, v % 4
                            a_masked.wait(e, i, v)
                            if s == 0:
                                a_ot.wait(e, i, c - 2)
                            for r in range(R):
                                last = e.matmul(bank[4 + c % 2][PART * r:PART * r + D, s * P:(s + 1) * P], V9[:, c, 4 * s + r, 0:D],
                                                PA[:, v % 3, r * P:(r + 1) * P], start=True, stop=True)
                            last.then_inc(a_pv.sem, 1)
                        if w["kv"] is not None:
                            c = w["kv"]
                            a_auxr.wait(e, i, aux_index("kv", c) - 1)
                            a_pool.wait(e, i, 0)
                            e.matmul(bank[7][:, 0:P].rearrange("p (h d) -> p h d", d=D), KN[:, c, :], V9[:, c, :, 0:D],
                                     start=True, stop=True).then_inc(a_aux.sem, 1)
                        if w["sel"] is not None:
                            c = w["sel"]
                            a_ot.wait(e, i, c)
                            if c % 4 == 0:
                                a_onorm.wait(e, i, c // 4 - 1)
                            to = bank[6][:, (c % 4) * P:(c % 4 + 1) * P]
                            for s in range(SLOTS):
                                last = e.matmul(to, OTS[:, c % 2, s * P:(s + 1) * P], sel[:, s, :], start=(s == 0), stop=(s == 3 and c == 0))
                            if c:
                                a_kv.wait(e, i, c - 1)
                                a_pool.wait(e, i, 1)
                                last = e.matmul(to, QL[:, c, :], KV[:, c % 2, :], start=False, stop=True)
                            last.then_inc(a_on.sem, 1)
                        if w["turn"] is not None:
                            g = w["turn"]
                            if g == 0:
                                (next_done, sel_done)[part].wait(e, turn * EXPM_STEPS[part] + (EXPM_STEPS[part] - 1), 1)
                            b = job(28 + g)
                            a_y.wait(e, i, g)
                            for j in range(4):
                                last = e.transpose(b[:, j * P:(j + 1) * P], ONS[:, j, :], ident[:, :])
                            last.then_inc(a_job.sem, 1)
                        if w["y"] is not None:
                            g = w["y"]
                            a_evac.wait(e, i, 28 + g)
                            a_auxr.wait(e, i, aux_index("y", g) - 1)
                            for j in range(4):
                                last = e.matmul(bank[7][:, j * P:(j + 1) * P], TR[:, (4 * g + j) * P:(4 * g + j + 1) * P], Woa[:, :], start=True, stop=True)
                            last.then_inc(a_aux.sem, 1)

        BJ = 28
        DJ = 2 * SLOTS
        GROUPS = SLOTS * TPB
        UNITS = GROUPS * R
        b_norm = Norm("b")
        b_job = Signal(sem("b_job_done"), BJ)
        b_evac = Signal(sem("b_job_evacuated"), BJ)
        b_ojob = Signal(sem("b_o_natural"), DJ)
        b_onorm = Signal(sem("b_o_normalised"), DJ)
        b_split = Signal(sem("b_split_done"), 16)
        b_qpad = [Signal(sem(f"b_q_padded{s}"), 1, 16 * (R + (s == 0))) for s in range(SLOTS)]
        b_kpad = [Signal(sem(f"b_k_copied{s}"), 1, 16) for s in range(SLOTS)]
        b_mscore = Signal(sem("b_max_scores_done"), GROUPS * R)
        b_mred = Signal(sem("b_max_reduced"), GROUPS * R)
        b_shift = Signal(sem("b_shift_stored"), 1, 16)
        b_mjob = Signal(sem("b_natural_done"), 4)
        b_mread = Signal(sem("b_natural_read"), 4)
        b_bound = Signal(sem("b_bound_ready"), 1)
        b_sum = Signal(sem("b_bound_summed"), 1)
        b_sumread = Signal(sem("b_bound_read"), 1)
        b_flag = Signal(sem("b_flag_ready"), 1)
        b_score = Signal(sem("b_scores_done"), UNITS)
        b_diag = Signal(sem("b_diagonal_done"), UNITS)
        b_exp = Signal(sem("b_exponentials_done"), UNITS)
        b_pv = Signal(sem("b_pv_done"), GROUPS)
        b_ot = Signal(sem("b_ot_copied"), SLOTS)
        b_vjob = Signal(sem("b_v_done"), TPB)
        b_vread = Signal(sem("b_v_ready"), TPB)
        b_xb = Signal(sem("b_out_bias_added"), 1)
        b_yx = Signal(sem("b_y_added"), 2)
        b_y = Signal(sem("b_y_done"), 2)
        b_tables = sem("b_tables_loaded")
        b_rows = sem("b_rows_loaded")
        b_cleared = sem("b_cleared")
        b_begin = sem("b_may_begin")
        b_ones = sem("b_k_cleared_and_ones_set")

        QSTB = EX[:, 0:2, :]
        pairs = [pairA, pairB]

        def attn_b_sync(e):
            for s in b_qpad + b_kpad + [b_shift]:
                s.prime(e)
            e.wait_ge(b_begin, 1)
            for a, b in ((over, "over"), (overT, "overT"), (blkb, "blk"), (nbias, "nbias")):
                e.dma_start(a[:, :], I[b]).then_inc(b_tables, 16)
            e.dma_start(Wqkn[:, :, :], I["Wqkn"]).then_inc(b_tables, 16)
            e.wait_ge(b_rows, 16 * (R + 2))
            with e.Fori(0, BATCH) as i:
                for s in range(SLOTS):
                    b_split.wait(e, i, 4 * s + 1)
                    pass_wait(e)
                    b_score.wait(e, i, -1)
                    if s == 0:
                        e.dma_start(Qpad[SHIFT:SHIFT + 1, :, :, :].bitcast(F32), Qpad[SHIFT + 1:SHIFT + 2, :, :, :].bitcast(F32)).then_inc(b_qpad[0].sem, 16)
                    for r in range(R):
                        e.dma_start(Qpad[ROWS * r:ROWS * (r + 1), s, r, :].bitcast(F32),
                                    QSTB[ROWS * r:ROWS * (r + 1), s % 2, :]).then_inc(b_qpad[s].sem, 16)
                    b_split.wait(e, i, 4 * s + 3)
                    e.dma_start(KB[0:BIAS, s, :].bitcast(F32), KA[0:BIAS, s, :].bitcast(F32)).then_inc(b_kpad[s].sem, 16)
                b_evac.wait(e, i, SJ)
                e.dma_start(Qpad[SHIFT:SHIFT + 1, :, :, :].bitcast(F32).rearrange("a s r (t n) -> a (s r t) n", n=P),
                            MXT[:, :].bitcast(F32)).then_inc(b_shift.sem, 16)

        SQ = EX[:, 4:6, :].rearrange("p a (h n) -> p (a h) n", h=2)
        LATE = 12
        SJ = 22
        OJ = 23
        BJ = 25
        for g in (b_job, b_evac):
            g.per = BJ

        JBANKS = 5

        def QJ(m):
            return 2 + m + (4 if m >= LATE else 0)

        def SQJ(n):
            return 2 + LATE + n

        def job_order():
            order = [("a", n) for n in (0, 1)] + [("a", QJ(m)) for m in range(LATE)] + [("a", SQJ(n)) for n in range(4)]
            order += [("a", QJ(m)) for m in range(LATE, 16)] + [("m", n) for n in range(4)] + [("v", n) for n in range(TPB)]
            order += [("s", 0), ("a", SJ)]
            order += [("a", OJ), ("a", OJ + 1)]
            order += [("y", 0), ("y", 1)]
            assert len(order) % JBANKS == 0
            return order

        ORDER = job_order()
        READ_BY = {"a": b_evac, "y": b_yx, "m": b_mread, "s": b_sumread, "v": b_vread}

        def job_bank(kind, n):
            return bank[ORDER.index((kind, n)) % JBANKS]

        def job_free(e, i, kind, n):
            at = ORDER.index((kind, n))
            k, m = ORDER[at - JBANKS]
            g = READ_BY[k]
            g.wait(e, i, m if at >= JBANKS else m - g.per)
            return bank[at % JBANKS]

        def ring_order():
            order = []
            for s in range(SLOTS):
                for g in range(TPB):
                    order += [("u", (s * TPB + g) * R), ("u", (s * TPB + g) * R + 1)]
                    if s and g == 2:
                        order.append(("o", s - 1))
                    order += [("u", (s * TPB + g) * R + 2), ("u", (s * TPB + g) * R + 3)]
            return order + [("o", SLOTS - 1)]

        RING = ring_order()
        pairs3 = [pairA, pairB, pairJ]

        def ring_pair(kind, n):
            return pairs3[RING.index((kind, n)) % 3]

        def ring_free(e, i, kind, n):
            at = RING.index((kind, n))
            if at == 2:
                b_evac.wait(e, i, SJ)
                b_sumread.wait(e, i, 0)
            elif at > 2:
                k, m = RING[at - 3]
                if k == "u":
                    b_exp.wait(e, i, m)
                else:
                    b_onorm.wait(e, i, 2 * m + 1)
            else:
                b_exp.wait(e, i, at - 2)
            return pairs3[at % 3]

        def attn_b_gpsimd(e):
            b_norm.prime_gpsimd(e)
            b_xb.prime(e)
            e.wait_ge(b_begin, 1)
            b_norm.gpsimd(e, 0)
            e.memset(Qpad[:, :, :, :].bitcast(F32), 0.0).then_inc(b_cleared, 1)
            e.wait_ge(b_cleared, 1)
            e.wait_ge(b_ones, 3)
            for r in range(R):
                e.dma_start(Qpad[BIAS + AUG * r:BIAS + AUG * (r + 1), :, r, :], I["augq"][r]).then_inc(b_rows, 16)
            e.dma_start(KA[BIAS:SHIFT + 1, :, :], I["auga"]).then_inc(b_rows, 16)
            e.dma_start(KB[BIAS:SHIFT + 1, :, :], I["augb"]).then_inc(b_rows, 16)
            def bias(i):
                b_norm.xn_ready.wait(e, i, 1)
                xs = X[:, bass.ds(i * TPB, TPB), :]
                e.tensor_tensor(xs, xs, obias[:, None, :].to_broadcast([P, TPB, P]), ALU.add).then_inc(b_xb.sem, 1)
            with e.Fori(0, BATCH - 1) as i:
                g_steps.loop(i, 1)
                bias(i)
                b_norm.gpsimd(e, i + 1)
            g_steps.end(BATCH - 1)
            bias(BATCH - 1)

        def attn_b_scalar(e):
            b_evac.prime(e)
            b_exp.prime(e)
            e.wait_ge(qb_ready, 1)
            e.wait_ge(b_tables, 16 * 5)
            with e.Fori(0, BATCH) as i:
                def job(n):
                    b_job.wait(e, i, n)
                    return job_bank("a", n)
                for half in range(2):
                    e.activation(XTB[:, half * 512:(half + 1) * 512], job(half), ACT.Copy).then_inc(b_evac.sem, 1)
                for m in range(16):
                    s, side = m // 4, (m // 2) % 2
                    if m == LATE:
                        b_pv.wait(e, i, -1)
                        for n in range(4):
                            e.activation(SQ[:, n, :], job(SQJ(n)), ACT.Square, bias=nbias[:, n // 2:n // 2 + 1]).then_inc(b_evac.sem, 1)
                    b_split.wait(e, i, m - 2)
                    if side:
                        e.activation(TH[0:BIAS, m % 2, :], job(QJ(m))[0:BIAS, :], ACT.Identity, bias=kbias[0:BIAS, s:s + 1])
                    e.activation(T[0:BIAS, m % 2, :], job(QJ(m))[0:BIAS, :], ACT.Identity, bias=(qbs if side == 0 else kbias)[0:BIAS, s:s + 1],
                                 scale=(QSCALE if side == 0 else 1.0)).then_inc(b_evac.sem, 1)
                for g in b_qpad + b_kpad:
                    g.wait(e, i, 0)
                b = job(SJ)
                b_shift.wait(e, i, -1)
                e.activation(MXT[:, :], b[:, 0:P], ACT.Copy, scale=-1.0).then_inc(b_evac.sem, 1)
                for s in range(SLOTS):
                    for n in range(s * TPB * R, (s + 1) * TPB * R):
                        b_diag.wait(e, i, n)
                        if n % R == 0:
                            b_pv.wait(e, i, n // R - 2)
                        e.activation(EX[:, n % 8, :], ring_pair("u", n)[:, :], ACT.Exp).then_inc(b_exp.sem, 1)
                for half in range(2):
                    e.activation(TRB[:, half * 512:(half + 1) * 512], job(OJ + half), ACT.Copy).then_inc(b_evac.sem, 1)

        qb_ready = sem("q_bias_scaled")

        def attn_b_vector(e):
            b_norm.prime_vector(e)
            for g in (b_split, b_mred, b_diag, b_ot, b_onorm, b_yx, b_mread, b_bound, b_sumread, b_flag, b_vread):
                g.prime(e)
            e.wait_ge(b_begin, 1)
            b_norm.vector(e, 0)
            e.tensor_scalar(qbs[0:BIAS, :], qbias[0:BIAS, :], QSCALE, None, ALU.mult).then_inc(qb_ready, 1)
            e.memset(KA[:, :, :].bitcast(F32), 0.0).then_inc(b_ones, 1)
            e.memset(KB[:, :, :].bitcast(F32), 0.0).then_inc(b_ones, 1)
            e.memset(V9[:, :, :, :], 1.0).then_inc(b_ones, 1)
            for b in (6, 7):
                v_steps.add(e.memset(bank[b], 0.0))
            v_steps.settle(e)
            e.memset(MX[:, :], 0.0).then_inc(b_otzero, 1)
            e.wait_ge(b_tables, 16 * 5)
            e.wait_ge(b_ones, 3)
            with e.Fori(0, BATCH - 1) as i:
                v_steps.loop(i, B_V)
                attn_b_vector_turn(e, i, True)
            v_steps.end(BATCH - 1)
            attn_b_vector_turn(e, BATCH - 1, False)

        def attn_b_vector_turn(e, i, more):
            for m in range(16):
                s, side, half = m // 4, (m // 2) % 2, m % 2
                b_evac.wait(e, i, QJ(m))
                if side == 0 and half == 0:
                    if s < 2:
                        b_pv.wait(e, i, -1)
                    else:
                        b_qpad[s - 2].wait(e, i, 0)
                if side == 0:
                    v_steps.chain(e, e.tensor_copy(TH[0:BIAS, m % 2, :], T[0:BIAS, m % 2, :]))
                if side:
                    b_kpad[s].wait(e, i, -1)
                to = (QSTB[0:BIAS, s % 2, half * 512:(half + 1) * 512].bitcast(F32R) if side == 0
                      else KA[0:BIAS, s, half * 512:(half + 1) * 512])
                e.scalar_tensor_tensor(out=to, in0=TH[0:BIAS, m % 2, :].bitcast(F32), scalar=(negqb if side == 0 else negkb)[0:BIAS, 0:1],
                                       in1=T[0:BIAS, m % 2, :], op0=ALU.mult, op1=ALU.add).then_inc(b_split.sem, 1)
                if m == 15:
                    for n in range(4):
                        b_mjob.wait(e, i, n)
                        e.tensor_reduce(top[:, n:n + 1], job_bank("m", n), AX.X, ALU.max).then_inc(b_mread.sem, 1)
                    b_mread.wait(e, i, 3)
                    v_steps.add(e.tensor_tensor(bound[:, 0:1], top[:, 0:1], top[:, 1:2], ALU.max))
                    v_steps.chain(e, e.tensor_tensor(bound[:, 1:2], top[:, 2:3], top[:, 3:4], ALU.max))
                    b_sum.wait(e, i, -1)
                    e.tensor_tensor(top[:, 0:1], bound[:, 0:1], bound[:, 1:2], ALU.mult).then_inc(b_bound.sem, 1)

            b_pv.wait(e, i, -1)
            for c in range(TPB):
                b_vjob.wait(e, i, c)
                e.tensor_tensor(V9[:, c, :, 0:D], job_bank("v", c)[:, 0:P].rearrange("p (h d) -> p h d", d=D),
                                vbias[:, :].rearrange("p (h d) -> p h d", d=D), ALU.add).then_inc(b_vread.sem, 1)

            def normalise(s):
                for half in range(2):
                    b_ojob.wait(e, i, 2 * s + half)
                    b = ring_pair("o", s)[:, 512 * half:512 * (half + 1)].rearrange("p (t c n) -> p t c n", t=GROUP, c=R)
                    v_steps.chain(e, e.reciprocal(DEN[:, :, :], b[:, :, :, D]))
                    e.tensor_tensor(ATT[:, GROUP * half:GROUP * half + GROUP, R * D * s:R * D * (s + 1)].rearrange("p t (c d) -> p t c d", d=D),
                                    b[:, :, :, 0:D], DEN[:, :, :].unsqueeze(3).to_broadcast([P, GROUP, R, D]), ALU.mult).then_inc(b_onorm.sem, 1)
                    b_onorm.wait(e, i, 2 * s + half)

            def copy_ot(s):
                b_pv.wait(e, i, TPB * (s + 1) - 1)
                if s:
                    b_ojob.wait(e, i, 2 * s - 1)
                e.tensor_copy(OTB, pairC[:, :]).then_inc(b_ot.sem, 1)

            b_sum.wait(e, i, 0)
            e.tensor_reduce(large[:, :], job_bank("s", 0)[0:1, 0:P], AX.X, ALU.max).then_inc(b_sumread.sem, 1)
            b_sumread.wait(e, i, 0)
            e.tensor_scalar(flag[:, :], large[:, :], (SAFE / QSCALE) ** 2, None, ALU.is_gt).then_inc(b_flag.sem, 1)
            b_flag.wait(e, i, 0)
            b_job.wait(e, i, SJ - BJ)
            pass_wait(e)
            needed = e.value_load(flag[0:1, 0:1], min_val=0, max_val=1)
            with e.If(needed > 0):
                for n in range(UNITS):
                    s, q, r = n // (TPB * R), n // R % TPB, n % R
                    b_mscore.wait(e, i, n)
                    b = pairs[n % 2]
                    v_steps.chain(e, e.scalar_tensor_tensor(out=b[:, q * P:(q + 1) * P], in0=overT[:, :], scalar=-2.0 * SL[R * s + r],
                                                            in1=b[:, q * P:(q + 1) * P], op0=ALU.mult, op1=ALU.add))
                    at = TPB * (R * s + r) + q
                    e.tensor_reduce(MX[:, at:at + 1], b[:, :], AX.X, ALU.max).then_inc(b_mred.sem, 1)
            with e.Else():
                e.memset(MX[:, :], 0.0).then_inc(b_mred.sem, 1)
                e.sem_inc(b_mred.sem, UNITS - 1)
                e.sem_inc(v_steps.sem, UNITS)
            for s in range(SLOTS):
                for g in range(TPB):
                    if more and s == 1:
                        b_norm.tile_statistics(e, i + 1, g)
                    if more and s == 2 and g == 0:
                        b_norm.turn_variances(e)
                    if more and s == 3:
                        b_norm.normalise_tile(e, i + 1, g)
                    for r in range(R):
                        if g == 2 and r == 2 and s:
                            normalise(s - 1)
                        n = (s * TPB + g) * R + r
                        b_score.wait(e, i, n)
                        b = ring_pair("u", n)
                        e.scalar_tensor_tensor(out=b[:, g * P:(g + 1) * P], in0=over[:, :], scalar=-2.0 * SL[R * s + r],
                                               in1=b[:, g * P:(g + 1) * P], op0=ALU.mult, op1=ALU.add).then_inc(b_diag.sem, 1)
                    if g == 0 and s:
                        copy_ot(s - 1)
            copy_ot(SLOTS - 1)
            normalise(SLOTS - 1)
            for g in range(2):
                b_y.wait(e, i, g)
                b_xb.wait(e, i, 0)
                xs = X[:, bass.ds(i * TPB + 4 * g, 4), :]
                e.tensor_tensor(xs, job_bank("y", g).rearrange("p (t n) -> p t n", n=P), xs, ALU.add).then_inc(b_yx.sem, 1)
                b_yx.wait(e, i, g)

        B_V = 8 + 7 + 6 + 2 + 8 + 8 + GROUPS * R
        b_otzero = sem("b_ot_zeroed")

        def attn_b_tensor(e):
            for g in (b_job, b_ojob, b_mscore, b_score, b_pv, b_y, b_mjob, b_sum, b_vjob):
                g.prime(e)
            e.wait_ge(b_otzero, 1)
            e.wait_ge(b_tables, 16 * 5)
            with e.Fori(0, BATCH) as i:
                for half in range(2):
                    b = job_free(e, i, "a", half)
                    b_norm.transposes(e, i, half, b).then_inc(b_job.sem, 1)
                b_evac.wait(e, i, 1)
                for m in range(16):
                    s, side, half = m // 4, (m // 2) % 2, m % 2
                    if m == LATE:
                        for n in range(4):
                            e.matmul(job_free(e, i, "a", SQJ(n)), Wqkn[:, n // 2, :], XTB[:, (n % 2) * 512:(n % 2 + 1) * 512],
                                     start=True, stop=True).then_inc(b_job.sem, 1)
                    e.matmul(job_free(e, i, "a", QJ(m))[0:BIAS, :], (Wqb if side == 0 else Wkb)[:, s, :], XTB[:, half * 512:(half + 1) * 512],
                             start=True, stop=True).then_inc(b_job.sem, 1)
                    if m == 15:
                        for n in range(4):
                            b_evac.wait(e, i, SQJ(n))
                            e.matmul(job_free(e, i, "m", n), blkb[:, :], SQ[:, n, :], start=True, stop=True).then_inc(b_mjob.sem, 1)
                for c in range(TPB):
                    e.matmul(job_free(e, i, "v", c)[:, 0:P], XTB[:, c * P:(c + 1) * P], Wvb[:, :], start=True, stop=True).then_inc(b_vjob.sem, 1)
                b_bound.wait(e, i, 0)
                e.matmul(job_free(e, i, "s", 0)[0:1, 0:P], top[:, 0:1], ident[:, :], start=True, stop=True).then_inc(b_sum.sem, 1)
                b_vread.wait(e, i, TPB - 1)

                def exp_scores(s, g, r):
                    n = (s * TPB + g) * R + r
                    b = ring_free(e, i, "u", n)
                    for half in range(2):
                        lo, hi = 512 * half, 512 * (half + 1)
                        cut = min(max(g * P, lo), hi)
                        for m, a, z in ((KB, lo, cut), (KA, cut, hi)):
                            if a < z:
                                last = e.matmul(b[:, a:z], m[:, s, g * P:(g + 1) * P], Qpad[:, s, r, a:z], start=True, stop=True)
                    last.then_inc(b_score.sem, 1)

                def max_scores(s, q, r):
                    n = (s * TPB + q) * R + r
                    if n < 2:
                        b_exp.wait(e, i, n - 2)
                    else:
                        b_mred.wait(e, i, n - 2)
                    b = pairs[n % 2]
                    for half in range(2):
                        lo, hi = 512 * half, 512 * (half + 1)
                        cut = min(max((q + 1) * P, lo), hi)
                        for k, a, z in ((KA, lo, cut), (KB, cut, hi)):
                            if a < z:
                                last = e.matmul(b[:, a:z], Qpad[:, s, r, q * P:(q + 1) * P], k[:, s, a:z], start=True, stop=True)
                    last.then_inc(b_mscore.sem, 1)

                def pv(s, g, half):
                    n = s * TPB + g
                    if half == 0:
                        b_exp.wait(e, i, R * n + R - 1)
                        if g == 0:
                            b_ot.wait(e, i, s - 1)
                    for r in range(R):
                        last = e.matmul(pairC[PART * r:PART * r + D + 1, 512 * half:512 * (half + 1)], V9[:, g, R * s + r, :],
                                        EX[:, (R * n + r) % 8, 512 * half:512 * (half + 1)], start=(g == 0), stop=(g == TPB - 1))
                    if half == 1:
                        last.then_inc(b_pv.sem, 1)

                def naturals(s):
                    b_ot.wait(e, i, s)
                    pair = ring_free(e, i, "o", s)
                    for half in range(2):
                        b = pair[:, 512 * half:512 * (half + 1)]
                        for j in range(GROUP):
                            last = e.transpose(b[:, j * P:(j + 1) * P], OTB[:, (GROUP * half + j) * P:(GROUP * half + j + 1) * P], ident[:, :])
                        last.then_inc(b_ojob.sem, 1)

                for s in range(SLOTS):
                    b_qpad[s].wait(e, i, 0)
                    b_kpad[s].wait(e, i, 0)
                b_flag.wait(e, i, 0)
                pass_wait(e)
                needed = e.value_load(flag[0:1, 0:1], min_val=0, max_val=1)
                with e.If(needed > 0):
                    for n in range(UNITS):
                        max_scores(n // (TPB * R), n // R % TPB, n % R)
                with e.Else():
                    e.sem_inc(b_mscore.sem, UNITS)
                b_mred.wait(e, i, UNITS - 1)
                e.transpose(job_free(e, i, "a", SJ)[:, 0:P], MX[:, :], ident[:, :]).then_inc(b_job.sem, 1)
                b_shift.wait(e, i, 0)
                for s in range(SLOTS):
                    for g in range(TPB):
                        exp_scores(s, g, 0)
                        exp_scores(s, g, 1)
                        before = s * TPB + g - 1
                        if before >= 0:
                            pv(before // TPB, before % TPB, 0)
                        if g == 2 and s:
                            naturals(s - 1)
                        exp_scores(s, g, 2)
                        exp_scores(s, g, 3)
                        if before >= 0:
                            pv(before // TPB, before % TPB, 1)
                pv(SLOTS - 1, TPB - 1, 0)
                pv(SLOTS - 1, TPB - 1, 1)
                naturals(SLOTS - 1)
                b_onorm.wait(e, i, DJ - 1)
                for half in range(2):
                    b = job_free(e, i, "a", OJ + half)
                    for j in range(GROUP):
                        last = e.transpose(b[:, j * P:(j + 1) * P], ATT[:, GROUP * half + j, :], ident[:, :])
                    last.then_inc(b_job.sem, 1)
                for g in range(2):
                    b_evac.wait(e, i, OJ + g)
                    b = job_free(e, i, "y", g)
                    for j in range(GROUP):
                        last = e.matmul(b[:, j * P:(j + 1) * P], TRB[:, (GROUP * g + j) * P:(GROUP * g + j + 1) * P], Wob[:, :], start=True, stop=True)
                    last.then_inc(b_y.sem, 1)

        ff = ExitStack()
        XNR = sb("XNR", [P, 2, TPB, ROW], scope=ff)
        FMV = sb("FMV", [P, NT, 2], scope=ff)
        VAR = sb("VAR", [P, 2, TPB], scope=ff)
        RR = sb("RR", [P, 2, NT], scope=ff)
        MR = sb("MR", [P, NT], scope=ff)
        half32 = sb("half32", [P, 2, TPB], scope=ff)
        S = sb("S", [P, NT, P], scope=ff)
        AB = sb("AB", [P, NT, P], scope=ff)
        W1 = sb("W1", [P, EXPERTS, DF + FC], scope=ff)
        TMP = sb("TMP", [P, TPB, P], scope=ff)
        b2row = sb("b2row", [1, EXPERTS, P], scope=ff)
        b2all = sb("b2all", [P, EXPERTS, P], scope=ff)
        LG = sb("LG", [P, TPB, EXPERTS], scope=ff)
        R1 = sb("R1", [P, TPB, EXPERTS], scope=ff)
        R2 = sb("R2", [P, TPB, EXPERTS], scope=ff)
        RS = sb("RS", [P, TPB, EXPERTS], scope=ff)
        RK = sb("RK", [P, TPB, EXPERTS], scope=ff)
        BASE = sb("BASE", [P, TPB + 1, EXPERTS], scope=ff)
        DF2 = sb("DF2", [P, TPB, 2], scope=ff)
        DI = sb("DI", [P, 2, TPB, 2], I32, ff)
        C1 = sb("C1", [P, NT], scope=ff)
        C2 = sb("C2", [P, NT], scope=ff)
        C3 = sb("C3", [P, NT], scope=ff)
        C4 = sb("C4", [P, TPB], scope=ff)
        ZA = sb("ZA", [P, NT], scope=ff)
        ZN = sb("ZN", [P, NT], scope=ff)
        tok = sb("tok", [P, NT], scope=ff)
        tri = sb("tri", [P, P], scope=ff)
        ones = sb("ones", [P, P], scope=ff)
        tab = sb("tab", [P, TAB], scope=ff)
        NEED = sb("NEED", [P, EXPERTS, MAXT], scope=ff)
        CUM = sb("CUM", [P, EXPERTS + 1], scope=ff)
        START = sb("START", [P, EXPERTS + 1], scope=ff)
        HOT = sb("HOT", [P, NTILES, EXPERTS + 1], scope=ff)
        HOT8 = sb("HOT8", [P, NTILES, EXPERTS], scope=ff)
        EJ = sb("EJ", [P, NTILES], scope=ff)
        RJ = sb("RJ", [P, NTILES], scope=ff)
        EI = sb("EI", [P, NTILES], I32, ff)
        RI = sb("RI", [P, NTILES], I32, ff)
        BI = sb("BI", [P, EXPERTS], I32, ff)
        XG = sb("XG", [P, DEPTH, 2, ROW], scope=ff)
        XGT = sb("XGT", [P, DEPTH, TILE], scope=ff)
        WT1 = sb("WT1", [P, DEPTH, DF + FC], scope=ff)
        HT = sb("HT", [P, DEPTH, FC, TILE], scope=ff)
        YG = sb("YG", [P, DEPTH, 2, P], scope=ff)
        DT = sb("DT", [P, 2, EXPERTS], scope=ff)
        DTF = sb("DTF", [P, 2], scope=ff)
        DTI = sb("DTI", [P, DEPTH, 2], I32, ff)
        O = sb("O", [P, 2, NT, P], scope=ff)
        ff.close()

        AGO = [-1, -2, 0]

        class Ffn:
            sems = {}

            def __init__(self, k, begin):
                self.begin, self.fold = begin, k == 0
                tiles = NTILES // DEPTH

                def count(name):
                    if name not in self.sems:
                        self.sems[name] = sem("f_" + name)
                    return self.sems[name]

                def signal(name, per, turns=BATCH, unit=1):
                    return Signal(count(name), per, unit, k * (turns + 1) * per * unit)

                def mark(name, total):
                    return Mark(count(name), k * total)
                self.stats, self.rstd, self.xscale = signal("stats_ready", 1), signal("rstd_ready", 1), mark("x_scale_ready", 1)
                self.xn = signal("xn_ready", 4, BATCH // 2)
                self.tjob, self.tevac = signal("transposed", 4, BATCH // 2), signal("xt_ready", 4, BATCH // 2)
                self.ajob, self.aread = signal("abel_done", 8, BATCH // 2), signal("abel_read", 8, BATCH // 2)
                self.gelu = signal("abel_ready", 2, BATCH // 2)
                self.hot, self.count, self.ranked = [signal(n, 2, BATCH // 2) for n in ("experts_chosen", "counted", "rows_ready")]
                self.kept = signal("s_ready", 2, BATCH // 2)
                self.tables, self.pads, self.w1 = mark("tables_loaded", 48), mark("pads_stored", 16 * (EXPERTS + 1)), mark("w1_loaded", 32)
                self.tiles = mark("tile_table_ready", 1)
                self.dma_routed = [Count(count(f"tokens_scattered{b}"), 16 * 2 * TPB, k * BATCH // 2) for b in range(2)]
                self.routed = [signal(f"tokens_routed{b}", 1, BATCH // 2) for b in range(2)]
                self.ends = mark("ends_ready", 1)
                self.b2row, self.b2bank, self.b2read = mark("b2_row_loaded", 16), mark("b2_spread", 2), mark("b2_copied", 1)
                self.gap, self.ex, self.wd = mark("gap_ready", 1), mark("gap_exp", 1), mark("weights_ready", 1)
                self.load = [signal(f"tile_loaded{n}", 1, tiles, 32) for n in range(DEPTH)]
                self.turned, self.xt = signal("tile_turned", DEPTH, tiles), signal("tile_xt_ready", DEPTH, tiles)
                self.hjob, self.hevac = signal("hidden_done", DEPTH * FC, tiles), signal("hidden_ready", DEPTH * FC, tiles)
                self.yjob, self.yread = signal("expert_done", DEPTH, tiles), signal("expert_read", DEPTH, tiles)
                self.where = signal("places_ready", DEPTH, tiles)
                self.dma_back = [Count(count(f"tile_scattered{n}"), 32, k * tiles) for n in range(DEPTH)]
                self.back = [signal(f"tile_stored{n}", 1, tiles) for n in range(DEPTH)]
                self.oload = signal("results_loaded", 1, BATCH, 32)
                self.scaled, self.z, self.gate = signal("first_scaled", 1), signal("z_ready", 1), signal("gate_ready", 1)
                self.added = signal("x_updated", 1)
                self.summed, self.differ = signal("experts_summed", 1), signal("branches_subtracted", 1)

            def sync(self, e):
                for g in self.load + [self.oload] + self.back + self.routed:
                    g.prime(e)
                e.wait_ge(self.begin, 1)
                for a, b in ((tok[:, :], I["tok"]), (tri[:, :], I["tri"]), (tab[:, :], rowb(I["tab"]))):
                    e.dma_start(a, b).then_inc(self.tables.sem, 16)
                e.dma_start(W1[:, :, 0:DF], I["w1"]).then_inc(self.w1.sem, 16)
                e.dma_start(W1[:, :, DF:DF + FC], I["b1T"]).then_inc(self.w1.sem, 16)
                e.dma_start(routed[EXPERTS * REGION:EXPERTS * REGION + SPARE, :], I["pads"][EXPERTS * TILE:EXPERTS * TILE + SPARE, :]).then_inc(self.pads.sem, 16)
                with e.Fori(0, BATCH // 2) as i:
                    for b in range(2):
                        self.dma_routed[b].wait(e, i)
                        e.sem_inc(self.routed[b].sem, 1)
                e.wait_ge(fold_copied, EXPERTS + 1)
                e.dma_start(b2row[:, :, :], b2r[:, :]).then_inc(self.b2row.sem, 16)
                self.tiles.wait(e, 1)
                self.pads.wait(e, 16 * (EXPERTS + 1))
                self.w1.wait(e, 32)

                def load(tile, k):
                    x = e.value_load(EI[0:1, tile], min_val=0, max_val=EXPERTS - 1)
                    row = e.value_load(RI[0:1, tile], min_val=0, max_val=EXPERTS * REGION + SPARE - TILE)
                    e.dma_start(XG[:, k, :, :], routed[bass.ds(row, TILE), :].rearrange("(a p) c -> p a c", p=P)).then_inc(self.load[k].sem, 16)
                    e.dma_start(WT1[:, k, :], W1[:, bass.ds(x, 1), :].rearrange("p a c -> p (a c)")).then_inc(self.load[k].sem, 16)

                def stored(i, k):
                    self.dma_back[k].wait(e, i)
                    e.sem_inc(self.back[k].sem, 1)
                turns = NTILES // DEPTH
                for k in range(DEPTH):
                    load(slice(k, k + 1), k)

                def following(i, k):
                    self.turned.wait(e, i, k)
                    pass_wait(e)
                    self.where.wait(e, i, k)
                    pass_wait(e)
                    self.hevac.wait(e, i, (k + 1) * FC - 1)
                    pass_wait(e)
                    load(bass.ds(i * DEPTH + (DEPTH + k), 1), k)
                following(0, 0)
                following(0, 1)
                following(0, 2)
                stored(0, 0)
                with e.Fori(1, turns - 1) as i:
                    following(i, 0)
                    stored(i - 1, 1)
                    following(i, 1)
                    stored(i - 1, 2)
                    following(i, 2)
                    stored(i, 0)
                for at, k in ((turns - 2, 1), (turns - 2, 2), (turns - 1, 0), (turns - 1, 1), (turns - 1, 2)):
                    stored(at, k)
                for g in self.back:
                    g.wait(e, turns - 1, 0)
                with e.Fori(0, BATCH) as i:
                    self.oload.wait(e, i, -1)
                    pass_wait(e)
                    for k in range(2):
                        e.dma_start(O[:, k, bass.ds(i * TPB, TPB), :],
                                    placed[bass.ds(i * SEQ + k * (NT * P), SEQ), :].rearrange("(t p) d -> p t d", p=P)).then_inc(self.oload.sem, 16)

            def gpsimd(self, e):
                e.wait_ge(self.begin, 1)
                self.scaled.prime(e)
                self.differ.prime(e)
                self.rstd.prime(e)
                g_steps.chain(e, e.memset(half32[:, :, :], -0.5))
                with e.Fori(0, BATCH) as i:
                    self.stats.wait(e, i, 0)
                    e.tensor_tensor(RR[:, :, bass.ds(i * TPB, TPB)], VAR[:, :, :], half32[:, :, :], ALU.pow).then_inc(self.rstd.sem, 1)
                with e.Fori(0, BATCH // 2) as i:
                    for b in range(2):
                        self.ranked.wait(e, i, b)
                        pass_wait(e)
                        for t in range(TPB):
                            for k in range(2):
                                e.indirect_dma_start(out=routed, out_offset=bass.IndirectOffsetOnAxis(ap=DI[:, b, t, k:k + 1], axis=0),
                                                     in_=XNR[:, b, t, :], in_offset=None).then_inc(self.dma_routed[b].sem, 16)
                with e.Fori(0, NTILES // DEPTH) as i:
                    for k in range(DEPTH):
                        self.yread.wait(e, i, k)
                        pass_wait(e)
                        self.where.wait(e, i, k)
                        pass_wait(e)
                        for a in range(2):
                            e.indirect_dma_start(out=placed, out_offset=bass.IndirectOffsetOnAxis(ap=DTI[:, k, a:a + 1], axis=0),
                                                 in_=YG[:, k, a, :], in_offset=None).then_inc(self.dma_back[k].sem, 16)
                self.wd.wait(e, 1)
                with e.Fori(0, BATCH) as i:
                    self.oload.wait(e, i, 0)
                    ts = bass.ds(i * TPB, TPB)
                    e.tensor_tensor(O[:, 0, ts, :], O[:, 0, ts, :], C1[:, ts].unsqueeze(2).to_broadcast([P, TPB, P]), ALU.mult).then_inc(self.scaled.sem, 1)
                    self.summed.wait(e, i, 0)
                    e.tensor_tensor(O[:, 1, ts, :], O[:, 0, ts, :], AB[:, ts, :], ALU.subtract).then_inc(self.differ.sem, 1)

            def scalar(self, e):
                for g in (self.tevac, self.gelu, self.xt, self.hevac, self.gate, self.kept):
                    g.prime(e)
                e.wait_ge(self.begin, 1)
                if self.fold:
                    fold_scalar(e)
                self.xscale.wait(e, 1)
                with e.Fori(0, BATCH // 2) as i:
                    for b in range(2):
                        for half in range(2):
                            self.tjob.wait(e, i, 2 * b + half)
                            self.ajob.wait(e, i, 4 * b - 1)
                            e.activation(XTB[:, half * 512:(half + 1) * 512], bank[half], ACT.Identity,
                                         bias=lnbT[:, 0:1], scale=lngT[:, 0:1]).then_inc(self.tevac.sem, 1)
                        self.aread.wait(e, i, 4 * b + 3)
                        ab = AB[:, bass.ds(i * (2 * TPB) + b * TPB, TPB), :]
                        e.activation(ab, ab, ACT.Gelu).then_inc(self.gelu.sem, 1)
                        for t in range(TPB):
                            at = bass.ds(i * (2 * TPB) + b * TPB + t, 1)
                            ins = e.activation(S[:, at, :].rearrange("p a d -> p (a d)"), X[:, at, :].rearrange("p a d -> p (a d)"), ACT.Identity,
                                               scale=RR[:, 0, at], bias=MR[:, at])
                        ins.then_inc(self.kept.sem, 1)
                self.ends.wait(e, 1)
                for x in range(EXPERTS):
                    end = e.value_load(BI[0:1, x:x + 1], min_val=0, max_val=EXPERTS * REGION - TILE)
                    e.dma_start(routed[bass.ds(end, TILE), :], I["pads"][x * TILE:(x + 1) * TILE, :]).then_inc(self.pads.sem, 16)
                self.gap.wait(e, 1)
                e.activation(C3[:, :], C3[:, :], ACT.Exp).then_inc(self.ex.sem, 1)
                with e.Fori(0, NTILES // DEPTH) as i:
                    for k in range(DEPTH):
                        self.turned.wait(e, i, k)
                        self.hjob.wait(e, i, (k + 1) * FC - 1 - DEPTH * FC)
                        e.activation(XGT[:, k, :], bank[k % 2][:, 0:TILE], ACT.Identity,
                                     bias=lnbT[:, 0:1], scale=lngT[:, 0:1]).then_inc(self.xt.sem, 1)
                        if k:
                            self.hidden(e, i, k - 1)
                    self.hidden(e, i, DEPTH - 1)
                with e.Fori(0, BATCH) as i:
                    self.z.wait(e, i, 0)
                    ts = bass.ds(i * TPB, TPB)
                    e.activation(ZA[:, ts], ZA[:, ts], ACT.Sigmoid, bias=mixb[:, 0:1]).then_inc(self.gate.sem, 1)

            def hidden(self, e, i, k):
                for c in range(FC):
                    if c % 2 == 0:
                        self.hjob.wait(e, i, k * FC + c + 1)
                    if c == 0:
                        self.yjob.wait(e, i, k - DEPTH)
                    e.activation(HT[:, k, c, :], pairs[k % 2][:, c * TILE:(c + 1) * TILE], ACT.Gelu,
                                 bias=WT1[:, k, DF + c:DF + c + 1]).then_inc(self.hevac.sem, 1)

            def route(self, e, i, b, every, one_hot):
                ts = bass.ds(i * (2 * TPB) + b * TPB, TPB)

                def steps(ins):
                    v_steps.chain(e, ins)
                self.routed[b].wait(e, i, -1)
                for t in range(TPB):
                    at = bass.ds(i * (2 * TPB) + b * TPB + t, 1)
                    ins = e.tensor_scalar(XNR[:, b, t, 0:P], X[:, at, :].rearrange("p a d -> p (a d)"), FMV[:, at, 0:1].rearrange("p a c -> p (a c)"),
                                          RR[:, 1, at], ALU.subtract, ALU.mult)
                    ins.then_inc(self.xn.sem, 1) if t % GROUP == GROUP - 1 else v_steps.add(ins)
                for j in range(4):
                    self.ajob.wait(e, i, 4 * b + j)
                    y = bank[2 + j % 2][:, 0:2 * (P + EXPERTS)].rearrange("p (t n) -> p t n", t=2)
                    tt = bass.ds(i * (2 * TPB) + b * TPB + 2 * j, 2)
                    v_steps.add(e.tensor_tensor(LG[:, 2 * j:2 * j + 2, :], y[:, :, P:P + EXPERTS], abias[:, None, P:P + EXPERTS].to_broadcast([P, 2, EXPERTS]), ALU.add))
                    e.tensor_tensor(AB[:, tt, :], y[:, :, 0:P], abias[:, None, 0:P].to_broadcast([P, 2, P]), ALU.add).then_inc(self.aread.sem, 1)
                v_steps.settle(e)
                pass_wait(e)
                one_hot(C1[:, ts], R1, steps)
                steps(e.scalar_tensor_tensor(out=LG[:, :, :], in0=R1[:, :, :], scalar=-3.0e38, in1=LG[:, :, :], op0=ALU.mult, op1=ALU.add))
                one_hot(C2[:, ts], R2, steps)
                e.tensor_tensor(RS[:, :, :], R1[:, :, :], R2[:, :, :], ALU.add).then_inc(self.hot.sem, 1)
                self.hot.wait(e, i, b)
                to = XNR[:, b, :, P:ROW]
                steps(e.tensor_tensor(to, RS[:, :, :], every(tok[:, ts]), ALU.mult))
                v_steps.add(e.scalar_tensor_tensor(out=to, in0=R2[:, :, :], scalar=float(NT * P), in1=to, op0=ALU.mult, op1=ALU.add))
                steps(e.tensor_copy(BASE[:, 0, :], BASE[:, TPB, :]))
                self.count.wait(e, i, b)
                cnt = bank[4][:, 0:2 * TPB * EXPERTS].rearrange("p (k t x) -> p k t x", k=2, t=TPB)
                for t in range(TPB):
                    steps(e.tensor_tensor(BASE[:, t + 1, :], BASE[:, t, :], cnt[:, 1, t, :], ALU.add))
                steps(e.tensor_tensor(RK[:, :, :], BASE[:, 0:TPB, :], cnt[:, 0, :, :], ALU.add))
                for k, r in enumerate((R1, R2)):
                    steps(e.tensor_tensor(RS[:, :, :], RK[:, :, :], r[:, :, :], ALU.mult))
                    steps(e.tensor_reduce(DF2[:, :, k], RS[:, :, :], AX.X, ALU.add))
                e.tensor_copy(DI[:, b, :, :], DF2[:, :, :]).then_inc(self.ranked.sem, 1)
                self.ranked.wait(e, i, b)

            def vector(self, e):
                for g in (self.stats, self.xn, self.aread, self.hot, self.ranked, self.yread, self.where, self.z, self.added, self.summed):
                    g.prime(e)
                v_steps.add(e.memset(ones[:, :], 1.0))
                with e.Fori(0, BATCH) as i:
                    v_steps.loop(i, 2 * TPB + 2)
                    for t in range(TPB):
                        v_steps.add(e.bn_stats(stats[:, t, :], X[:, bass.ds(i * TPB + t, 1), :].rearrange("p a d -> p (a d)")))
                    v_steps.settle(e)
                    pass_wait(e)
                    for t in range(TPB):
                        v_steps.add(e.bn_aggr(mv[:, t, :], stats[:, t, :]))
                    v_steps.settle(e)
                    self.rstd.wait(e, i, -1)
                    v_steps.add(e.tensor_scalar(VAR[:, 0, :], mv[:, :, 1], EPS, None, ALU.add))
                    e.tensor_scalar(VAR[:, 1, :], mv[:, :, 1], 1.0 + EPS, EPS * EPS, ALU.mult, ALU.add).then_inc(self.stats.sem, 1)
                    v_steps.chain(e, e.tensor_copy(FMV[:, bass.ds(i * TPB, TPB), :], mv[:, :, :]))
                    self.stats.wait(e, i, 0)
                v_steps.end(BATCH)
                self.rstd.wait(e, BATCH - 1, 0)
                v_steps.chain(e, e.scalar_tensor_tensor(out=MR[:, :], in0=FMV[:, :, 0], scalar=-1.0, in1=RR[:, 0, :], op0=ALU.mult, op1=ALU.mult))
                e.tensor_scalar(RR[:, 0, :], RR[:, 0, :], 1.0, None, ALU.add).then_inc(self.xscale.sem, 1)
                self.tables.wait(e, 48)
                v_steps.chain(e, e.tensor_copy(BASE[:, TPB, :], tab[:, T_BASE:T_BASE + EXPERTS]))

                def every(c):
                    return c.unsqueeze(2).to_broadcast([P, TPB, EXPERTS])

                def one_hot(top, hot, steps):
                    steps(e.tensor_reduce(top, LG[:, :, :], AX.X, ALU.max))
                    steps(e.tensor_tensor(hot[:, :, :], LG[:, :, :], every(top), ALU.is_equal))
                    steps(e.tensor_tensor(hot[:, :, :], hot[:, :, :], rank8[:, None, :].to_broadcast([P, TPB, EXPERTS]), ALU.mult))
                    steps(e.tensor_reduce(C4[:, :], hot[:, :, :], AX.X, ALU.max))
                    steps(e.tensor_tensor(hot[:, :, :], hot[:, :, :], every(C4[:, :]), ALU.is_equal))

                with e.Fori(0, BATCH // 2) as i:
                    v_steps.loop(i, 2 * (4 + 11 + 3 + TPB + 1 + 4 + 6))
                    for b in range(2):
                        self.route(e, i, b, every, one_hot)
                v_steps.end(BATCH // 2)
                v_steps.settle(e)

                def st(ins):
                    v_steps.chain(e, ins)

                def of(n, width):
                    return tab[:, n:n + width]
                e.tensor_tensor(C3[:, :], C2[:, :], C1[:, :], ALU.subtract).then_inc(self.gap.sem, 1)
                e.tensor_copy(BI[:, :], BASE[:, TPB, :]).then_inc(self.ends.sem, 1)
                st(e.tensor_tensor(BASE[:, 0, :], BASE[:, TPB, :], of(T_BASE, EXPERTS), ALU.subtract))
                st(e.tensor_tensor(NEED[:, :, :], BASE[:, 0, :].unsqueeze(2).to_broadcast([P, EXPERTS, MAXT]),
                                   of(T_FULL, MAXT).unsqueeze(1).to_broadcast([P, EXPERTS, MAXT]), ALU.is_gt))
                st(e.tensor_reduce(BASE[:, 1, :], NEED[:, :, :], AX.X, ALU.add))
                st(e.memset(CUM[:, 0:1], 0.0))
                for x in range(EXPERTS):
                    st(e.tensor_tensor(CUM[:, x + 1:x + 2], CUM[:, x:x + 1], BASE[:, 1, x:x + 1], ALU.add))
                st(e.scalar_tensor_tensor(out=START[:, :], in0=CUM[:, :], scalar=-float(TILE), in1=of(T_BASE, EXPERTS + 1), op0=ALU.mult, op1=ALU.add))
                number = of(T_TILE, NTILES)
                st(e.tensor_tensor(HOT8[:, :, :], number.unsqueeze(2).to_broadcast([P, NTILES, EXPERTS]),
                                   CUM[:, 1:EXPERTS + 1].unsqueeze(1).to_broadcast([P, NTILES, EXPERTS]), ALU.is_ge))
                st(e.tensor_reduce(EJ[:, :], HOT8[:, :, :], AX.X, ALU.add))
                st(e.tensor_tensor(HOT[:, :, :], EJ[:, :].unsqueeze(2).to_broadcast([P, NTILES, EXPERTS + 1]),
                                   of(T_NAME, EXPERTS + 1).unsqueeze(1).to_broadcast([P, NTILES, EXPERTS + 1]), ALU.is_equal))
                st(e.tensor_tensor(HOT[:, :, :], HOT[:, :, :], START[:, :].unsqueeze(1).to_broadcast([P, NTILES, EXPERTS + 1]), ALU.mult))
                st(e.tensor_reduce(RJ[:, :], HOT[:, :, :], AX.X, ALU.add))
                st(e.scalar_tensor_tensor(out=RJ[:, :], in0=number, scalar=float(TILE), in1=RJ[:, :], op0=ALU.mult, op1=ALU.add))
                st(e.tensor_scalar(EJ[:, :], EJ[:, :], float(EXPERTS - 1), None, ALU.min))
                st(e.tensor_tensor(HOT8[:, :, :], EJ[:, :].unsqueeze(2).to_broadcast([P, NTILES, EXPERTS]),
                                   of(T_NAME, EXPERTS).unsqueeze(1).to_broadcast([P, NTILES, EXPERTS]), ALU.is_equal))
                st(e.tensor_copy(EI[:, :], EJ[:, :]))
                e.tensor_copy(RI[:, :], RJ[:, :]).then_inc(self.tiles.sem, 1)
                self.kept.wait(e, BATCH // 2 - 1, 1)
                with e.Fori(0, BATCH) as i:
                    v_steps.loop(i, 3)
                    ts = bass.ds(i * TPB, TPB)
                    v_steps.add(e.tensor_tensor(S[:, ts, :], S[:, ts, :], AB[:, ts, :], ALU.add))
                    st(e.tensor_tensor(TMP[:, :, :], AB[:, ts, :], mixa[:, None, :].to_broadcast([P, TPB, P]), ALU.mult))
                    st(e.tensor_reduce(ZA[:, ts], TMP[:, :, :], AX.X, ALU.add))
                v_steps.end(BATCH)
                self.b2bank.wait(e, 2)
                e.tensor_copy(b2all[:, :, :].rearrange("p x n -> p (x n)"), pairC[:, :]).then_inc(self.b2read.sem, 1)
                self.b2read.wait(e, 1)
                self.ex.wait(e, 1)
                st(e.tensor_scalar(C1[:, :], C3[:, :], 1.0, None, ALU.add))
                st(e.reciprocal(C1[:, :], C1[:, :]))
                e.tensor_tensor(C2[:, :], C3[:, :], C1[:, :], ALU.mult).then_inc(self.wd.sem, 1)
                self.wd.wait(e, 1)

                with e.Fori(0, NTILES // DEPTH) as i:
                    v_steps.loop(i, 2 * DEPTH)

                    def place(k):
                        self.load[k].wait(e, i, 0)
                        v_steps.chain(e, e.tensor_tensor(DT[:, :, :], XG[:, k, :, P:ROW],
                                                         HOT8[:, bass.ds(i * DEPTH + k, 1), :].to_broadcast([P, 2, EXPERTS]), ALU.mult))
                        v_steps.chain(e, e.tensor_reduce(DTF[:, :], DT[:, :, :], AX.X, ALU.add))
                        self.back[k].wait(e, i, -1)
                        e.tensor_copy(DTI[:, k, :], DTF[:, :]).then_inc(self.where.sem, 1)
                        self.where.wait(e, i, k)

                    def result(k):
                        self.yjob.wait(e, i, k)
                        pass_wait(e)
                        x = e.value_load(EI[0:1, bass.ds(i * DEPTH + k, 1)], min_val=0, max_val=EXPERTS - 1)
                        e.tensor_tensor(YG[:, k, :, :], bank[6 + k % 2][:, 0:TILE].rearrange("p (a n) -> p a n", n=P),
                                        b2all[:, bass.ds(x, 1), :].to_broadcast([P, 2, P]), ALU.add).then_inc(self.yread.sem, 1)
                    place(0)
                    place(1)
                    result(0)
                    place(2)
                    result(1)
                    result(2)
                v_steps.end(NTILES // DEPTH)

                with e.Fori(0, BATCH) as i:
                    v_steps.loop(i, TPB + 1)
                    ts = bass.ds(i * TPB, TPB)

                    def tile(m, t):
                        return m[:, bass.ds(i * TPB + t, 1), :].rearrange("p a d -> p (a d)")
                    self.scaled.wait(e, i, 0)
                    for t in range(TPB):
                        ins = e.scalar_tensor_tensor(out=tile(O[:, 0, :, :], t), in0=tile(O[:, 1, :, :], t), scalar=C2[:, bass.ds(i * TPB + t, 1)],
                                                     in1=tile(O[:, 0, :, :], t), op0=ALU.mult, op1=ALU.add)
                        ins.then_inc(self.summed.sem, 1) if t == TPB - 1 else v_steps.add(ins)
                    v_steps.settle(e)
                    self.summed.wait(e, i, 0)
                    pass_wait(e)
                    v_steps.chain(e, e.tensor_tensor(TMP[:, :, :], O[:, 0, ts, :], mixn[:, None, :].to_broadcast([P, TPB, P]), ALU.mult))
                    v_steps.chain(e, e.tensor_reduce(ZN[:, ts], TMP[:, :, :], AX.X, ALU.add))
                    e.tensor_tensor(ZA[:, ts], ZA[:, ts], ZN[:, ts], ALU.add).then_inc(self.z.sem, 1)
                    self.differ.wait(e, i, 0)
                    pass_wait(e)
                    self.gate.wait(e, i, 0)
                    for t in range(TPB):
                        ins = e.scalar_tensor_tensor(out=tile(X, t), in0=tile(O[:, 1, :, :], t), scalar=ZA[:, bass.ds(i * TPB + t, 1)], in1=tile(S, t),
                                                     op0=ALU.mult, op1=ALU.add)
                    ins.then_inc(self.added.sem, 1)
                v_steps.end(BATCH)
                self.added.wait(e, BATCH - 1, 0)

            def tensor(self, e):
                for g in (self.tjob, self.ajob, self.count, self.turned, self.hjob, self.yjob):
                    g.prime(e)
                e.wait_ge(self.begin, 1)
                self.tables.wait(e, 48)
                if self.fold:
                    fold_tensor(e)
                    e.wait_ge(fold_copied, EXPERTS + 1)
                with e.Fori(0, BATCH // 2) as i:
                    for b in range(2):
                        for half in range(2):
                            self.tevac.wait(e, i, 2 * b + half - 2)
                            self.xn.wait(e, i, 2 * b + half)
                            for j in range(GROUP):
                                last = e.transpose(bank[half][:, j * P:(j + 1) * P], XNR[:, b, GROUP * half + j, 0:P], ident[:, :])
                            last.then_inc(self.tjob.sem, 1)
                        for j in range(4):
                            self.tevac.wait(e, i, 2 * b + j // 2)
                            self.aread.wait(e, i, 4 * b + j - 2)
                            for t in (2 * j, 2 * j + 1):
                                last = e.matmul(bank[2 + j % 2][:, (t % 2) * (P + EXPERTS):(t % 2 + 1) * (P + EXPERTS)], XTB[:, t * P:(t + 1) * P],
                                                Wab[:, :], start=True, stop=True)
                            last.then_inc(self.ajob.sem, 1)
                        self.hot.wait(e, i, b)
                        self.ranked.wait(e, i, b - 1)
                        n = TPB * EXPERTS
                        chosen = RS[:, :, :].rearrange("p t x -> p (t x)")
                        e.matmul(bank[4][:, 0:n], tri[:, :], chosen, start=True, stop=True)
                        e.matmul(bank[4][:, n:2 * n], ones[:, :], chosen, start=True, stop=True).then_inc(self.count.sem, 1)
                self.tevac.wait(e, BATCH // 2 - 1, 3)
                self.ranked.wait(e, BATCH // 2 - 1, 1)
                self.b2row.wait(e, 16)
                for half in range(2):
                    e.matmul(bank[6 + half], ones[0:1, :], b2row[0:1, 4 * half:4 * half + 4, :].rearrange("a x n -> a (x n)"),
                             start=True, stop=True).then_inc(self.b2bank.sem, 1)
                self.b2read.wait(e, 1)
                self.tiles.wait(e, 1)

                def turn(i, k, before):
                    self.load[k].wait(e, i, 0)
                    before()
                    for a in range(2):
                        last = e.transpose(bank[k % 2][:, a * P:(a + 1) * P], XG[:, k, a, 0:P], ident[:, :])
                    last.then_inc(self.turned.sem, 1)

                def first(i, k):
                    self.xt.wait(e, i, k)
                    self.hevac.wait(e, i, (AGO[k] + 1) * FC - 1)
                    for c in range(FC):
                        e.matmul(pairs[k % 2][:, c * TILE:(c + 1) * TILE], WT1[:, k, c * P:(c + 1) * P], XGT[:, k, :], start=True, stop=True).then_inc(self.hjob.sem, 1)

                def second(i, k, more):
                    self.hevac.wait(e, i, k * FC + FC - 1)
                    self.yread.wait(e, i, AGO[k])
                    pass_wait(e)
                    x = e.value_load(EI[0:1, bass.ds(i * DEPTH + k, 1) if more else slice(NTILES - DEPTH + k, NTILES - DEPTH + k + 1)], min_val=0, max_val=EXPERTS - 1)
                    for a in range(2):
                        y = bank[6 + k % 2][:, a * P:(a + 1) * P]
                        for c in range(FC):
                            last = e.matmul(y, HT[:, k, c, a * P:(a + 1) * P], w2r[:, bass.ds(x * FC + c, 1), :].rearrange("p a n -> p (a n)"),
                                            start=(c == 0), stop=(c == FC - 1))
                    last.then_inc(self.yjob.sem, 1)

                def tiles(i, more):
                    turn(i, 1, lambda: self.xt.wait(e, i, AGO[1]))
                    first(i, 0)
                    turn(i, 2, lambda: self.xt.wait(e, i, AGO[2]))
                    first(i, 1)
                    second(i, 0, more)
                    first(i, 2)
                    second(i, 1, more)
                    if more:
                        turn(i + 1, 0, lambda: self.xt.wait(e, i, 2))
                    second(i, 2, more)
                turns = NTILES // DEPTH
                turn(0, 0, lambda: None)
                with e.Fori(0, turns - 1) as i:
                    tiles(i, True)
                tiles(turns - 1, False)

        def rowb(ap):
            return ap.partition_broadcast(P)

        wloads = [
            (Wqa[:, :, :], I["Wqa"]), (Wka[:, :, :], I["Wka"]), (Wnat[:, 0:2 * P], I["Wkv"]), (Wnat[:, 3 * P:4 * P], I["Wqn"]),
            (Wg1T[:, :], I["Wg1T"]), (Wg2[:, :], I["Wg2"]), (Woa[:, :], I["Woa"]), (gam[:, :], rowb(I["gam"])), (bet[:, :], rowb(I["bet"])),
            (negq[:, :], I["negq"]), (negk[:, :], I["negk"]),
        ]
        late_loads = [
            (negqb[:, :], I["negqb"]), (negkb[:, :], I["negkb"]),
            (Wqb[:, :, :], I["Wqb"]), (Wkb[:, :, :], I["Wkb"]), (Wvb[:, :], I["Wvb"]), (Wob[:, :], I["Wob"]),
            (qbias[0:BIAS, :], I["qbias"]), (kbias[0:BIAS, :], I["kbias"]), (vbias[:, :], rowb(I["vbias"])), (obias[:, :], rowb(I["obias"])),
            (lngT[:, :], I["lngT"]), (lnbT[:, :], I["lnbT"]), (Wab[:, 0:P], I["abel_w"]), (Wab[:, P:P + EXPERTS], I["gate_w"]),
            (abias[:, 0:P], rowb(I["abel_b"])), (abias[:, P:P + EXPERTS], rowb(I["gate_b"])), 
            (mixa[:, :], rowb(I["mixa"])), (mixn[:, :], rowb(I["mixn"])), (mixb[:, :], rowb(I["mixb"])), (rank8[:, :], rowb(I["rank8"])),
        ]
        N_WLOADS = len(wloads)

        def loads_sync(e):
            for a, b in ((ident[:, :], I["ident"]), (A[:, :, :], I["gens"]), (AT[:, :, :], I["gensT"]), (inv[:, :], rowb(I["inv"])),
                         (thr[:, :, :].rearrange("p a b -> p (a b)"), rowb(I["thr"]))):
                e.dma_start(a, b).then_inc(gens_loaded, 16)
            for b in range(BATCH):
                e.dma_start(X[:, b * TPB:(b + 1) * TPB, :], I["x"][b].rearrange("(t p) d -> p t d", p=P)).then_inc(x_loaded, 16)
            e.dma_start(w2r[:, :, :].rearrange("p c n -> p (c n)"), I["w2T"].rearrange("p x f -> p (x f)")).then_inc(w2_loaded, 16)
            e.dma_start(b2T[:, :], I["b2T"]).then_inc(w2_loaded, 16)

        def loads_scalar(e):
            for a, b in wloads:
                e.dma_start(a, b).then_inc(w_loaded, 16)
            for a, b in late_loads:
                e.dma_start(a, b).then_inc(w_late, 16)

        def tables_sync(e):
            for a, b in ((maskT, "maskT"), (sel, "sel"), (lamq, "lamq"), (lamk, "lamk"), (lamc, "lamc"), (blk, "blk")):
                e.dma_start(a[tuple(slice(None) for _ in a.shape)], I[b]).then_inc(a_tables, 16)

        begins = [sem(f"phase{n}_may_begin") for n in range(2)]
        ffns = [Ffn(n, begins[n]) for n in range(2)]
        block = ctx.enter_context(nc.Block())

        @block.sync
        def _(e):
            loads_sync(e)
            tables_sync(e)
            attn_a_sync(e)
            ffns[0].sync(e)
            attn_b_sync(e)
            ffns[1].sync(e)
            with e.Fori(0, BATCH) as i:
                ffns[1].added.wait(e, i, 0)
                e.dma_start(out[bass.ds(i, 1), :, :].rearrange("b (t p) d -> p (b t) d", p=P), X[:, bass.ds(i * TPB, TPB), :]).then_inc(out_stored, 16)
            e.wait_ge(out_stored, 16 * BATCH)

        @block.scalar
        def _(e):
            loads_scalar(e)
            attn_a_scalar(e)
            ffns[0].scalar(e)
            attn_b_scalar(e)
            ffns[1].scalar(e)

        @block.gpsimd
        def _(e):
            e.memset(Qpad[:, :, :, :].bitcast(F32), 0.0).then_inc(zeroed, 1)
            expm_gpsimd(e)
            attn_a_gpsimd(e)
            ffns[0].gpsimd(e)
            attn_b_gpsimd(e)
            ffns[1].gpsimd(e)

        @block.vector
        def _(e):
            attn_a_vector(e)
            expm_vector(e)
            e.wait_ge(x_loaded, 16 * BATCH)
            attn_a_vector_loop(e)
            e.wait_ge(zeroed, 1)
            e.wait_ge(a_tables, 96)
            e.wait_ge(w_late, 16 * len(late_loads))
            e.memset(rstd2[:, :], 0.0).then_inc(begins[0], 1)
            e.wait_ge(begins[0], 1)
            ffns[0].vector(e)
            e.memset(rstd2[:, :], 0.0).then_inc(b_begin, 1)
            e.wait_ge(b_begin, 1)
            attn_b_vector(e)
            e.memset(rstd2[:, :], 0.0).then_inc(begins[1], 1)
            e.wait_ge(begins[1], 1)
            ffns[1].vector(e)

        @block.tensor
        def _(e):
            expm_tensor(e)
            attn_a_tensor(e)
            ffns[0].tensor(e)
            attn_b_tensor(e)
            ffns[1].tensor(e)


def slot_columns(w):
    t = w.reshape(w.shape[0], SLOTS, R, 1, D)
    o = np.zeros((w.shape[0], SLOTS, R, PART), np.float32)
    o[..., :ROWS] = np.broadcast_to(t, (w.shape[0], SLOTS, R, 3, D)).reshape(w.shape[0], SLOTS, R, ROWS)
    return o.reshape(w.shape[0], SLOTS, P)


def packed_columns(w):
    t = w.reshape(w.shape[0], SLOTS, R, 1, D)
    return np.broadcast_to(t, (w.shape[0], SLOTS, R, 3, D)).reshape(w.shape[0], SLOTS, BIAS)


def constants():
    c = {}
    c["ident"] = np.eye(P, dtype=np.float32)
    start = 2.0 ** (-2.0 ** (-(np.log2(H) - 3)))
    s = np.array([start * start ** i for i in range(H)], dtype=np.float32)
    s = (s * (1.0 - 0 / 11 + 1e-05)).astype(np.float32)
    idx = np.arange(P, dtype=np.float32)
    diff = idx[None, :] - idx[:, None]
    m = np.where(diff >= 0, np.exp(-s[:, None, None] * np.maximum(diff, 0)), 0).astype(np.float32)
    c["maskT"] = np.ascontiguousarray(m.transpose(1, 0, 2))
    sh = np.repeat(s, D)
    c["lamq"] = np.exp(-sh[:, None] * (idx[None, :] + 1)).astype(np.float32)
    c["lamk"] = np.exp(-sh[None, :] * (P - 1.0 - idx[:, None])).astype(np.float32)
    c["lamc"] = np.exp(-sh * P).astype(np.float32)[:, None]
    h = np.arange(P) // D
    c["blk"] = (h[:, None] == h[None, :]).astype(np.float32)
    sel = np.zeros((P, SLOTS, P), np.float32)
    for q in range(SLOTS):
        for r in range(R):
            for d in range(D):
                sel[PART * r + d, q, (R * q + r) * D + d] = 1
    c["sel"] = sel
    row = np.arange(P) % PART
    c["negq"] = -((row >= 2 * D) & (row < 3 * D)).astype(np.float32)[:, None]
    c["negk"] = -((row >= D) & (row < 2 * D)).astype(np.float32)[:, None]
    part = np.arange(P) % ROWS // D
    c["negqb"] = -(part == 2).astype(np.float32)[:, None]
    c["negkb"] = -(part == 1).astype(np.float32)[:, None]
    c["inv"] = (1.0 / np.arange(TAYLOR, 0, -1)).astype(np.float32)
    c["thr"] = np.repeat(THETA * 2.0 ** np.arange(SQUARINGS), NROT).astype(np.float32)
    c["tok"] = (np.arange(NT)[None, :] * P + np.arange(P)[:, None]).astype(np.float32)
    c["tri"] = (np.arange(P)[:, None] < np.arange(P)[None, :]).astype(np.float32)
    c["tab"] = np.concatenate([np.arange(EXPERTS + 1) * REGION, np.arange(MAXT) * TILE, np.arange(NTILES), np.arange(EXPERTS + 1)]).astype(np.float32)
    pads = np.zeros((EXPERTS * TILE + SPARE, ROW), np.float32)
    pads[:, P:] = 2 * NT * P + np.arange(len(pads))[:, None]
    c["pads"] = pads
    c["rank8"] = np.arange(EXPERTS, 0, -1).astype(np.float32)
    sl = alibi_slopes()
    hi = (sl.view(np.uint32) & np.uint32(0xFFFFF000)).view(np.float32)
    lo = (sl - hi).astype(np.float32)
    pos = np.arange(SEQ, dtype=np.float32)
    one = np.ones(SEQ, np.float32)
    aq = np.zeros((R, AUG, SLOTS, SEQ), np.float32)
    ak = np.zeros((R, AUG, SLOTS, SEQ), np.float32)
    for q in range(SLOTS):
        for r in range(R):
            a, b = hi[R * q + r], lo[R * q + r]
            aq[r, :, q] = [-pos, a * one, -pos, b * one]
            ak[r, :, q] = [a * one, pos, b * one, pos]
    c["augq"] = aq
    ones = np.ones((1, SLOTS, SEQ), np.float32)
    c["auga"] = np.concatenate([ak.reshape(R * AUG, SLOTS, SEQ), ones])
    c["augb"] = np.concatenate([-ak.reshape(R * AUG, SLOTS, SEQ), ones])
    k = np.arange(P)
    c["over"] = np.maximum(k[:, None] - k[None, :], 0).astype(np.float32)
    c["overT"] = np.ascontiguousarray(c["over"].T)
    return c


def layouts(a):
    g = lambda n: np.asarray(a[n])
    L = {"x": g("L0_attn_a_x")}
    L["Wqa"] = slot_columns(g("L0_attn_a_Wq"))
    L["Wka"] = slot_columns(g("L0_attn_a_Wk"))
    L["Wkv"] = np.concatenate([g("L0_attn_a_Wk"), g("L0_attn_a_Wv")], axis=1)
    L["Wqn"] = g("L0_attn_a_Wq")
    L["Wg1T"] = g("L0_attn_a_Wg1").T
    L["Wg2"] = g("L0_attn_a_Wg2")
    L["Woa"] = g("L0_attn_a_Wo")
    L["gam"], L["bet"] = g("L0_attn_a_gamma"), g("L0_attn_a_beta")
    W, B = g("L0_attn_b_W_qkv"), g("L0_attn_b_b_qkv")
    L["Wqb"], L["Wkb"] = packed_columns(W[:P].T), packed_columns(W[P:2 * P].T)
    L["Wvb"] = W[2 * P:].T
    L["Wob"] = g("L0_attn_b_W_out").T
    L["Wqkn"] = W[:2 * P].reshape(2, P, P).transpose(2, 0, 1)
    L["nbias"] = B[:2 * P].reshape(2, P).T
    L["qbias"] = packed_columns(B[None, :P])[0].T
    L["kbias"] = packed_columns(B[None, P:2 * P])[0].T
    L["vbias"], L["obias"] = B[2 * P:], g("L0_attn_b_b_out")
    L["lngT"], L["lnbT"] = g("L0_ffn_ln_g")[:, None], g("L0_ffn_ln_b")[:, None]
    L["abel_w"], L["gate_w"] = g("L0_ffn_abel_w"), g("L0_ffn_gate_w_moe")
    L["abel_b"], L["gate_b"] = g("L0_ffn_abel_b"), g("L0_ffn_gate_b_moe")
    L["w1"] = g("L0_ffn_w1").transpose(1, 0, 2)
    L["b1T"] = g("L0_ffn_b1").reshape(EXPERTS, FC, P).transpose(2, 0, 1)
    L["w2T"] = g("L0_ffn_w2").transpose(2, 0, 1)
    L["b2T"] = g("L0_ffn_b2").T
    L["gens"] = g("L0_ffn_gens").transpose(1, 0, 2)
    L["gensT"] = g("L0_ffn_gens").transpose(2, 0, 1)
    mix = g("L0_ffn_mix_w").reshape(2 * P)
    L["mixa"], L["mixn"], L["mixb"] = mix[:P], mix[P:], g("L0_ffn_mix_b")
    L.update(constants())
    return L


def kernel(**inputs):
    import numpy as _np
    import concourse.bacc as _bacc
    from concourse import mybir as _mybir
    from concourse.bass_utils import run_bass_kernel_spmd as _run

    nc = _bacc.Bacc("TRN2", target_bir_lowering=False, num_devices=1)
    arrays, args = {}, {}
    for name, a in layouts(inputs).items():
        a = _np.ascontiguousarray(a)
        arrays[f"in_{name}_dram"] = a
        args[name] = nc.dram_tensor(f"in_{name}_dram", a.shape, _mybir.dt.from_np(a.dtype), kind="ExternalInput").ap()
    out = nc.dram_tensor("out_0_dram", (BATCH, SEQ, P), _mybir.dt.from_np(_np.dtype("float32")), kind="ExternalOutput").ap()
    build(nc, args, out)
    r = _run(nc, [arrays], core_ids=[0])
    return r.results[0]["out_0_dram"]
```
